# Optimizing a Trainium2 kernel written in Bass

```python
import numpy as np
import jax
import jax.numpy as jnp

def _softmax(x, axis=-1):
    return jax.nn.softmax(x, axis=axis)

def _gelu(x):
    return jax.nn.gelu(x, approximate=True)

def _silu(x):
    return jax.nn.silu(x)

def _sigmoid(x):
    return jax.nn.sigmoid(x)

def _layernorm(x, axis=-1, eps=1e-05):
    m = jnp.mean(x, axis=axis, keepdims=True)
    v = jnp.var(x, axis=axis, keepdims=True)
    return (x - m) / jnp.sqrt(v + eps)

def _scatter_add(tgt, idx, src, axis=0):
    return tgt.at[idx].add(src)

def _segment_sum(src, seg, n):
    return jax.ops.segment_sum(src, seg, n)
kernel_name = 'mk_gnn_ffn_d1_gnn_r8_b3309c'

def setup_inputs(seed: int=0):
    np.random.seed(seed)
    _w = jnp.asarray

    def _rec_inputs():
        import jax
        import jax.numpy as jnp
        _gk = jax.random.key(seed)
        x = -8.776e-05 + 1 * jax.random.normal(jax.random.fold_in(_gk, 1), (6250, 256), jnp.float32)
        src = jax.random.randint(jax.random.fold_in(_gk, 2), (100000,), 0, 6250, jnp.int32)
        dst = jax.random.randint(jax.random.fold_in(_gk, 3), (100000,), 0, 6250, jnp.int32)
        _o = jnp.argsort(dst, stable=True)
        src = src[_o]
        dst = dst[_o]
        edge_weight = jax.random.uniform(jax.random.fold_in(_gk, 12), (100000,), jnp.float32, 0.0, 0.999998)
        return (x, src, dst, edge_weight)
    x, src, dst, edge_weight = _rec_inputs()

    def _L0_gnn_setup():
        import jax, jax.numpy as jnp
        import numpy as np
        N, E, D, H, C = (2500, 40000, 256, 8, 32)
        NEG_SLOPE = 0.2
        key = jax.random.key(seed)
        ks = jax.random.split(key, 9)
        s = 1.0 / np.sqrt(D)
        x = jax.random.normal(ks[0], (N, D), dtype=jnp.float32)
        edge_index = jax.random.randint(ks[1], (2, E), 0, N, dtype=jnp.int32)
        edge_attr = jax.random.uniform(ks[2], (E,), dtype=jnp.float32, minval=0.05, maxval=1.0)
        W_l = jax.random.normal(ks[3], (D, H * C), dtype=jnp.float32) * s
        b_l = jax.random.normal(ks[4], (H * C,), dtype=jnp.float32) * 0.01
        W_r = jax.random.normal(ks[5], (D, H * C), dtype=jnp.float32) * s
        b_r = jax.random.normal(ks[6], (H * C,), dtype=jnp.float32) * 0.01
        att = jax.random.normal(ks[7], (H, C), dtype=jnp.float32) * (1.0 / np.sqrt(C))
        bias = jax.random.normal(ks[8], (H * C,), dtype=jnp.float32) * 0.01
        return {'x': x, 'edge_index': edge_index, 'edge_attr': edge_attr, 'W_l': W_l, 'b_l': b_l, 'W_r': W_r, 'b_r': b_r, 'att': att, 'bias': bias}
    _L0_gnn_all = _L0_gnn_setup()
    _L0_gnn_in = {k: v for k, v in _L0_gnn_all.items() if k in ('W_l', 'b_l', 'W_r', 'b_r', 'att', 'bias')}
    del _L0_gnn_all

    def _L0_ffn_setup():
        import jax, jax.numpy as jnp
        import numpy as np
        B, S, D, E, H, K = (4, 512, 256, 8, 512, 2)
        key = jax.random.key(seed)
        ks = jax.random.split(key, 6)
        x = jax.random.normal(ks[0], (B, S, D), jnp.float32)
        Wg = jax.random.normal(ks[1], (D, E), jnp.float32) * 0.02
        bg = jnp.zeros((E,), jnp.float32)
        W1 = jax.random.normal(ks[2], (E, D, H), jnp.float32) * 0.02
        b1 = jnp.zeros((E, H), jnp.float32)
        W2 = jax.random.normal(ks[3], (E, H, D), jnp.float32) * 0.02
        b2 = jnp.zeros((E, D), jnp.float32)
        return {'x': x, 'Wg': Wg, 'bg': bg, 'W1': W1, 'b1': b1, 'W2': W2, 'b2': b2}
    _L0_ffn_all = _L0_ffn_setup()
    _L0_ffn_in = {k: v for k, v in _L0_ffn_all.items() if k in ('Wg', 'bg', 'W1', 'b1', 'W2', 'b2')}
    del _L0_ffn_all
    return {'x': x, 'src': src, 'dst': dst, 'edge_weight': edge_weight, 'L0_gnn_W_l': _L0_gnn_in['W_l'], 'L0_gnn_b_l': _L0_gnn_in['b_l'], 'L0_gnn_W_r': _L0_gnn_in['W_r'], 'L0_gnn_b_r': _L0_gnn_in['b_r'], 'L0_gnn_att': _L0_gnn_in['att'], 'L0_gnn_bias': _L0_gnn_in['bias'], 'L0_ffn_Wg': _L0_ffn_in['Wg'], 'L0_ffn_bg': _L0_ffn_in['bg'], 'L0_ffn_W1': _L0_ffn_in['W1'], 'L0_ffn_b1': _L0_ffn_in['b1'], 'L0_ffn_W2': _L0_ffn_in['W2'], 'L0_ffn_b2': _L0_ffn_in['b2']}

def reference(x, src, dst, edge_weight, L0_gnn_W_l, L0_gnn_b_l, L0_gnn_W_r, L0_gnn_b_r, L0_gnn_att, L0_gnn_bias, L0_ffn_Wg, L0_ffn_bg, L0_ffn_W1, L0_ffn_b1, L0_ffn_W2, L0_ffn_b2):
    import jax
    import jax.numpy as jnp

    def _L0_gnn_ref(x, edge_index, edge_attr, W_l, b_l, W_r, b_r, att, bias):
        import jax, jax.numpy as jnp
        import numpy as np
        N, E, D, H, C = (2500, 40000, 256, 8, 32)
        NEG_SLOPE = 0.2
        n = x.shape[0]
        x_l = (x @ W_l + b_l).reshape(n, H, C)
        x_r = (x @ W_r + b_r).reshape(n, H, C)
        src, dst = (edge_index[0], edge_index[1])
        x_j = x_l[src]
        g = jax.nn.leaky_relu(x_r[dst] + x_j, NEG_SLOPE)
        alpha = jnp.einsum('ehc,hc->eh', g, att)
        alpha = alpha + jnp.log(edge_attr)[:, None]
        amax = jax.ops.segment_max(alpha, dst, num_segments=n)
        ex = jnp.exp(alpha - amax[dst])
        denom = jax.ops.segment_sum(ex, dst, num_segments=n)
        alpha = ex / (denom[dst] + 1e-16)
        out = jax.ops.segment_sum(x_j * alpha[..., None], dst, num_segments=n)
        return out.reshape(n, H * C) + bias

    def _L0_ffn_ref(x, Wg, bg, W1, b1, W2, b2):
        import jax, jax.numpy as jnp
        import numpy as np
        B, S, D, E, H, K = (4, 512, 256, 8, 512, 2)
        Bv, Sv, Dv = x.shape
        gate_scores = x @ Wg + bg
        _, idx = jax.lax.top_k(gate_scores, K)
        mask = jax.nn.one_hot(idx, E, dtype=x.dtype).sum(axis=-2)
        xf = x.reshape(-1, Dv)
        mf = mask.reshape(-1, E)
        h = jax.nn.gelu(jnp.einsum('td,edh->teh', xf, W1) + b1[None], approximate=False)
        y = jnp.einsum('teh,ehd->ted', h, W2) + b2[None]
        out = jnp.einsum('ted,te->td', y, mf)
        return out.reshape(Bv, Sv, Dv)
    edge_index = jnp.stack([src, dst])
    x = x + _L0_gnn_ref(_layernorm(x, axis=-1), edge_index, edge_weight, L0_gnn_W_l, L0_gnn_b_l, L0_gnn_W_r, L0_gnn_b_r, L0_gnn_att, L0_gnn_bias)
    x = x + _L0_ffn_ref(_layernorm(x, axis=-1)[None], L0_ffn_Wg, L0_ffn_bg, L0_ffn_W1, L0_ffn_b1, L0_ffn_W2, L0_ffn_b2)[0]
    return x

_drawn_inputs = setup_inputs


def setup_inputs(seed=0):
    import zlib

    import numpy as np

    out = dict(_drawn_inputs(seed))
    spreads = {'L0_ffn_bg': (0.0, 0.1), 'L0_ffn_b1': (0.0, 0.1), 'L0_ffn_b2': (0.0, 0.1)}
    factors = {'L0_gnn_b_l': 3.285, 'L0_gnn_b_r': 25.985, 'L0_gnn_bias': 2.899}
    for name, (base, spread) in spreads.items():
        noise = np.random.default_rng([zlib.crc32(name.encode()), seed]).standard_normal(out[name].shape)
        drawn = base * np.exp(spread * noise) if base else spread * noise
        out[name] = jnp.asarray(drawn.astype(out[name].dtype))
    for name, factor in factors.items():
        out[name] = (out[name] * factor).astype(out[name].dtype)
    return out
```

```python
from contextlib import ExitStack

import concourse.bass as bass
from concourse import mybir

F32 = mybir.dt.float32
BF16 = mybir.dt.bfloat16
I32 = mybir.dt.int32
U32 = mybir.dt.uint32
ALU = mybir.AluOpType
ACT = mybir.ActivationFunctionType
AX = mybir.AxisListType

P = 128
N, D = 6250, 256
E = 100000
H, C = 8, 32
EXPERTS, HID = 8, 512
KD = D // P
KH = HID // P
SLOPE = 0.2
EPS = 1e-5

NT = 50
NODE_TILES = -(-N // P)
ET = -(-E // P)
EPAD = ET * P
ITEMS = -(-(ET + NODE_TILES - 1) // 64) * 64
QI = -(-ITEMS // P)
BLOCKS = P // H
U = ITEMS // BLOCKS
SCAN = U * P
PAD_DST = NODE_TILES * P - 1
BIG = 1e30
TINY_WEIGHT = 1e-19


class Chain:

    def __init__(self, eng, sem, base=0):
        self.eng, self.sem, self.base, self.n = eng, sem, base, 0

    def __call__(self, ins, constant=None):
        self.n += 1
        ins.then_inc(self.sem, 1)
        if constant is not None:
            goal = self.eng.to_reg(self.base + self.n)
            self.eng.wait_ge(constant, 1)
            self.eng.wait_ge(self.sem, goal)
            return
        self.eng.wait_ge(self.sem, self.base + self.n)


def build(nc, x, src, dst, edge_weight, W_l, b_l, W_r, b_r, att, bias, Wg, bg, W1, b1, W2, b2, out):
    with ExitStack() as whole:
        def keep(name, shape, dt=F32):
            return whole.enter_context(nc.sbuf_tensor(name, shape, dt))

        def dram(name, shape, dt=F32):
            return nc.dram_tensor(name, shape, dt, kind="Internal").ap()

        d = dict(
            src=dram("src_tiles", (ET, P), I32), dst=dram("dst_tiles", (ET, P), I32),
            weight=dram("weight_tiles", (ET, P)),
            key=dram("item_keys", (1 + QI * P * P + 1, 1)), item_weight=dram("item_weights", (QI * P, P)),
            node_tile=dram("item_node_tile", (QI * P, 1), I32),
            left=dram("left_rows", (NT * P, D)),
            rows=dram("item_rows", (ITEMS // 4, P, 4 * D)),
        )
        s = dict(
            ident=keep("ident", [P, P]), identb=keep("identb", [P, P], BF16),
            iota=keep("iota_row", [P, P]), ones=keep("ones_row", [1, P]),
            X=keep("X", [P, NT, D]),
            jrow=keep("item_node_tile_row", [1, QI * P], I32),
            dl=keep("item_local_dst", [P, QI * P]),
        )
        constants(nc, s)
        with ExitStack() as scope:
            s["alpha"] = keep("alpha", [P, ITEMS, H])
            s["srcs"] = scope.enter_context(nc.sbuf_tensor("item_src", [P, QI * P], I32))
            schedule(nc, d, s, src, dst, edge_weight)
            s["right"] = scope.enter_context(nc.sbuf_tensor("right_rows", [P, NT, 3, D], BF16))
            project(nc, d, s, x, W_l, b_l, W_r, b_r)
            scores(nc, d, s, att)
        segment_softmax(nc, d, s)
        with ExitStack() as scope:
            s["acc"] = scope.enter_context(nc.sbuf_tensor("acc", [P, NT, D + H], F32))
            aggregate(nc, d, s)
            normalise(nc, s, bias)
        experts(nc, s, Wg, bg, W1, b1, W2, b2, out)


def constants(nc, s):
    set_, ramp = nc.alloc_semaphore("const_set"), nc.alloc_semaphore("const_ramp")
    with nc.Block() as block:
        @block.gpsimd
        def _(pool):
            nc.gpsimd.memset(s["ident"][:, :], 0.0).then_inc(set_, 1)
            nc.gpsimd.memset(s["identb"][:, :], 0.0).then_inc(set_, 1)
            nc.gpsimd.memset(s["ones"][:, :], 1.0)
            nc.gpsimd.iota(s["iota"][:, :], [[1, P]], base=0, channel_multiplier=0,
                           allow_small_or_imprecise_dtypes=True).then_inc(ramp, 1)
            pool.wait_ge(set_, 2)
            for m in ("ident", "identb"):
                nc.gpsimd.affine_select(out=s[m][:, :], in_=s[m][:, :], compare_op=ALU.not_equal, fill=1.0,
                                        base=0, pattern=[[-1, P]], channel_multiplier=1).then_inc(ramp, 1)
            pool.wait_ge(ramp, 3)


def schedule(nc, d, s, src, dst, edge_weight):
    sem = nc.alloc_semaphore
    pads_set, padded, ends_in, ends_done = sem("pads_set"), sem("padded"), sem("ends_in"), sem("ends_done")
    spread, spread_copied, items_done = sem("spread"), sem("spread_copied"), sem("items_done")
    gathered = [sem(f"gathered{i}") for i in range(3)]
    local_done, turned, turned_copied = sem("local_done"), sem("turned"), sem("turned_copied")
    stored, row_in, dve, numbered = sem("stored"), sem("row_in"), sem("dve_schedule"), sem("numbered")
    with ExitStack() as scope:
        def sb(name, shape, dt=F32):
            return scope.enter_context(nc.sbuf_tensor(name, shape, dt))

        npad = EPAD - E
        pad_d, pad_s, pad_w = sb("pad_d", [1, npad], I32), sb("pad_s", [1, npad], I32), sb("pad_w", [1, npad])
        pad_k = sb("pad_k", [1, 2])
        ends = sb("ends", [1, 2, ET], I32)
        tile_i = sb("tile_i", [1, 2, ET], I32)
        tile_f = sb("tile_f", [1, 2, ET])
        count = sb("count", [1, ET])
        cum = sb("cum", [1, ET])
        one = sb("one", [1, ET])
        offs = sb("offs", [1, 2, ET])
        offs_all = sb("offs_all", [P, 2, ET])
        number = sb("number", [P, QI])
        work = sb("work", [P, ET])
        found = sb("found", [P, 3, QI])
        jt = sb("jt", [P, QI])
        t_idx, j_idx, base = sb("t_idx", [P, QI], I32), sb("j_idx", [P, QI], I32), sb("base", [P, QI])
        rows_s, rows_d = sb("rows_s", [P, QI, P], I32), sb("rows_d", [P, QI, P], I32)
        rows_w = sb("rows_w", [P, QI, P])
        sf, df = sb("sf", [P, QI, P]), sb("df", [P, QI, P])
        local, live, key = sb("local", [P, QI, P]), sb("live", [P, QI, P]), sb("key", [P, QI, P])
        ps = scope.enter_context(nc.psum_tensor("ps_spread", [P, 4, 512], F32))
        pt = scope.enter_context(nc.psum_tensor("ps_turn", [P, 2, 512], F32))
        half = ET // 2
        with nc.Block() as block:
            @block.gpsimd
            def _(pool):
                nc.gpsimd.memset(pad_d[:, :], PAD_DST).then_inc(pads_set, 1)
                nc.gpsimd.memset(pad_s[:, :], 0).then_inc(pads_set, 1)
                nc.gpsimd.memset(pad_w[:, :], 1.0).then_inc(pads_set, 1)
                nc.gpsimd.memset(pad_k[:, :], -2.0).then_inc(pads_set, 1)
                nc.gpsimd.memset(one[:, :], 1.0).then_inc(pads_set, 1)
                nc.gpsimd.iota(number[:, :], [[P, QI]], base=0, channel_multiplier=1,
                               allow_small_or_imprecise_dtypes=True).then_inc(numbered, 1)
                pool.wait_ge(items_done, 1)
                pool.wait_ge(padded, 16 * 6)
                for q in range(QI):
                    for i, (rows, table) in enumerate(((rows_d, "dst"), (rows_s, "src"), (rows_w, "weight"))):
                        nc.gpsimd.indirect_dma_start(
                            out=rows[:, q, :], out_offset=None, in_=d[table][:, :],
                            in_offset=bass.IndirectOffsetOnAxis(ap=t_idx[:, q:q + 1], axis=0),
                        ).then_inc(gathered[i], 16)

            @block.sync
            def _(sp):
                flat = {k: d[k].rearrange("t p -> (t p)") for k in ("src", "dst", "weight")}
                for k, a in (("src", src), ("dst", dst), ("weight", edge_weight)):
                    sp.dma_start(flat[k][0:E].rearrange("(a b) -> a b", a=16),
                                 a.rearrange("(a b) -> a b", a=16)).then_inc(padded, 16)
                sp.wait_ge(pads_set, 5)
                for k, pad in (("src", pad_s), ("dst", pad_d), ("weight", pad_w)):
                    sp.dma_start(flat[k][E:EPAD].rearrange("(a b) -> a b", a=1), pad[:, :]).then_inc(padded, 16)
                for at, i in ((0, 0), (1 + QI * P * P, 1)):
                    sp.dma_start(d["key"][at:at + 1, :], pad_k[:, i:i + 1]).then_inc(stored, 16)
                sp.wait_ge(padded, 16 * 6)
                for i, at in ((0, 0), (1, P - 1)):
                    sp.dma_start(ends[:, i:i + 1, :].rearrange("a i t -> a (i t)"),
                                 d["dst"][:, at:at + 1].rearrange("t o -> o t"),
                                 allow_slow_non_contiguous=True).then_inc(ends_in, 16)
                sp.wait_ge(items_done, 1)
                sp.dma_start(d["node_tile"].rearrange("(q p) o -> p (q o)", p=P), j_idx[:, :],
                             allow_slow_non_contiguous=True).then_inc(stored, 16)
                sp.wait_ge(local_done, 2)
                sp.dma_start(d["key"][1:1 + QI * P * P, :].rearrange("(q p e) o -> p q (e o)", p=P, q=QI),
                             key[:, :, :]).then_inc(stored, 16)
                sp.wait_ge(gathered[2], 16 * QI)
                sp.dma_start(d["item_weight"].rearrange("(q p) e -> p q e", p=P), rows_w[:, :, :]).then_inc(stored, 16)
                sp.wait_ge(stored, 16 * 5)
                sp.dma_start(s["jrow"][:, :], d["node_tile"].rearrange("n o -> o n"),
                             allow_slow_non_contiguous=True).then_inc(row_in, 16)
                sp.wait_ge(row_in, 16)

            @block.tensor
            def _(pe):
                pe.wait_ge(ends_done, 1)
                for a in range(2):
                    for b in range(2):
                        last = nc.tensor.matmul(ps[:, 2 * a + b, 0:half], s["ones"][0:1, :],
                                                offs[0:1, a, b * half:(b + 1) * half], start=True, stop=True)
                last.then_inc(spread, 1)
                for i in range(2 * QI):
                    pe.wait_ge(local_done, 1 if i < QI else 3)
                    if i >= 2:
                        pe.wait_ge(turned_copied, i - 1)
                    from_ = local if i < QI else sf
                    nc.tensor.transpose(pt[:, i % 2, 0:P], from_[:, i % QI, :], s["ident"][:, :]).then_inc(turned, 1)

            @block.scalar
            def _(act):
                for i in range(2 * QI):
                    act.wait_ge(turned, i + 1)
                    to = (s["dl"] if i < QI else s["srcs"])[:, (i % QI) * P:(i % QI + 1) * P]
                    nc.scalar.activation(to, pt[:, i % 2, 0:P], ACT.Copy).then_inc(turned_copied, 1)

            @block.vector
            def _(v):
                step = Chain(v, dve)
                v.wait_ge(ends_in, 32)
                step(nc.vector.tensor_scalar(tile_i[:, :, :], ends[:, :, :], 7, None, ALU.logical_shift_right))
                step(nc.vector.tensor_copy(tile_f[:, :, :], tile_i[:, :, :]))
                step(nc.vector.scalar_tensor_tensor(count[:, :], tile_f[:, 1, :], 1.0, tile_f[:, 0, :],
                                                    ALU.add, ALU.subtract))
                v.wait_ge(pads_set, 5)
                step(nc.vector.tensor_tensor_scan(cum[:, :], one[:, :], count[:, :], 0.0, ALU.mult, ALU.add))
                step(nc.vector.tensor_tensor(offs[:, 0, :], cum[:, :], count[:, :], ALU.subtract))
                nc.vector.tensor_copy(offs[:, 1, :], tile_f[:, 0, :]).then_inc(ends_done, 1)
                v.wait_ge(spread, 1)
                for a in range(2):
                    step(nc.vector.tensor_copy(offs_all[:, a, :].rearrange("p (b n) -> p b n", b=2),
                                               ps[:, 2 * a:2 * a + 2, 0:half]))
                v.wait_ge(numbered, 1)
                for q in range(QI):
                    own = number[:, q:q + 1]
                    step(nc.vector.tensor_scalar(work[:, :], offs_all[:, 0, :], own, None, ALU.is_le))
                    step(nc.vector.tensor_reduce(found[:, 0, q:q + 1], work[:, :], AX.X, ALU.add))
                    for a in range(2):
                        step(nc.vector.scalar_tensor_tensor(work[:, :], offs_all[:, 0, :], own, offs_all[:, a, :],
                                                            ALU.is_le, ALU.mult))
                        step(nc.vector.tensor_reduce(found[:, 1 + a, q:q + 1], work[:, :], AX.X, ALU.max))
                step(nc.vector.tensor_scalar(t_idx[:, :], found[:, 0, :], -1.0, None, ALU.add))
                step(nc.vector.tensor_tensor(jt[:, :], found[:, 2, :], number[:, :], ALU.add))
                step(nc.vector.tensor_tensor(jt[:, :], jt[:, :], found[:, 1, :], ALU.subtract))
                step(nc.vector.tensor_scalar(base[:, :], jt[:, :], float(P), None, ALU.mult))
                nc.vector.tensor_scalar(j_idx[:, :], jt[:, :], float(NT - 1), None, ALU.min).then_inc(items_done, 1)
                v.wait_ge(gathered[0], 16 * QI)
                step(nc.vector.tensor_copy(df[:, :, :], rows_d[:, :, :]))
                for q in range(QI):
                    last = nc.vector.tensor_scalar(local[:, q, :], df[:, q, :], base[:, q:q + 1], None, ALU.subtract)
                last.then_inc(local_done, 1)
                v.wait_ge(local_done, 1)
                step(nc.vector.tensor_scalar(live[:, :, :], local[:, :, :], 0.0, None, ALU.is_ge))
                step(nc.vector.scalar_tensor_tensor(live[:, :, :], local[:, :, :], float(P), live[:, :, :],
                                                    ALU.is_lt, ALU.mult))
                step(nc.vector.scalar_tensor_tensor(key[:, :, :], df[:, :, :], 1.0, live[:, :, :],
                                                    ALU.add, ALU.mult))
                nc.vector.tensor_scalar(key[:, :, :], key[:, :, :], -1.0, None, ALU.add).then_inc(local_done, 1)
                v.wait_ge(gathered[1], 16 * QI)
                nc.vector.tensor_copy(sf[:, :, :], rows_s[:, :, :]).then_inc(local_done, 1)


def moments(nc, v, step, stats, mv, std, X, sqrt_ready, sqrt_done):
    for i in range(NT):
        last = nc.vector.bn_stats(stats[:, i, :], X[:, i, :])
    step(last)
    for i in range(NT):
        last = nc.vector.bn_aggr(mv[:, i, :], stats[:, i, :])
    step(last)
    nc.vector.tensor_scalar(std[:, 0, :], mv[:, :, 1], EPS, None, ALU.add).then_inc(sqrt_ready, 1)
    v.wait_ge(sqrt_done, 1)
    step(nc.vector.reciprocal(std[:, 2, :], std[:, 1, :]))


def project(nc, d, s, x, W_l, b_l, W_r, b_r):
    sem = nc.alloc_semaphore
    x_in, w_in, cleared = sem("x_in"), sem("w_in"), sem("x_cleared")
    sqrt_ready, sqrt_done, dve = sem("p_sqrt_ready"), sem("p_sqrt_done"), sem("dve_project")
    normed, turned, turned_copied = sem("p_normed"), sem("p_turned"), sem("p_turned_copied")
    projected, biased, split1, act_part = sem("p_projected"), sem("p_biased"), sem("p_split"), sem("p_part")
    stored = [sem(f"left_stored{i}") for i in range(2)]
    CH = 3
    with ExitStack() as scope:
        def sb(name, shape, dt=F32):
            return scope.enter_context(nc.sbuf_tensor(name, shape, dt))

        X = s["X"]
        W = sb("p_W", [P, KD, 2 * D])
        bb = sb("p_b", [P, 2 * D])
        stats, mv, std = sb("p_stats", [P, NT, 6]), sb("p_mv", [P, NT, 2]), sb("p_std", [P, 3, NT])
        xn = sb("p_xn", [P, 2, D])
        xT = sb("p_xT", [P, 2, KD * P])
        y = sb("p_y", [P, 2, 2 * D])
        r1, r2 = sb("p_r1", [P, D]), sb("p_r2", [P, D])
        pt = scope.enter_context(nc.psum_tensor("p_pt", [P, 2, 512], F32))
        py = scope.enter_context(nc.psum_tensor("p_py", [P, 2, 512], F32))
        full = N // P
        rest = N - full * P
        with nc.Block() as block:
            @block.gpsimd
            def _(pool):
                nc.gpsimd.memset(X[:, full:NT, :], 0.0).then_inc(cleared, 1)

            @block.sync
            def _(sp):
                sp.dma_start(X[:, 0:full, :], x[0:full * P, :].rearrange("(t p) f -> p t f", p=P)).then_inc(x_in, 16)
                sp.wait_ge(cleared, 1)
                sp.dma_start(X[0:rest, full, :], x[full * P:N, :]).then_inc(x_in, 16)
                for i, (w, b) in enumerate(((W_l, b_l), (W_r, b_r))):
                    sp.dma_start(W[:, :, i * D:(i + 1) * D], w.rearrange("(k p) f -> p k f", p=P)).then_inc(w_in, 16)
                    sp.dma_start(bb[:, i * D:(i + 1) * D], b.partition_broadcast(P)).then_inc(w_in, 16)
                with sp.Fori(0, NT // 2) as i:
                    for k in range(2):
                        sp.wait_ge(biased, 2 * i + k + 1)
                        sp.dma_start(d["left"][bass.ds((2 * i + k) * P, P), :], y[:, k, 0:D]).then_inc(stored[k], 16)
                for k in range(2):
                    sp.wait_ge(stored[k], 16 * (NT // 2))

            @block.vector
            def _(v):
                step = Chain(v, dve)
                v.wait_ge(x_in, 32)
                moments(nc, v, step, stats, mv, std, X, sqrt_ready, sqrt_done)
                v.wait_ge(w_in, 64)
                first = step.n
                with v.Fori(0, NT // 2) as i:
                    step = Chain(v, dve, first + i * (2 * CH))
                    for k in range(2):
                        t = 2 * i + k
                        nc.vector.tensor_scalar(xn[:, k, :], X[:, bass.ds(t, 1), :].rearrange("p a f -> p (a f)"),
                                                mv[:, bass.ds(t, 1), 0], std[:, 2, bass.ds(t, 1)],
                                                ALU.subtract, ALU.mult).then_inc(normed, 1)
                        v.wait_ge(projected, t + 1)
                        v.wait_ge(stored[k], i * 16)
                        nc.vector.tensor_tensor(y[:, k, :], py[:, k, :], bb[:, :], ALU.add).then_inc(biased, 1)
                        v.wait_ge(biased, t + 1)
                        part = s["right"][:, bass.ds(t, 1), :, :].rearrange("p a c f -> p (a c) f")
                        v.wait_ge(act_part, t + 1)
                        step(nc.vector.tensor_tensor(r1[:, :], y[:, k, D:2 * D], part[:, 0, :], ALU.subtract))
                        step(nc.vector.tensor_copy(part[:, 1, :], r1[:, :]))
                        step(nc.vector.tensor_tensor(r2[:, :], r1[:, :], part[:, 1, :], ALU.subtract))
                        nc.vector.tensor_copy(part[:, 2, :], r2[:, :]).then_inc(split1, 1)

            @block.scalar
            def _(act):
                act.wait_ge(sqrt_ready, 1)
                nc.scalar.activation(std[:, 1, :], std[:, 0, :], ACT.Sqrt).then_inc(sqrt_done, 1)
                with act.Fori(0, NT // 2) as i:
                    for k in range(2):
                        t = 2 * i + k
                        act.wait_ge(turned, t + 1)
                        nc.scalar.activation(xT[:, k, :], pt[:, k, 0:KD * P], ACT.Copy).then_inc(turned_copied, 1)
                        act.wait_ge(biased, t + 1)
                        nc.scalar.activation(s["right"][:, bass.ds(t, 1), 0, :].rearrange("p a f -> p (a f)"),
                                             y[:, k, D:2 * D], ACT.Copy).then_inc(act_part, 1)

            @block.tensor
            def _(pe):
                pe.wait_ge(w_in, 64)
                with pe.Fori(0, NT // 2) as i:
                    for k in range(2):
                        t = 2 * i + k
                        pe.wait_ge(normed, t + 1)
                        for h in range(KD):
                            last = nc.tensor.transpose(pt[:, k, h * P:(h + 1) * P], xn[:, k, h * P:(h + 1) * P],
                                                       s["ident"][:, :])
                        last.then_inc(turned, 1)
                        pe.wait_ge(turned_copied, t + 1)
                        for h in range(KD):
                            last = nc.tensor.matmul(py[:, k, :], xT[:, k, h * P:(h + 1) * P], W[:, h, :],
                                                    start=(h == 0), stop=(h == KD - 1))
                        last.then_inc(projected, 1)


G = 4
GROUPS = ITEMS // G


def scores(nc, d, s, att):
    sem = nc.alloc_semaphore
    att_in, att_set = sem("att_in"), sem("att_set")
    listed = sem("listed")
    gathered = [sem(f"g_gathered{i}") for i in range(2)]
    spilled = [sem(f"g_spilled{i}") for i in range(2)]
    hot, hot_turned, hot_copied = sem("g_hot"), sem("g_hot_turned"), sem("g_hot_copied")
    spread, summed, leaked = sem("g_spread"), sem("g_summed"), sem("g_leaked")
    turned, turned_copied, scored, kept = sem("g_turned"), sem("g_turned_copied"), sem("g_scored"), sem("g_kept")
    with ExitStack() as scope:
        def sb(name, shape, dt=F32):
            return scope.enter_context(nc.sbuf_tensor(name, shape, dt))

        def pb(name, shape, dt=F32):
            return scope.enter_context(nc.psum_tensor(name, shape, dt))

        idx = sb("idx", [P, 2, G], I32)
        rows = sb("rows", [P, 2, G, D])
        hots = sb("hots", [P, 2, G, P], BF16)
        hotT = sb("hotT", [P, 2, G, P], BF16)
        S = sb("S", [P, 2, G, D])
        L = sb("L", [P, 2, G, D])
        LT = sb("LT", [P, 2, G * KD, P])
        attm = sb("attm", [P, KD, H])
        p_hot = pb("p_hot", [P, G, P], BF16)
        p_row = pb("p_row", [P, G // 2, 2, D])
        p_T = pb("p_T", [P, 2, 2, 512])
        p_a = pb("p_a", [P, G, H])
        with nc.Block() as block:
            @block.gpsimd
            def _(pool):
                nc.gpsimd.memset(attm[:, :, :], 0.0).then_inc(att_set, 1)
                with pool.Fori(0, GROUPS // 2) as i:
                    for k in range(2):
                        g = 2 * i + k
                        pool.wait_ge(gathered[k], i * (16 * G))
                        nc.gpsimd.tensor_copy(idx[:, k, :], s["srcs"][:, bass.ds(g * G, G)]).then_inc(listed, 1)
                        rows_stored, rows_added = pool.to_reg(i * 16), pool.to_reg(2 * i)
                        listed_now = pool.to_reg(g + 1)
                        pool.wait_ge(att_set, 1)
                        pool.wait_ge(listed, listed_now)
                        pool.wait_ge(spilled[k], rows_stored)
                        pool.wait_ge(summed, rows_added)
                        for n in range(G):
                            nc.gpsimd.indirect_dma_start(
                                out=rows[:, k, n, :], out_offset=None, in_=d["left"][:, :],
                                in_offset=bass.IndirectOffsetOnAxis(ap=idx[:, k, n:n + 1], axis=0),
                            ).then_inc(gathered[k], 16)

            @block.sync
            def _(sp):
                sp.wait_ge(att_set, 1)
                for h in range(H):
                    at = h * C
                    sp.dma_start(attm[at % P:at % P + C, at // P, h:h + 1],
                                 att[h:h + 1, :].rearrange("a c -> c a"),
                                 allow_slow_non_contiguous=True).then_inc(att_in, 16)
                with sp.Fori(0, GROUPS // 2) as i:
                    for k in range(2):
                        g = 2 * i + k
                        sp.wait_ge(gathered[k], i * (16 * G) + 16 * G)
                        sp.dma_start(d["rows"][bass.ds(g, 1), :, :].rearrange("a p f -> (a p) f"),
                                     rows[:, k, :, :].rearrange("p g f -> p (g f)")).then_inc(spilled[k], 16)
                for k in range(2):
                    sp.wait_ge(spilled[k], 16 * (GROUPS // 2))

            @block.vector
            def _(v):
                def hots_of(g, k):
                    nc.vector.tensor_tensor(
                        hots[:, k, :, :],
                        s["iota"][:, :].unsqueeze(1).to_broadcast([P, G, P]),
                        s["dl"][:, bass.ds(g * G, G)].unsqueeze(2).to_broadcast([P, G, P]),
                        ALU.is_equal).then_inc(hot, 1)

                with v.Fori(0, GROUPS // 2) as i:
                    for k in range(2):
                        g = 2 * i + k
                        v.wait_ge(hot_turned, 2 * i)
                        hots_of(g, k)
                        v.wait_ge(spread, g + 1)
                        v.wait_ge(gathered[k], i * (16 * G) + 16 * G)
                        nc.vector.tensor_tensor(S[:, k, :, :].rearrange("p g f -> p (g f)"),
                                                p_row[:, :, :, :].rearrange("p a b f -> p (a b f)"),
                                                rows[:, k, :, :].rearrange("p g f -> p (g f)"),
                                                ALU.add).then_inc(summed, 1)
                        v.wait_ge(summed, g + 1)
                        v.wait_ge(turned, 2 * i)
                        flat = S[:, k, :, :].rearrange("p g f -> p (g f)")
                        nc.vector.scalar_tensor_tensor(L[:, k, :, :].rearrange("p g f -> p (g f)"), flat, SLOPE, flat,
                                                       ALU.mult, ALU.max).then_inc(leaked, 1)

            @block.scalar
            def _(act):
                with act.Fori(0, GROUPS // 2) as i:
                    for k in range(2):
                        g = 2 * i + k
                        act.wait_ge(hot_turned, g + 1)
                        nc.scalar.activation(hotT[:, k, :, :], p_hot[:, :, :], ACT.Copy).then_inc(hot_copied, 1)
                        act.wait_ge(turned, g + 1)
                        act.wait_ge(scored, 2 * i)
                        nc.scalar.activation(LT[:, k, :, :].rearrange("p a b -> p (a b)"),
                                             p_T[:, k, :, :].rearrange("p a b -> p (a b)"),
                                             ACT.Copy).then_inc(turned_copied, 1)
                        act.wait_ge(scored, g + 1)
                        nc.scalar.activation(s["alpha"][:, bass.ds(g * G, G), :], p_a[:, :, :], ACT.Copy).then_inc(kept, 1)

            @block.tensor
            def _(pe):
                pe.wait_ge(att_in, 16 * H)
                with pe.Fori(0, GROUPS // 2) as i:
                    for k in range(2):
                        g = 2 * i + k
                        pe.wait_ge(hot, g + 1)
                        pe.wait_ge(hot_copied, g)
                        for n in range(G):
                            last = nc.tensor.transpose(p_hot[:, n, :], hots[:, k, n, :], s["identb"][:, :])
                        last.then_inc(hot_turned, 1)
                        pe.wait_ge(hot_copied, g + 1)
                        pe.wait_ge(summed, g)
                        for n in range(G):
                            j = nc.tensor.value_load(s["jrow"][0:1, bass.ds(g * G + n, 1)], min_val=0, max_val=NT - 1)
                            for c in range(3):
                                last = nc.tensor.matmul(p_row[:, n // 2, n % 2, :], hotT[:, k, n, :],
                                                        s["right"][:, bass.ds(j, 1), c, :].rearrange("p a f -> p (a f)"),
                                                        start=(c == 0), stop=(c == 2))
                        last.then_inc(spread, 1)
                        pe.wait_ge(leaked, g + 1)
                        pe.wait_ge(turned_copied, 2 * i)
                        for n in range(G * KD):
                            last = nc.tensor.transpose(p_T[:, k, n // 4, (n % 4) * P:(n % 4 + 1) * P],
                                                       L[:, k, n // KD, (n % KD) * P:(n % KD + 1) * P], s["ident"][:, :])
                        last.then_inc(turned, 1)
                        pe.wait_ge(turned_copied, g + 1)
                        pe.wait_ge(kept, g)
                        for n in range(G):
                            for h in range(KD):
                                last = nc.tensor.matmul(p_a[:, n, :], LT[:, k, n * KD + h, :], attm[:, h, :],
                                                        start=(h == 0), stop=(h == KD - 1))
                        last.then_inc(scored, 1)


def segment_softmax(nc, d, s):
    sem = nc.alloc_semaphore
    keys_in, weights_in, logged, floored = sem("m_keys_in"), sem("m_weights_in"), sem("m_logged"), sem("m_floored")
    turned, turned_copied, dve = sem("m_turned"), sem("m_turned_copied"), sem("dve_softmax")
    to_row, row, to_col, col = sem("m_to_row"), sem("m_row"), sem("m_to_col"), sem("m_col")
    shifted, expd, flattened = sem("m_shifted"), sem("m_expd"), sem("m_flattened")
    back, back_copied = sem("m_back"), sem("m_back_copied")
    with ExitStack() as scope:
        def sb(name, shape, dt=F32):
            return scope.enter_context(nc.sbuf_tensor(name, shape, dt))

        A = sb("m_A", [P, SCAN])
        K = sb("m_K", [P, SCAN + 2])
        R = sb("m_R", [P, SCAN + 1])
        M = sb("m_M", [P, SCAN])
        ends = sb("m_ends", [P, 4])
        rows = sb("m_rows", [1, 8, P])
        carry = sb("m_carry", [P, 2])
        flat = sb("m_flat", [P, 2, P])
        pt = scope.enter_context(nc.psum_tensor("m_pt", [P, 2, 512], F32))
        pr = scope.enter_context(nc.psum_tensor("m_pr", [P, 512], F32))
        with nc.Block() as block:
            @block.sync
            def _(sp):
                for h in range(H):
                    sp.dma_start(M[h * BLOCKS:(h + 1) * BLOCKS, :],
                                 d["item_weight"][0:ITEMS, :].rearrange("(b u) e -> b (u e)", b=BLOCKS)).then_inc(weights_in, 16)
                for h in range(H):
                    to = K[h * BLOCKS:(h + 1) * BLOCKS, :]
                    for at, n, c in ((1, SCAN, 1), (0, 1, 0), (SCAN + 1, 1, SCAN + 1)):
                        sp.dma_start(to[:, c:c + n],
                                     d["key"][at:at + BLOCKS * SCAN, :].rearrange("(b e) o -> b (e o)", b=BLOCKS)[:, 0:n]
                                     if at <= 1 else
                                     d["key"][1 + SCAN:1 + SCAN + (BLOCKS - 1) * SCAN + 1, :]
                                     .rearrange("e o -> (e o)")[::SCAN].unsqueeze(1),
                                     allow_slow_non_contiguous=True).then_inc(keys_in, 16)

            @block.vector
            def _(v):
                by_block = s["alpha"][:, :, :].rearrange("p (b u) h -> p u h b", b=BLOCKS)
                with v.Fori(0, U // 2) as i:
                    for k in range(2):
                        v.wait_ge(turned, 2 * i)
                        nc.vector.tensor_copy(flat[:, k, :].rearrange("p (h b) -> p h b", h=H),
                                              by_block[:, bass.ds(2 * i + k, 1), :, :].rearrange("p a h b -> p (a h) b")
                                              ).then_inc(flattened, 1)
                step = Chain(v, dve)
                v.wait_ge(weights_in, 16 * H)
                step(nc.vector.tensor_scalar(R[:, 0:SCAN], M[:, :], TINY_WEIGHT, -BIG, ALU.is_lt, ALU.mult))
                nc.vector.tensor_scalar(M[:, :], M[:, :], TINY_WEIGHT, None, ALU.max).then_inc(floored, 1)
                v.wait_ge(logged, 1)
                v.wait_ge(turned_copied, U)
                step(nc.vector.tensor_tensor(A[:, :], A[:, :], M[:, :], ALU.add))
                step(nc.vector.tensor_tensor(A[:, :], A[:, :], R[:, 0:SCAN], ALU.add))
                v.wait_ge(keys_in, 16 * 3 * H)
                step(nc.vector.tensor_scalar(M[:, :], K[:, 1:SCAN + 1], 0.0, -BIG, ALU.is_lt, ALU.mult))
                step(nc.vector.tensor_tensor(A[:, :], A[:, :], M[:, :], ALU.add))
                step(nc.vector.tensor_tensor(R[:, :], K[:, 0:SCAN + 1], K[:, 1:SCAN + 2], ALU.not_equal))
                step(nc.vector.tensor_scalar(R[:, :], R[:, :], -BIG, None, ALU.mult))
                step(nc.vector.tensor_tensor(ends[:, 3:4], K[:, 1:2], K[:, SCAN:SCAN + 1], ALU.not_equal))
                step(nc.vector.tensor_tensor_scan(M[:, :], R[:, 0:SCAN], A[:, :], -BIG, ALU.add, ALU.max))
                step(nc.vector.tensor_copy(ends[:, 0:1], M[:, SCAN - 1:SCAN]))
                step(nc.vector.tensor_copy(ends[:, 1:2], R[:, 0:1]))
                step(nc.vector.tensor_scalar(ends[:, 2:3], ends[:, 3:4], -BIG, None, ALU.mult))
                nc.vector.engine_nop().then_inc(to_row, 1)
                v.wait_ge(row, 1)
                step(nc.vector.tensor_copy(rows[:, 0:3, :], pr[0:1, 0:3 * P].rearrange("o (c b) -> o c b", c=3)))
                step(nc.vector.memset(rows[:, 3:8, :], -BIG))
                heads = lambda a: rows[:, a, :].rearrange("o (h b) -> o h b", h=H)
                for b in range(1, BLOCKS):
                    step(nc.vector.tensor_tensor(heads(4)[:, :, b:b + 1], heads(3)[:, :, b - 1:b],
                                                 heads(2)[:, :, b - 1:b], ALU.add))
                    step(nc.vector.tensor_tensor(heads(4)[:, :, b:b + 1], heads(4)[:, :, b:b + 1],
                                                 heads(0)[:, :, b - 1:b], ALU.max))
                    step(nc.vector.tensor_tensor(heads(3)[:, :, b:b + 1], heads(4)[:, :, b:b + 1],
                                                 heads(1)[:, :, b:b + 1], ALU.add))
                step(nc.vector.tensor_scalar(rows[:, 3, :], rows[:, 3, :], -BIG, None, ALU.max))
                nc.vector.engine_nop().then_inc(to_col, 1)
                v.wait_ge(col, 1)
                step(nc.vector.tensor_copy(carry[:, 0:1], pr[:, 0:1]))
                step(nc.vector.tensor_tensor_scan(M[:, :], R[:, 0:SCAN], A[:, :], carry[:, 0:1], ALU.add, ALU.max))
                step(nc.vector.tensor_tensor_scan(K[:, SCAN - 1::-1], R[:, SCAN:0:-1], M[:, ::-1], -BIG,
                                                  ALU.add, ALU.max))
                step(nc.vector.tensor_copy(ends[:, 0:1], K[:, 0:1]))
                step(nc.vector.tensor_copy(ends[:, 1:2], R[:, SCAN:SCAN + 1]))
                nc.vector.engine_nop().then_inc(to_row, 1)
                v.wait_ge(row, 2)
                step(nc.vector.tensor_copy(rows[:, 0:3, :], pr[0:1, 0:3 * P].rearrange("o (c b) -> o c b", c=3)))
                step(nc.vector.memset(rows[:, 3:8, :], -BIG))
                for b in range(BLOCKS - 2, -1, -1):
                    step(nc.vector.tensor_tensor(heads(4)[:, :, b:b + 1], heads(3)[:, :, b + 1:b + 2],
                                                 heads(2)[:, :, b + 1:b + 2], ALU.add))
                    step(nc.vector.tensor_tensor(heads(4)[:, :, b:b + 1], heads(4)[:, :, b:b + 1],
                                                 heads(0)[:, :, b + 1:b + 2], ALU.max))
                    step(nc.vector.tensor_tensor(heads(3)[:, :, b:b + 1], heads(4)[:, :, b:b + 1],
                                                 heads(1)[:, :, b:b + 1], ALU.add))
                step(nc.vector.tensor_scalar(rows[:, 3, :], rows[:, 3, :], -BIG, None, ALU.max))
                nc.vector.engine_nop().then_inc(to_col, 1)
                v.wait_ge(col, 2)
                step(nc.vector.tensor_copy(carry[:, 1:2], pr[:, 0:1]))
                step(nc.vector.tensor_tensor_scan(K[:, SCAN - 1::-1], R[:, SCAN:0:-1], M[:, ::-1], carry[:, 1:2],
                                                  ALU.add, ALU.max))
                nc.vector.tensor_tensor(A[:, :], A[:, :], K[:, 0:SCAN], ALU.subtract).then_inc(shifted, 1)

            @block.scalar
            def _(act):
                with act.Fori(0, U // 2) as i:
                    for k in range(2):
                        act.wait_ge(turned, 2 * i + k + 1)
                        nc.scalar.activation(A[:, bass.ds((2 * i + k) * P, P)], pt[:, k, 0:P], ACT.Copy).then_inc(turned_copied, 1)
                act.wait_ge(floored, 1)
                nc.scalar.activation(M[:, :], M[:, :], ACT.Ln).then_inc(logged, 1)
                act.wait_ge(shifted, 1)
                by_block = s["alpha"][:, :, :].rearrange("p (b u) h -> p u h b", b=BLOCKS)
                with act.Fori(0, U // 2) as i:
                    for k in range(2):
                        act.wait_ge(back, 2 * i)
                        nc.scalar.activation(flat[:, k, :], A[:, bass.ds((2 * i + k) * P, P)], ACT.Exp).then_inc(expd, 1)
                        act.wait_ge(back, 2 * i + k + 1)
                        nc.scalar.activation(by_block[:, bass.ds(2 * i + k, 1), :, :].rearrange("p a h b -> p (a h) b"),
                                             pt[:, k, 0:P].rearrange("p (h b) -> p h b", h=H),
                                             ACT.Copy).then_inc(back_copied, 1)

            @block.tensor
            def _(pe):
                with pe.Fori(0, U // 2) as i:
                    for k in range(2):
                        pe.wait_ge(turned_copied, 2 * i)
                        pe.wait_ge(flattened, 2 * i + k + 1)
                        nc.tensor.transpose(pt[:, k, 0:P], flat[:, k, :], s["ident"][:, :]).then_inc(turned, 1)
                for r in range(2):
                    pe.wait_ge(to_row, r + 1)
                    if r:
                        pe.wait_ge(dve, 1)
                    for c in range(3):
                        last = nc.tensor.matmul(pr[0:1, c * P:(c + 1) * P], ends[:, c:c + 1], s["ident"][:, :],
                                                start=True, stop=True)
                    last.then_inc(row, 1)
                    pe.wait_ge(to_col, r + 1)
                    nc.tensor.matmul(pr[:, 0:1], rows[0:1, 3, :], s["ones"][0:1, 0:1], start=True, stop=True).then_inc(col, 1)
                with pe.Fori(0, U // 2) as i:
                    for k in range(2):
                        pe.wait_ge(back_copied, 2 * i)
                        pe.wait_ge(expd, 2 * i + k + 1)
                        nc.tensor.transpose(pt[:, k, 0:P], flat[:, k, :], s["ident"][:, :]).then_inc(back, 1)


def aggregate(nc, d, s):
    sem = nc.alloc_semaphore
    R = 3
    loaded = [sem(f"a_loaded{i}") for i in range(2)]
    cleared, hot, weighted, summed, added = sem("a_cleared"), sem("a_hot"), sem("a_weighted"), sem("a_summed"), sem("a_added")
    with ExitStack() as scope:
        def sb(name, shape, dt=F32):
            return scope.enter_context(nc.sbuf_tensor(name, shape, dt))

        rows = sb("a_rows", [P, 2, G, D])
        hots = sb("a_hots", [P, 2, G, P])
        W = sb("a_W", [P, 2, G, D + H])
        acc = s["acc"]
        ps = scope.enter_context(nc.psum_tensor("a_ps", [P, 2, G, 512], F32))
        with nc.Block() as block:
            @block.gpsimd
            def _(pool):
                nc.gpsimd.memset(acc[:, :, :], 0.0).then_inc(cleared, 1)

            @block.sync
            def _(sp):
                with sp.Fori(0, GROUPS // 2) as i:
                    for k in range(2):
                        g = 2 * i + k
                        sp.wait_ge(weighted, 2 * i)
                        sp.dma_start(rows[:, k, :, :].rearrange("p g f -> p (g f)"),
                                     d["rows"][bass.ds(g, 1), :, :].rearrange("a p f -> (a p) f")).then_inc(loaded[k], 16)

            @block.vector
            def _(v):
                v.wait_ge(cleared, 1)

                def make(i, k):
                    g = 2 * i + k
                    v.wait_ge(summed, 2 * i)
                    nc.vector.tensor_tensor(
                        hots[:, k, :, :], s["iota"][:, :].unsqueeze(1).to_broadcast([P, G, P]),
                        s["dl"][:, bass.ds(g * G, G)].unsqueeze(2).to_broadcast([P, G, P]),
                        ALU.is_equal).then_inc(hot, 1)
                    v.wait_ge(loaded[k], i * 16 + 16)
                    w = s["alpha"][:, bass.ds(g * G, G), :]
                    nc.vector.tensor_copy(W[:, k, :, D:D + H], w)
                    for n in range(G):
                        last = nc.vector.tensor_tensor(
                            W[:, k, n, 0:D].rearrange("p (h c) -> p h c", h=H),
                            rows[:, k, n, :].rearrange("p (h c) -> p h c", h=H),
                            s["alpha"][:, bass.ds(g * G + n, 1), :].rearrange("p a h -> p (a h)").unsqueeze(2).to_broadcast([P, H, C]),
                            ALU.mult)
                    last.then_inc(weighted, 1)

                def add(i, k):
                    g = 2 * i + k
                    v.wait_ge(summed, g + 1)
                    for n in range(G):
                        j = nc.vector.value_load(s["jrow"][0:1, bass.ds(g * G + n, 1)], min_val=0, max_val=NT - 1)
                        to = acc[:, bass.ds(j, 1), :].rearrange("p a f -> p (a f)")
                        v.wait_ge(added, g * G + n)
                        nc.vector.tensor_tensor(to, to, ps[:, k, n, 0:D + H], ALU.add).then_inc(added, 1)

                with v.Fori(0, GROUPS // 2) as i:
                    for k in range(2):
                        make(i, k)
                    for k in range(2):
                        add(i, k)

            @block.tensor
            def _(pe):
                with pe.Fori(0, GROUPS // 2) as i:
                    for k in range(2):
                        g = 2 * i + k
                        pe.wait_ge(weighted, g + 1)
                        pe.wait_ge(hot, g + 1)
                        pe.wait_ge(added, i * (2 * G))
                        for n in range(G):
                            last = nc.tensor.matmul(ps[:, k, n, 0:D + H], hots[:, k, n, :], W[:, k, n, :],
                                                    start=True, stop=True)
                        last.then_inc(summed, 1)


def normalise(nc, s, bias):
    bias_in, dve = nc.alloc_semaphore("n_bias_in"), nc.alloc_semaphore("dve_normalise")
    with nc.sbuf_tensor("n_bias", [P, D], F32) as bb, nc.sbuf_tensor("n_inv", [P, NT, H], F32) as inv, nc.Block() as block:
        @block.sync
        def _(sp):
            sp.dma_start(bb[:, :], bias.partition_broadcast(P)).then_inc(bias_in, 16)

        @block.vector
        def _(v):
            step = Chain(v, dve)
            acc, X = s["acc"], s["X"]
            step(nc.vector.tensor_scalar(inv[:, :, :], acc[:, :, D:D + H], 1e-16, None, ALU.add))
            step(nc.vector.reciprocal(inv[:, :, :], inv[:, :, :]))
            v.wait_ge(bias_in, 16)
            first = step.n
            with v.Fori(0, NT) as i:
                step = Chain(v, dve, first + i * 3)
                a = acc[:, bass.ds(i, 1), 0:D].rearrange("p a f -> p (a f)")
                xi = X[:, bass.ds(i, 1), :].rearrange("p a f -> p (a f)")
                step(nc.vector.tensor_tensor(
                    a.rearrange("p (h c) -> p h c", h=H), a.rearrange("p (h c) -> p h c", h=H),
                    inv[:, bass.ds(i, 1), :].rearrange("p a h -> p (a h)").unsqueeze(2).to_broadcast([P, H, C]), ALU.mult))
                step(nc.vector.tensor_tensor(a, a, bb[:, :], ALU.add))
                step(nc.vector.tensor_tensor(xi, xi, a, ALU.add))


def experts(nc, s, Wg, bg, W1, b1, W2, b2, out):
    sem = nc.alloc_semaphore
    w_in, gate_in, w2_in = sem("e_w_in"), sem("e_gate_in"), sem("e_w2_in")
    sqrt_ready, sqrt_done, dve = sem("e_sqrt_ready"), sem("e_sqrt_done"), sem("dve_experts")
    iota8_set, normed, turned, turned_copied, gated = sem("e_iota8"), sem("e_normed"), sem("e_turned"), sem("e_turned_copied"), sem("e_gated")
    up, gelued, down, added, stored = sem("e_up"), sem("e_gelued"), sem("e_down"), sem("e_added"), sem("e_stored")
    T2 = NT // 2
    CH = 2 * 6
    with ExitStack() as scope:
        def sb(name, shape, dt=F32):
            return scope.enter_context(nc.sbuf_tensor(name, shape, dt))

        X = s["X"]
        w1 = sb("e_w1", [P, EXPERTS, KD, HID])
        w2 = sb("e_w2", [P, EXPERTS, KH, D])
        wg = sb("e_wg", [P, KD, EXPERTS])
        bgb = sb("e_bg", [P, EXPERTS])
        b1c = sb("e_b1", [P, EXPERTS, KH])
        b2b = sb("e_b2", [P, EXPERTS, D])
        iota8 = sb("e_iota8s", [P, EXPERTS])
        stats, mv, std = sb("e_stats", [P, NT, 6]), sb("e_mv", [P, NT, 2]), sb("e_std", [P, 3, NT])
        xn = sb("e_xn", [P, 2, D])
        xT = sb("e_xT", [P, KD, 2 * P])
        g8 = sb("e_g8", [P, 2, 8])
        top = sb("e_top", [P, 2, 8])
        topi = sb("e_topi", [P, 2, 8], U32)
        topf = sb("e_topf", [P, 2, 8])
        mask = sb("e_mask", [P, 2, 8])
        hT = sb("e_hT", [P, 2, KH, 2 * P])
        tmp = sb("e_tmp", [P, 2, D])
        pt = scope.enter_context(nc.psum_tensor("e_pt", [P, 512], F32))
        pg = scope.enter_context(nc.psum_tensor("e_pg", [P, 2, 8], F32))
        ph = scope.enter_context(nc.psum_tensor("e_ph", [P, 2, KH, 2 * P], F32))
        py = scope.enter_context(nc.psum_tensor("e_py", [P, 2, 2 * D], F32))
        full = N // P
        rest = N - full * P
        with nc.Block() as block:
            @block.gpsimd
            def _(pool):
                nc.gpsimd.iota(iota8[:, :], [[1, EXPERTS]], base=0, channel_multiplier=0,
                               allow_small_or_imprecise_dtypes=True).then_inc(iota8_set, 1)

            @block.sync
            def _(sp):
                sp.dma_start(wg[:, :, :], Wg.rearrange("(k p) e -> p k e", p=P)).then_inc(gate_in, 16)
                sp.dma_start(bgb[:, :], bg.partition_broadcast(P)).then_inc(gate_in, 16)
                sp.dma_start(b1c[:, :, :], b1.rearrange("e (k p) -> p e k", p=P), allow_slow_non_contiguous=True).then_inc(gate_in, 16)
                sp.dma_start(b2b[:, :, :], b2.rearrange("e f -> (e f)").partition_broadcast(P)
                             .rearrange("p (e f) -> p e f", e=EXPERTS)).then_inc(gate_in, 16)
                sp.dma_start(w1[:, :, :, :], W1.rearrange("e (k p) f -> p e k f", p=P)).then_inc(w_in, 16)
                sp.dma_start(w2[:, :, :, :], W2.rearrange("e (k p) f -> p e k f", p=P)).then_inc(w_in, 16)
                sp.wait_ge(added, T2 * EXPERTS * 2)
                sp.dma_start(out[0:full * P, :].rearrange("(t p) f -> p t f", p=P), X[:, 0:full, :]).then_inc(stored, 16)
                sp.dma_start(out[full * P:N, :], X[0:rest, full, :]).then_inc(stored, 16)
                sp.wait_ge(stored, 32)

            @block.vector
            def _(v):
                step = Chain(v, dve)
                moments(nc, v, step, stats, mv, std, X, sqrt_ready, sqrt_done)
                v.wait_ge(gate_in, 64)
                v.wait_ge(iota8_set, 1)
                first = step.n
                with v.Fori(0, T2) as i:
                    step = Chain(v, dve, first + i * (CH + 2 * EXPERTS))
                    for k in range(2):
                        t = 2 * i + k
                        nc.vector.tensor_scalar(xn[:, k, :], X[:, bass.ds(t, 1), :].rearrange("p a f -> p (a f)"),
                                                mv[:, bass.ds(t, 1), 0], std[:, 2, bass.ds(t, 1)],
                                                ALU.subtract, ALU.mult).then_inc(normed, 1)
                    v.wait_ge(gated, i + 1)
                    for k in range(2):
                        step(nc.vector.tensor_tensor(g8[:, k, :], pg[:, k, :], bgb[:, :], ALU.add), iota8_set)
                        step(nc.vector.max(top[:, k, :], g8[:, k, :]), iota8_set)
                        step(nc.vector.max_index(topi[:, k, :], top[:, k, :], g8[:, k, :]))
                        step(nc.vector.tensor_copy(topf[:, k, :], topi[:, k, :]))
                        step(nc.vector.tensor_scalar(mask[:, k, :], iota8[:, :], topf[:, k, 0:1], None, ALU.is_equal))
                        step(nc.vector.scalar_tensor_tensor(mask[:, k, :], iota8[:, :], topf[:, k, 1:2], mask[:, k, :],
                                                            ALU.is_equal, ALU.add))
                    for e in range(EXPERTS):
                        v.wait_ge(down, i * EXPERTS + e + 1)
                        for k in range(2):
                            xi = X[:, bass.ds(2 * i + k, 1), :].rearrange("p a f -> p (a f)")
                            step(nc.vector.tensor_tensor(tmp[:, k, :], py[:, e % 2, k * D:(k + 1) * D], b2b[:, e, :], ALU.add))
                            v.wait_ge(added, i * (2 * EXPERTS) + 2 * e + k)
                            nc.vector.scalar_tensor_tensor(xi, tmp[:, k, :], mask[:, k, e:e + 1], xi,
                                                           ALU.mult, ALU.add).then_inc(added, 1)

            @block.scalar
            def _(act):
                act.wait_ge(sqrt_ready, 1)
                nc.scalar.activation(std[:, 1, :], std[:, 0, :], ACT.Sqrt).then_inc(sqrt_done, 1)
                with act.Fori(0, T2) as i:
                    act.wait_ge(turned, i + 1)
                    act.wait_ge(up, i * EXPERTS)
                    nc.scalar.activation(xT[:, :, :].rearrange("p k t -> p (k t)"), pt[:, :], ACT.Copy).then_inc(turned_copied, 1)
                    for e in range(EXPERTS):
                        act.wait_ge(up, i * EXPERTS + e + 1)
                        if e >= 2:
                            act.wait_ge(down, i * EXPERTS + e - 1)
                        else:
                            act.wait_ge(down, i * EXPERTS)
                        for m in range(KH):
                            last = nc.scalar.activation(hT[:, e % 2, m, :], ph[:, e % 2, m, :], ACT.Gelu,
                                                        bias=b1c[:, e, m:m + 1])
                        last.then_inc(gelued, 1)

            @block.tensor
            def _(pe):
                pe.wait_ge(gate_in, 64)
                pe.wait_ge(w_in, 32)

                def up_of(i, e):
                    if e >= 2:
                        pe.wait_ge(gelued, i * EXPERTS + e - 1)
                    else:
                        pe.wait_ge(gelued, i * EXPERTS)
                    for m in range(KH):
                        for h in range(KD):
                            last = nc.tensor.matmul(ph[:, e % 2, m, :], w1[:, e, h, m * P:(m + 1) * P], xT[:, h, :],
                                                    start=(h == 0), stop=(h == KD - 1))
                    last.then_inc(up, 1)

                def down_of(i, e):
                    pe.wait_ge(gelued, i * EXPERTS + e + 1)
                    if e >= 2:
                        pe.wait_ge(added, i * (2 * EXPERTS) + 2 * e - 2)
                    else:
                        pe.wait_ge(added, i * (2 * EXPERTS))
                    for k in range(2):
                        for m in range(KH):
                            last = nc.tensor.matmul(py[:, e % 2, k * D:(k + 1) * D], hT[:, e % 2, m, k * P:(k + 1) * P],
                                                    w2[:, e, m, :], start=(m == 0), stop=(m == KH - 1))
                    last.then_inc(down, 1)

                with pe.Fori(0, T2) as i:
                    pe.wait_ge(normed, 2 * i + 2)
                    for k in range(2):
                        for h in range(KD):
                            last = nc.tensor.transpose(pt[:, h * 2 * P + k * P:h * 2 * P + (k + 1) * P],
                                                       xn[:, k, h * P:(h + 1) * P], s["ident"][:, :])
                    last.then_inc(turned, 1)
                    pe.wait_ge(turned_copied, i + 1)
                    for k in range(2):
                        for h in range(KD):
                            last = nc.tensor.matmul(pg[:, k, :], xT[:, h, k * P:(k + 1) * P], wg[:, h, :],
                                                    start=(h == 0), stop=(h == KD - 1))
                    last.then_inc(gated, 1)
                    up_of(i, 0)
                    for e in range(EXPERTS):
                        if e + 1 < EXPERTS:
                            up_of(i, e + 1)
                        down_of(i, e)


_INS = ["x", "src", "dst", "edge_weight", "L0_gnn_W_l", "L0_gnn_b_l", "L0_gnn_W_r", "L0_gnn_b_r", "L0_gnn_att",
        "L0_gnn_bias", "L0_ffn_Wg", "L0_ffn_bg", "L0_ffn_W1", "L0_ffn_b1", "L0_ffn_W2", "L0_ffn_b2"]


def kernel(**inputs):
    import numpy as np
    import concourse.bacc as bacc
    from concourse.bass_utils import run_bass_kernel_spmd

    nc = bacc.Bacc("TRN2", target_bir_lowering=False, num_devices=1)
    arrays, args = {}, []
    for name in _INS:
        a = np.ascontiguousarray(inputs[name])
        arrays[f"in_{name}"] = a
        args.append(nc.dram_tensor(f"in_{name}", a.shape, mybir.dt.from_np(a.dtype), kind="ExternalInput").ap())
    args.append(nc.dram_tensor("out", (N, D), F32, kind="ExternalOutput").ap())
    build(nc, *args)
    return run_bass_kernel_spmd(nc, [arrays], core_ids=[0]).results[0]["out"]
```

```python
from contextlib import ExitStack

import concourse.bass as bass
from concourse import mybir

F32 = mybir.dt.float32
BF16 = mybir.dt.bfloat16
I32 = mybir.dt.int32
U32 = mybir.dt.uint32
ALU = mybir.AluOpType
ACT = mybir.ActivationFunctionType
AX = mybir.AxisListType

P = 128
N, D = 6250, 256
E = 100000
H, C = 8, 32
EXPERTS, HID = 8, 512
KD = D // P
KH = HID // P
SLOPE = 0.2
EPS = 1e-5

NT = 50
NODE_TILES = -(-N // P)
ET = -(-E // P)
EPAD = ET * P
ITEMS = -(-(ET + NODE_TILES - 1) // 64) * 64
QI = -(-ITEMS // P)
BLOCKS = P // H
U = ITEMS // BLOCKS
SCAN = U * P
PAD_DST = NODE_TILES * P - 1
BIG = 1e30
SLOT_TILES = -(-((2 * N + EXPERTS * (P - 1)) // P) // 4) * 4
TINY_WEIGHT = 1e-19


class Chain:

    def __init__(self, eng, sem, base=0):
        self.eng, self.sem, self.base, self.n = eng, sem, base, 0

    def __call__(self, ins, constant=None):
        self.n += 1
        ins.then_inc(self.sem, 1)
        if constant is not None:
            goal = self.eng.to_reg(self.base + self.n)
            self.eng.wait_ge(constant, 1)
            self.eng.wait_ge(self.sem, goal)
            return
        self.eng.wait_ge(self.sem, self.base + self.n)


UN = 4


class Step:

    def __init__(self, i, c):
        self.i, self.c = i, c
        self.n = i * UN + c

    def ahead(self, by):
        return Step(self.i, self.c + by)

    def slot(self, ring):
        return self.c % ring

    def turn(self, ring):
        return self.i * (UN // ring) + self.c // ring


def wait(eng, sem, value):
    if not (isinstance(value, int) and value <= 0):
        eng.wait_ge(sem, value)


def pipeline(eng, steps, stages):
    most, least = max(a for a, _ in stages), min(a for a, _ in stages)

    def at(i, c):
        for by, stage in stages:
            g = Step(i, c + by)
            if not isinstance(i, int) or 0 <= g.n < steps:
                stage(g)

    turns = (steps - max(most, 0)) // UN
    for c in range(-most, UN):
        at(0, c)
    with eng.Fori(1, turns) as i:
        for c in range(UN):
            at(i, c)
    for c in range(turns * UN, steps - least):
        at(0, c)


def build(nc, x, src, dst, edge_weight, W_l, b_l, W_r, b_r, att, bias, Wg, bg, W1, b1, W2, b2, out):
    with ExitStack() as whole:
        def keep(name, shape, dt=F32):
            return whole.enter_context(nc.sbuf_tensor(name, shape, dt))

        def dram(name, shape, dt=F32):
            return nc.dram_tensor(name, shape, dt, kind="Internal").ap()

        d = dict(
            src=dram("src_tiles", (ET, P), I32), dst=dram("dst_tiles", (ET, P), I32),
            weight=dram("weight_tiles", (ET, P)),
            key=dram("item_keys", (1 + QI * P * P + 1, 1)), item_weight=dram("item_weights", (QI * P, P)),
            node_tile=dram("item_node_tile", (QI * P, 1), I32),
            left=dram("left_rows", (NT * P, D)),
            rows=dram("item_rows", (ITEMS // 4, P, 4 * D)),
            slots_in=dram("slots_in", (SLOT_TILES * P, D)), slots_out=dram("slots_out", (SLOT_TILES * P, D)),
        )
        s = dict(
            ident=keep("ident", [P, P]), identb=keep("identb", [P, P], BF16),
            iota=keep("iota_row", [P, P]), ones=keep("ones_row", [1, P]),
            X=keep("X", [P, NT, D]),
            slot_of=keep("slot_of", [P, NT, 2], I32), tile_expert=keep("tile_expert", [1, P], I32),
        )
        constants(nc, s)
        with ExitStack() as graph:
            def held(name, shape, dt=F32):
                s[name] = graph.enter_context(nc.sbuf_tensor(name, shape, dt))

            held("jrow", [1, QI * P], I32)
            held("dl", [P, QI * P])
            held("alpha", [P, ITEMS, H])
            with ExitStack() as scope:
                s["srcs"] = scope.enter_context(nc.sbuf_tensor("item_src", [P, QI * P], I32))
                schedule(nc, d, s, src, dst, edge_weight)
                s["right"] = scope.enter_context(nc.sbuf_tensor("right_rows", [P, NT, 3, D], BF16))
                project(nc, d, s, x, W_l, b_l, W_r, b_r, bias)
                scores(nc, d, s, att)
            segment_softmax(nc, d, s)
            held("acc", [P, NT, D + H])
            aggregate(nc, d, s)
            route(nc, s, Wg, bg)
            spread_tokens(nc, d, s)
        experts(nc, d, s, W1, b1, W2, b2)
        combine(nc, d, s, out)


def constants(nc, s):
    set_, ramp = nc.alloc_semaphore("const_set"), nc.alloc_semaphore("const_ramp")
    with nc.Block() as block:
        @block.gpsimd
        def _(pool):
            nc.gpsimd.memset(s["ident"][:, :], 0.0).then_inc(set_, 1)
            nc.gpsimd.memset(s["identb"][:, :], 0.0).then_inc(set_, 1)
            nc.gpsimd.memset(s["ones"][:, :], 1.0)
            nc.gpsimd.iota(s["iota"][:, :], [[1, P]], base=0, channel_multiplier=0,
                           allow_small_or_imprecise_dtypes=True).then_inc(ramp, 1)
            pool.wait_ge(set_, 2)
            for m in ("ident", "identb"):
                nc.gpsimd.affine_select(out=s[m][:, :], in_=s[m][:, :], compare_op=ALU.not_equal, fill=1.0,
                                        base=0, pattern=[[-1, P]], channel_multiplier=1).then_inc(ramp, 1)
            pool.wait_ge(ramp, 3)


def schedule(nc, d, s, src, dst, edge_weight):
    sem = nc.alloc_semaphore
    pads_set, padded, ends_in, ends_done = sem("pads_set"), sem("padded"), sem("ends_in"), sem("ends_done")
    spread, spread_copied, items_done = sem("spread"), sem("spread_copied"), sem("items_done")
    gathered = [sem(f"gathered{i}") for i in range(3)]
    local_done, turned, turned_copied = sem("local_done"), sem("turned"), sem("turned_copied")
    zero_set, zeroed = sem("zero_set"), sem("zeroed")
    stored, row_in, dve, numbered = sem("stored"), sem("row_in"), sem("dve_schedule"), sem("numbered")
    with ExitStack() as scope:
        def sb(name, shape, dt=F32):
            return scope.enter_context(nc.sbuf_tensor(name, shape, dt))

        npad = EPAD - E
        pad_d, pad_s, pad_w = sb("pad_d", [1, npad], I32), sb("pad_s", [1, npad], I32), sb("pad_w", [1, npad])
        pad_k = sb("pad_k", [1, 2])
        zero = sb("zero", [P, 4 * D])
        ends = sb("ends", [1, 2, ET], I32)
        tile_i = sb("tile_i", [1, 2, ET], I32)
        tile_f = sb("tile_f", [1, 2, ET])
        count = sb("count", [1, ET])
        cum = sb("cum", [1, ET])
        one = sb("one", [1, ET])
        offs = sb("offs", [1, 2, ET])
        offs_all = sb("offs_all", [P, 2, ET])
        number = sb("number", [P, QI])
        work = sb("work", [P, ET])
        found = sb("found", [P, 3, QI])
        jt = sb("jt", [P, QI])
        t_idx, j_idx, base = sb("t_idx", [P, QI], I32), sb("j_idx", [P, QI], I32), sb("base", [P, QI])
        rows_s, rows_d = sb("rows_s", [P, QI, P], I32), sb("rows_d", [P, QI, P], I32)
        rows_w = sb("rows_w", [P, QI, P])
        sf, df = sb("sf", [P, QI, P]), sb("df", [P, QI, P])
        local, live, key = sb("local", [P, QI, P]), sb("live", [P, QI, P]), sb("key", [P, QI, P])
        ps = scope.enter_context(nc.psum_tensor("ps_spread", [P, 4, 512], F32))
        pt = scope.enter_context(nc.psum_tensor("ps_turn", [P, 2, 512], F32))
        half = ET // 2
        with nc.Block() as block:
            @block.gpsimd
            def _(pool):
                nc.gpsimd.memset(zero[:, :], 0.0).then_inc(zero_set, 1)
                nc.gpsimd.memset(pad_d[:, :], PAD_DST).then_inc(pads_set, 1)
                nc.gpsimd.memset(pad_s[:, :], 0).then_inc(pads_set, 1)
                nc.gpsimd.memset(pad_w[:, :], 1.0).then_inc(pads_set, 1)
                nc.gpsimd.memset(pad_k[:, :], -2.0).then_inc(pads_set, 1)
                nc.gpsimd.memset(one[:, :], 1.0).then_inc(pads_set, 1)
                nc.gpsimd.iota(number[:, :], [[P, QI]], base=0, channel_multiplier=1,
                               allow_small_or_imprecise_dtypes=True).then_inc(numbered, 1)
                pool.wait_ge(items_done, 1)
                pool.wait_ge(padded, 16 * 6)
                for q in range(QI):
                    for i, (rows, table) in enumerate(((rows_d, "dst"), (rows_s, "src"), (rows_w, "weight"))):
                        nc.gpsimd.indirect_dma_start(
                            out=rows[:, q, :], out_offset=None, in_=d[table][:, :],
                            in_offset=bass.IndirectOffsetOnAxis(ap=t_idx[:, q:q + 1], axis=0),
                        ).then_inc(gathered[i], 16)

            @block.sync
            def _(sp):
                flat = {k: d[k].rearrange("t p -> (t p)") for k in ("src", "dst", "weight")}
                for k, a in (("src", src), ("dst", dst), ("weight", edge_weight)):
                    sp.dma_start(flat[k][0:E].rearrange("(a b) -> a b", a=16),
                                 a.rearrange("(a b) -> a b", a=16)).then_inc(padded, 16)
                sp.wait_ge(pads_set, 5)
                for k, pad in (("src", pad_s), ("dst", pad_d), ("weight", pad_w)):
                    sp.dma_start(flat[k][E:EPAD].rearrange("(a b) -> a b", a=1), pad[:, :]).then_inc(padded, 16)
                for at, i in ((0, 0), (1 + QI * P * P, 1)):
                    sp.dma_start(d["key"][at:at + 1, :], pad_k[:, i:i + 1]).then_inc(stored, 16)
                sp.wait_ge(padded, 16 * 6)
                for i, at in ((0, 0), (1, P - 1)):
                    sp.dma_start(ends[:, i:i + 1, :].rearrange("a i t -> a (i t)"),
                                 d["dst"][:, at:at + 1].rearrange("t o -> o t"),
                                 allow_slow_non_contiguous=True).then_inc(ends_in, 16)
                sp.wait_ge(items_done, 1)
                sp.dma_start(d["node_tile"].rearrange("(q p) o -> p (q o)", p=P), j_idx[:, :],
                             allow_slow_non_contiguous=True).then_inc(stored, 16)
                sp.wait_ge(local_done, 2)
                sp.dma_start(d["key"][1:1 + QI * P * P, :].rearrange("(q p e) o -> p q (e o)", p=P, q=QI),
                             key[:, :, :]).then_inc(stored, 16)
                sp.wait_ge(gathered[2], 16 * QI)
                sp.dma_start(d["item_weight"].rearrange("(q p) e -> p q e", p=P), rows_w[:, :, :]).then_inc(stored, 16)
                sp.wait_ge(stored, 16 * 5)
                sp.dma_start(s["jrow"][:, :], d["node_tile"].rearrange("n o -> o n"),
                             allow_slow_non_contiguous=True).then_inc(row_in, 16)
                sp.wait_ge(row_in, 16)

            @block.tensor
            def _(pe):
                pe.wait_ge(ends_done, 1)
                for a in range(2):
                    for b in range(2):
                        last = nc.tensor.matmul(ps[:, 2 * a + b, 0:half], s["ones"][0:1, :],
                                                offs[0:1, a, b * half:(b + 1) * half], start=True, stop=True)
                last.then_inc(spread, 1)
                for i in range(2 * QI):
                    pe.wait_ge(local_done, 1 if i < QI else 3)
                    if i >= 2:
                        pe.wait_ge(turned_copied, i - 1)
                    from_ = local if i < QI else sf
                    nc.tensor.transpose(pt[:, i % 2, 0:P], from_[:, i % QI, :], s["ident"][:, :]).then_inc(turned, 1)

            @block.scalar
            def _(act):
                act.wait_ge(zero_set, 1)
                for t in range(0, SLOT_TILES, 4):
                    act.dma_start(d["slots_in"][t * P:(t + 4) * P, :].rearrange("(p a) f -> p (a f)", a=4),
                                  zero[:, :]).then_inc(zeroed, 16)
                for i in range(2 * QI):
                    act.wait_ge(turned, i + 1)
                    to = (s["dl"] if i < QI else s["srcs"])[:, (i % QI) * P:(i % QI + 1) * P]
                    nc.scalar.activation(to, pt[:, i % 2, 0:P], ACT.Copy).then_inc(turned_copied, 1)
                act.wait_ge(zeroed, 16 * (SLOT_TILES // 4))

            @block.vector
            def _(v):
                step = Chain(v, dve)
                v.wait_ge(ends_in, 32)
                step(nc.vector.tensor_scalar(tile_i[:, :, :], ends[:, :, :], 7, None, ALU.logical_shift_right))
                step(nc.vector.tensor_copy(tile_f[:, :, :], tile_i[:, :, :]))
                step(nc.vector.scalar_tensor_tensor(count[:, :], tile_f[:, 1, :], 1.0, tile_f[:, 0, :],
                                                    ALU.add, ALU.subtract))
                v.wait_ge(pads_set, 5)
                step(nc.vector.tensor_tensor_scan(cum[:, :], one[:, :], count[:, :], 0.0, ALU.mult, ALU.add))
                step(nc.vector.tensor_tensor(offs[:, 0, :], cum[:, :], count[:, :], ALU.subtract))
                nc.vector.tensor_copy(offs[:, 1, :], tile_f[:, 0, :]).then_inc(ends_done, 1)
                v.wait_ge(spread, 1)
                for a in range(2):
                    step(nc.vector.tensor_copy(offs_all[:, a, :].rearrange("p (b n) -> p b n", b=2),
                                               ps[:, 2 * a:2 * a + 2, 0:half]))
                v.wait_ge(numbered, 1)
                for q in range(QI):
                    own = number[:, q:q + 1]
                    step(nc.vector.tensor_scalar(work[:, :], offs_all[:, 0, :], own, None, ALU.is_le))
                    step(nc.vector.tensor_reduce(found[:, 0, q:q + 1], work[:, :], AX.X, ALU.add))
                    for a in range(2):
                        step(nc.vector.scalar_tensor_tensor(work[:, :], offs_all[:, 0, :], own, offs_all[:, a, :],
                                                            ALU.is_le, ALU.mult))
                        step(nc.vector.tensor_reduce(found[:, 1 + a, q:q + 1], work[:, :], AX.X, ALU.max))
                step(nc.vector.tensor_scalar(t_idx[:, :], found[:, 0, :], -1.0, None, ALU.add))
                step(nc.vector.tensor_tensor(jt[:, :], found[:, 2, :], number[:, :], ALU.add))
                step(nc.vector.tensor_tensor(jt[:, :], jt[:, :], found[:, 1, :], ALU.subtract))
                step(nc.vector.tensor_scalar(base[:, :], jt[:, :], float(P), None, ALU.mult))
                nc.vector.tensor_scalar(j_idx[:, :], jt[:, :], float(NT - 1), None, ALU.min).then_inc(items_done, 1)
                v.wait_ge(gathered[0], 16 * QI)
                step(nc.vector.tensor_copy(df[:, :, :], rows_d[:, :, :]))
                for q in range(QI):
                    last = nc.vector.tensor_scalar(local[:, q, :], df[:, q, :], base[:, q:q + 1], None, ALU.subtract)
                last.then_inc(local_done, 1)
                v.wait_ge(local_done, 1)
                step(nc.vector.tensor_scalar(live[:, :, :], local[:, :, :], 0.0, None, ALU.is_ge))
                step(nc.vector.scalar_tensor_tensor(live[:, :, :], local[:, :, :], float(P), live[:, :, :],
                                                    ALU.is_lt, ALU.mult))
                step(nc.vector.scalar_tensor_tensor(key[:, :, :], df[:, :, :], 1.0, live[:, :, :],
                                                    ALU.add, ALU.mult))
                nc.vector.tensor_scalar(key[:, :, :], key[:, :, :], -1.0, None, ALU.add).then_inc(local_done, 1)
                v.wait_ge(gathered[1], 16 * QI)
                nc.vector.tensor_copy(sf[:, :, :], rows_s[:, :, :]).then_inc(local_done, 1)


def moments(nc, v, step, stats, mv, std, X, sqrt_ready, sqrt_done):
    for i in range(NT):
        last = nc.vector.bn_stats(stats[:, i, :], X[:, i, :])
    step(last)
    for i in range(NT):
        last = nc.vector.bn_aggr(mv[:, i, :], stats[:, i, :])
    step(last)
    nc.vector.tensor_scalar(std[:, 0, :], mv[:, :, 1], EPS, None, ALU.add).then_inc(sqrt_ready, 1)
    v.wait_ge(sqrt_done, 1)
    step(nc.vector.reciprocal(std[:, 2, :], std[:, 1, :]))


def project(nc, d, s, x, W_l, b_l, W_r, b_r, bias):
    sem = nc.alloc_semaphore
    x_in, w_in, cleared = sem("x_in"), sem("w_in"), sem("x_cleared")
    sqrt_ready, sqrt_done, dve = sem("p_sqrt_ready"), sem("p_sqrt_done"), sem("dve_project")
    normed, turned, turned_copied = sem("p_normed"), sem("p_turned"), sem("p_turned_copied")
    projected, biased, high, less_high = sem("p_projected"), sem("p_biased"), sem("p_high"), sem("p_less_high")
    middle, less_middle, low, residual = sem("p_middle"), sem("p_less_middle"), sem("p_low"), sem("p_residual")
    stored = [sem(f"left_stored{i}") for i in range(4)]
    with ExitStack() as scope:
        def sb(name, shape, dt=F32):
            return scope.enter_context(nc.sbuf_tensor(name, shape, dt))

        X = s["X"]
        W = sb("p_W", [P, KD, 2 * D])
        bb = sb("p_b", [P, 3 * D])
        stats, mv, std = sb("p_stats", [P, NT, 6]), sb("p_mv", [P, NT, 2]), sb("p_std", [P, 3, NT])
        xn = sb("p_xn", [P, 2, D])
        xT = sb("p_xT", [P, 2, KD * P])
        y = sb("p_y", [P, 4, 2 * D])
        r1, r2 = sb("p_r1", [P, 2, D]), sb("p_r2", [P, 2, D])
        pt = scope.enter_context(nc.psum_tensor("p_pt", [P, 2, 512], F32))
        py = scope.enter_context(nc.psum_tensor("p_py", [P, 2, 512], F32))
        full = N // P
        rest = N - full * P

        def row(g):
            return X[:, bass.ds(g.n, 1), :].rearrange("p a f -> p (a f)")

        def part(g, c):
            return s["right"][:, bass.ds(g.n, 1), c, :].rearrange("p a f -> p (a f)")

        with nc.Block() as block:
            @block.gpsimd
            def _(pool):
                nc.gpsimd.memset(X[:, full:NT, :], 0.0).then_inc(cleared, 1)
                pool.wait_ge(w_in, 80)

                def add_bias(g):
                    wait(pool, normed, g.n + 1)
                    nc.gpsimd.tensor_tensor(row(g), row(g), bb[:, 2 * D:3 * D], ALU.add).then_inc(residual, 1)

                pipeline(pool, NT, [(0, add_bias)])

            @block.sync
            def _(sp):
                sp.dma_start(X[:, 0:full, :], x[0:full * P, :].rearrange("(t p) f -> p t f", p=P)).then_inc(x_in, 16)
                sp.wait_ge(cleared, 1)
                sp.dma_start(X[0:rest, full, :], x[full * P:N, :]).then_inc(x_in, 16)
                for i, w in enumerate((W_l, W_r)):
                    sp.dma_start(W[:, :, i * D:(i + 1) * D], w.rearrange("(k p) f -> p k f", p=P)).then_inc(w_in, 16)
                for i, b in enumerate((b_l, b_r, bias)):
                    sp.dma_start(bb[:, i * D:(i + 1) * D], b.partition_broadcast(P)).then_inc(w_in, 16)

                def store(g):
                    wait(sp, biased, g.n + 1)
                    sp.dma_start(d["left"][bass.ds(g.n * P, P), :], y[:, g.slot(4), 0:D]).then_inc(stored[g.slot(4)], 16)

                pipeline(sp, NT, [(0, store)])
                for k in range(4):
                    sp.wait_ge(stored[k], 16 * len(range(k, NT, 4)))

            @block.vector
            def _(v):
                step = Chain(v, dve)
                v.wait_ge(x_in, 32)
                moments(nc, v, step, stats, mv, std, X, sqrt_ready, sqrt_done)
                v.wait_ge(w_in, 80)

                def norm(g):
                    wait(v, turned, g.n - 1)
                    nc.vector.tensor_scalar(xn[:, g.slot(2), :], row(g), mv[:, bass.ds(g.n, 1), 0],
                                            std[:, 2, bass.ds(g.n, 1)], ALU.subtract, ALU.mult).then_inc(normed, 1)

                def add_biases(g):
                    wait(v, projected, g.n + 1)
                    wait(v, stored[g.slot(4)], g.turn(4) * 16)
                    wait(v, less_high, g.n - 3)
                    nc.vector.tensor_tensor(y[:, g.slot(4), :], py[:, g.slot(2), :], bb[:, 0:2 * D],
                                            ALU.add).then_inc(biased, 1)

                def take_high(g):
                    wait(v, high, g.n + 1)
                    wait(v, middle, g.n - 1)
                    wait(v, less_middle, g.n - 1)
                    nc.vector.tensor_tensor(r1[:, g.slot(2), :], y[:, g.slot(4), D:2 * D], part(g, 0),
                                            ALU.subtract).then_inc(less_high, 1)

                def take_middle(g):
                    wait(v, middle, g.n + 1)
                    wait(v, low, g.n - 1)
                    nc.vector.tensor_tensor(r2[:, g.slot(2), :], r1[:, g.slot(2), :], part(g, 1),
                                            ALU.subtract).then_inc(less_middle, 1)

                pipeline(v, NT, [(2, norm), (0, add_biases), (-1, take_high), (-2, take_middle)])

            @block.scalar
            def _(act):
                act.wait_ge(sqrt_ready, 1)
                nc.scalar.activation(std[:, 1, :], std[:, 0, :], ACT.Sqrt).then_inc(sqrt_done, 1)

                def copy_turned(g):
                    wait(act, turned, g.n + 1)
                    wait(act, projected, g.n - 1)
                    nc.scalar.activation(xT[:, g.slot(2), :], pt[:, g.slot(2), 0:KD * P], ACT.Copy).then_inc(turned_copied, 1)

                def copy_high(g):
                    wait(act, biased, g.n + 1)
                    nc.scalar.activation(part(g, 0), y[:, g.slot(4), D:2 * D], ACT.Copy).then_inc(high, 1)

                def copy_middle(g):
                    wait(act, less_high, g.n + 1)
                    nc.scalar.activation(part(g, 1), r1[:, g.slot(2), :], ACT.Copy).then_inc(middle, 1)

                def copy_low(g):
                    wait(act, less_middle, g.n + 1)
                    nc.scalar.activation(part(g, 2), r2[:, g.slot(2), :], ACT.Copy).then_inc(low, 1)

                pipeline(act, NT, [(1, copy_turned), (0, copy_high), (-1, copy_middle), (-2, copy_low)])

            @block.tensor
            def _(pe):
                pe.wait_ge(w_in, 80)

                def turn(g):
                    wait(pe, normed, g.n + 1)
                    wait(pe, turned_copied, g.n - 1)
                    for h in range(KD):
                        last = nc.tensor.transpose(pt[:, g.slot(2), h * P:(h + 1) * P],
                                                   xn[:, g.slot(2), h * P:(h + 1) * P], s["ident"][:, :])
                    last.then_inc(turned, 1)

                def multiply(g):
                    wait(pe, turned_copied, g.n + 1)
                    wait(pe, biased, g.n - 1)
                    for h in range(KD):
                        last = nc.tensor.matmul(py[:, g.slot(2), :], xT[:, g.slot(2), h * P:(h + 1) * P], W[:, h, :],
                                                start=(h == 0), stop=(h == KD - 1))
                    last.then_inc(projected, 1)

                pipeline(pe, NT, [(1, turn), (0, multiply)])


G = 4
RING = 4
GROUPS = ITEMS // G


def node_tiles(eng, regs, s, g):
    eng.load(regs, s["jrow"][0:1, bass.ds(g.n * G, G)])
    return [eng.snap(r, min_val=0, max_val=NT - 1) for r in regs]


def scores(nc, d, s, att):
    sem = nc.alloc_semaphore
    att_in, att_set = sem("att_in"), sem("att_set")
    listed = sem("listed")
    gathered = [sem(f"g_gathered{i}") for i in range(RING)]
    spilled = [sem(f"g_spilled{i}") for i in range(RING)]
    hot, hot_turned, hot_copied = sem("g_hot"), sem("g_hot_turned"), sem("g_hot_copied")
    spread, summed, leaked = sem("g_spread"), sem("g_summed"), sem("g_leaked")
    turned, turned_copied, scored, kept = sem("g_turned"), sem("g_turned_copied"), sem("g_scored"), sem("g_kept")
    with ExitStack() as scope:
        def sb(name, shape, dt=F32):
            return scope.enter_context(nc.sbuf_tensor(name, shape, dt))

        def pb(name, shape, dt=F32):
            return scope.enter_context(nc.psum_tensor(name, shape, dt))

        idx = sb("idx", [P, RING, G], I32)
        rows = sb("rows", [P, RING, G, D])
        hots = sb("hots", [P, 2, G, P], BF16)
        hotT = sb("hotT", [P, 2, G, P], BF16)
        S = sb("S", [P, G * D])
        L = sb("L", [P, 2, G * D])
        LT = sb("LT", [P, 2, G * KD * P])
        attm = sb("attm", [P, KD, H])
        p_hot = pb("p_hot", [P, G, P], BF16)
        p_row = pb("p_row", [P, 2, G * D])
        p_T = pb("p_T", [P, G * KD * P])
        p_a = pb("p_a", [P, G, H])
        with nc.Block() as block:
            @block.gpsimd
            def _(pool):
                nc.gpsimd.memset(attm[:, :, :], 0.0).then_inc(att_set, 1)

                def gather(g):
                    r = g.slot(RING)
                    wait(pool, gathered[r], g.turn(RING) * (16 * G))
                    nc.gpsimd.tensor_copy(idx[:, r, :], s["srcs"][:, bass.ds(g.n * G, G)]).then_inc(listed, 1)
                    goals = ((listed, g.n + 1),
                             (spilled[r], g.turn(RING) * 16),
                             (summed, g.n - (RING - 1)))
                    goals = [(m, v if isinstance(v, int) else pool.to_reg(v)) for m, v in goals]
                    pool.wait_ge(att_set, 1)
                    for m, v in goals:
                        wait(pool, m, v)
                    for n in range(G):
                        nc.gpsimd.indirect_dma_start(
                            out=rows[:, r, n, :], out_offset=None, in_=d["left"][:, :],
                            in_offset=bass.IndirectOffsetOnAxis(ap=idx[:, r, n:n + 1], axis=0),
                        ).then_inc(gathered[r], 16)

                pipeline(pool, GROUPS, [(0, gather)])

            @block.sync
            def _(sp):
                sp.wait_ge(att_set, 1)
                for h in range(H):
                    at = h * C
                    sp.dma_start(attm[at % P:at % P + C, at // P, h:h + 1],
                                 att[h:h + 1, :].rearrange("a c -> c a"),
                                 allow_slow_non_contiguous=True).then_inc(att_in, 16)

                def spill(g):
                    r = g.slot(RING)
                    wait(sp, gathered[r], (g.turn(RING) + 1) * (16 * G))
                    sp.dma_start(d["rows"][bass.ds(g.n, 1), :, :].rearrange("a p f -> (a p) f"),
                                 rows[:, r, :, :].rearrange("p g f -> p (g f)")).then_inc(spilled[r], 16)

                pipeline(sp, GROUPS, [(0, spill)])
                for r in range(RING):
                    sp.wait_ge(spilled[r], 16 * (GROUPS // RING))

            @block.vector
            def _(v):
                def one_hot(g):
                    wait(v, hot_turned, g.n - 1)
                    nc.vector.tensor_tensor(
                        hots[:, g.slot(2), :, :],
                        s["iota"][:, :].unsqueeze(1).to_broadcast([P, G, P]),
                        s["dl"][:, bass.ds(g.n * G, G)].unsqueeze(2).to_broadcast([P, G, P]),
                        ALU.is_equal).then_inc(hot, 1)

                def add_and_leak(g):
                    r = g.slot(RING)
                    wait(v, spread, g.n + 1)
                    wait(v, gathered[r], (g.turn(RING) + 1) * (16 * G))
                    wait(v, leaked, g.n)
                    nc.vector.tensor_tensor(S[:, :], p_row[:, g.slot(2), :],
                                            rows[:, r, :, :].rearrange("p g f -> p (g f)"),
                                            ALU.add).then_inc(summed, 1)
                    wait(v, summed, g.n + 1)
                    wait(v, turned, g.n - 1)
                    nc.vector.scalar_tensor_tensor(L[:, g.slot(2), :], S[:, :], SLOPE, S[:, :],
                                                   ALU.mult, ALU.max).then_inc(leaked, 1)

                pipeline(v, GROUPS, [(3, one_hot), (1, add_and_leak)])

            @block.scalar
            def _(act):
                def copy_hot(g):
                    wait(act, hot_turned, g.n + 1)
                    wait(act, spread, g.n - 1)
                    nc.scalar.activation(hotT[:, g.slot(2), :, :], p_hot[:, :, :], ACT.Copy).then_inc(hot_copied, 1)

                def copy_turned(g):
                    wait(act, turned, g.n + 1)
                    wait(act, scored, g.n - 1)
                    nc.scalar.activation(LT[:, g.slot(2), :], p_T[:, :], ACT.Copy).then_inc(turned_copied, 1)

                def keep_scores(g):
                    wait(act, scored, g.n + 1)
                    nc.scalar.activation(s["alpha"][:, bass.ds(g.n * G, G), :], p_a[:, :, :], ACT.Copy).then_inc(kept, 1)

                pipeline(act, GROUPS, [(2, copy_hot), (0, copy_turned), (-1, keep_scores)])

            @block.tensor
            def _(pe):
                pe.wait_ge(att_in, 16 * H)

                def turn_hot(g):
                    wait(pe, hot, g.n + 1)
                    wait(pe, hot_copied, g.n)
                    for n in range(G):
                        last = nc.tensor.transpose(p_hot[:, n, :], hots[:, g.slot(2), n, :], s["identb"][:, :])
                    last.then_inc(hot_turned, 1)

                regs = [nc.tensor.alloc_register(f"right_tile{n}") for n in range(G)]

                def spread_rows(g):
                    tiles = node_tiles(nc.tensor, regs, s, g)
                    wait(pe, hot_copied, g.n + 1)
                    wait(pe, summed, g.n - 1)
                    for n in range(G):
                        j = tiles[n]
                        for c in range(3):
                            last = nc.tensor.matmul(p_row[:, g.slot(2), n * D:(n + 1) * D], hotT[:, g.slot(2), n, :],
                                                    s["right"][:, bass.ds(j, 1), c, :].rearrange("p a f -> p (a f)"),
                                                    start=(c == 0), stop=(c == 2))
                    last.then_inc(spread, 1)

                def turn_leaked(g):
                    wait(pe, leaked, g.n + 1)
                    wait(pe, turned_copied, g.n)
                    for n in range(G * KD):
                        last = nc.tensor.transpose(p_T[:, n * P:(n + 1) * P], L[:, g.slot(2), n * P:(n + 1) * P],
                                                   s["ident"][:, :])
                    last.then_inc(turned, 1)

                def score(g):
                    wait(pe, turned_copied, g.n + 1)
                    wait(pe, kept, g.n)
                    for n in range(G):
                        for h in range(KD):
                            at = (n * KD + h) * P
                            last = nc.tensor.matmul(p_a[:, n, :], LT[:, g.slot(2), at:at + P], attm[:, h, :],
                                                    start=(h == 0), stop=(h == KD - 1))
                    last.then_inc(scored, 1)

                pipeline(pe, GROUPS, [(2, turn_hot), (1, spread_rows), (0, turn_leaked), (-1, score)])


def segment_softmax(nc, d, s):
    sem = nc.alloc_semaphore
    keys_in, weights_in, logged, floored = sem("m_keys_in"), sem("m_weights_in"), sem("m_logged"), sem("m_floored")
    turned, turned_copied, dve = sem("m_turned"), sem("m_turned_copied"), sem("dve_softmax")
    to_row, row, to_col, col = sem("m_to_row"), sem("m_row"), sem("m_to_col"), sem("m_col")
    shifted, expd, flattened = sem("m_shifted"), sem("m_expd"), sem("m_flattened")
    back, back_copied = sem("m_back"), sem("m_back_copied")
    with ExitStack() as scope:
        def sb(name, shape, dt=F32):
            return scope.enter_context(nc.sbuf_tensor(name, shape, dt))

        A = sb("m_A", [P, SCAN])
        K = sb("m_K", [P, SCAN + 2])
        R = sb("m_R", [P, SCAN + 1])
        M = sb("m_M", [P, SCAN])
        ends = sb("m_ends", [P, 4])
        rows = sb("m_rows", [1, 8, P])
        carry = sb("m_carry", [P, 2])
        flat = sb("m_flat", [P, 2, P])
        pt = scope.enter_context(nc.psum_tensor("m_pt", [P, 2, 512], F32))
        pr = scope.enter_context(nc.psum_tensor("m_pr", [P, 512], F32))
        with nc.Block() as block:
            @block.sync
            def _(sp):
                for h in range(H):
                    sp.dma_start(M[h * BLOCKS:(h + 1) * BLOCKS, :],
                                 d["item_weight"][0:ITEMS, :].rearrange("(b u) e -> b (u e)", b=BLOCKS)).then_inc(weights_in, 16)
                for h in range(H):
                    to = K[h * BLOCKS:(h + 1) * BLOCKS, :]
                    for at, n, c in ((1, SCAN, 1), (0, 1, 0), (SCAN + 1, 1, SCAN + 1)):
                        sp.dma_start(to[:, c:c + n],
                                     d["key"][at:at + BLOCKS * SCAN, :].rearrange("(b e) o -> b (e o)", b=BLOCKS)[:, 0:n]
                                     if at <= 1 else
                                     d["key"][1 + SCAN:1 + SCAN + (BLOCKS - 1) * SCAN + 1, :]
                                     .rearrange("e o -> (e o)")[::SCAN].unsqueeze(1),
                                     allow_slow_non_contiguous=True).then_inc(keys_in, 16)

            @block.vector
            def _(v):
                by_block = s["alpha"][:, :, :].rearrange("p (b u) h -> p u h b", b=BLOCKS)
                with v.Fori(0, U // 2) as i:
                    for k in range(2):
                        v.wait_ge(turned, 2 * i)
                        nc.vector.tensor_copy(flat[:, k, :].rearrange("p (h b) -> p h b", h=H),
                                              by_block[:, bass.ds(2 * i + k, 1), :, :].rearrange("p a h b -> p (a h) b")
                                              ).then_inc(flattened, 1)
                step = Chain(v, dve)
                v.wait_ge(weights_in, 16 * H)
                step(nc.vector.tensor_scalar(R[:, 0:SCAN], M[:, :], TINY_WEIGHT, -BIG, ALU.is_lt, ALU.mult))
                nc.vector.tensor_scalar(M[:, :], M[:, :], TINY_WEIGHT, None, ALU.max).then_inc(floored, 1)
                v.wait_ge(logged, 1)
                v.wait_ge(turned_copied, U)
                step(nc.vector.tensor_tensor(A[:, :], A[:, :], M[:, :], ALU.add))
                step(nc.vector.tensor_tensor(A[:, :], A[:, :], R[:, 0:SCAN], ALU.add))
                v.wait_ge(keys_in, 16 * 3 * H)
                step(nc.vector.tensor_scalar(M[:, :], K[:, 1:SCAN + 1], 0.0, -BIG, ALU.is_lt, ALU.mult))
                step(nc.vector.tensor_tensor(A[:, :], A[:, :], M[:, :], ALU.add))
                step(nc.vector.tensor_tensor(R[:, :], K[:, 0:SCAN + 1], K[:, 1:SCAN + 2], ALU.not_equal))
                step(nc.vector.tensor_scalar(R[:, :], R[:, :], -BIG, None, ALU.mult))
                step(nc.vector.tensor_tensor(ends[:, 3:4], K[:, 1:2], K[:, SCAN:SCAN + 1], ALU.not_equal))
                step(nc.vector.tensor_tensor_scan(M[:, :], R[:, 0:SCAN], A[:, :], -BIG, ALU.add, ALU.max))
                step(nc.vector.tensor_copy(ends[:, 0:1], M[:, SCAN - 1:SCAN]))
                step(nc.vector.tensor_copy(ends[:, 1:2], R[:, 0:1]))
                step(nc.vector.tensor_scalar(ends[:, 2:3], ends[:, 3:4], -BIG, None, ALU.mult))
                nc.vector.engine_nop().then_inc(to_row, 1)
                v.wait_ge(row, 1)
                step(nc.vector.tensor_copy(rows[:, 0:3, :], pr[0:1, 0:3 * P].rearrange("o (c b) -> o c b", c=3)))
                step(nc.vector.memset(rows[:, 3:8, :], -BIG))
                heads = lambda a: rows[:, a, :].rearrange("o (h b) -> o h b", h=H)
                for b in range(1, BLOCKS):
                    step(nc.vector.tensor_tensor(heads(4)[:, :, b:b + 1], heads(3)[:, :, b - 1:b],
                                                 heads(2)[:, :, b - 1:b], ALU.add))
                    step(nc.vector.tensor_tensor(heads(4)[:, :, b:b + 1], heads(4)[:, :, b:b + 1],
                                                 heads(0)[:, :, b - 1:b], ALU.max))
                    step(nc.vector.tensor_tensor(heads(3)[:, :, b:b + 1], heads(4)[:, :, b:b + 1],
                                                 heads(1)[:, :, b:b + 1], ALU.add))
                step(nc.vector.tensor_scalar(rows[:, 3, :], rows[:, 3, :], -BIG, None, ALU.max))
                nc.vector.engine_nop().then_inc(to_col, 1)
                v.wait_ge(col, 1)
                step(nc.vector.tensor_copy(carry[:, 0:1], pr[:, 0:1]))
                step(nc.vector.tensor_tensor_scan(M[:, :], R[:, 0:SCAN], A[:, :], carry[:, 0:1], ALU.add, ALU.max))
                step(nc.vector.tensor_tensor_scan(K[:, SCAN - 1::-1], R[:, SCAN:0:-1], M[:, ::-1], -BIG,
                                                  ALU.add, ALU.max))
                step(nc.vector.tensor_copy(ends[:, 0:1], K[:, 0:1]))
                step(nc.vector.tensor_copy(ends[:, 1:2], R[:, SCAN:SCAN + 1]))
                nc.vector.engine_nop().then_inc(to_row, 1)
                v.wait_ge(row, 2)
                step(nc.vector.tensor_copy(rows[:, 0:3, :], pr[0:1, 0:3 * P].rearrange("o (c b) -> o c b", c=3)))
                step(nc.vector.memset(rows[:, 3:8, :], -BIG))
                for b in range(BLOCKS - 2, -1, -1):
                    step(nc.vector.tensor_tensor(heads(4)[:, :, b:b + 1], heads(3)[:, :, b + 1:b + 2],
                                                 heads(2)[:, :, b + 1:b + 2], ALU.add))
                    step(nc.vector.tensor_tensor(heads(4)[:, :, b:b + 1], heads(4)[:, :, b:b + 1],
                                                 heads(0)[:, :, b + 1:b + 2], ALU.max))
                    step(nc.vector.tensor_tensor(heads(3)[:, :, b:b + 1], heads(4)[:, :, b:b + 1],
                                                 heads(1)[:, :, b:b + 1], ALU.add))
                step(nc.vector.tensor_scalar(rows[:, 3, :], rows[:, 3, :], -BIG, None, ALU.max))
                nc.vector.engine_nop().then_inc(to_col, 1)
                v.wait_ge(col, 2)
                step(nc.vector.tensor_copy(carry[:, 1:2], pr[:, 0:1]))
                step(nc.vector.tensor_tensor_scan(K[:, SCAN - 1::-1], R[:, SCAN:0:-1], M[:, ::-1], carry[:, 1:2],
                                                  ALU.add, ALU.max))
                nc.vector.tensor_tensor(A[:, :], A[:, :], K[:, 0:SCAN], ALU.subtract).then_inc(shifted, 1)
                with v.Fori(0, U // 2) as i:
                    for k in range(2):
                        v.wait_ge(back, 2 * i + k + 1)
                        nc.vector.tensor_copy(by_block[:, bass.ds(2 * i + k, 1), :, :].rearrange("p a h b -> p (a h) b"),
                                              pt[:, k, 0:P].rearrange("p (h b) -> p h b", h=H)).then_inc(back_copied, 1)

            @block.scalar
            def _(act):
                with act.Fori(0, U // 2) as i:
                    for k in range(2):
                        act.wait_ge(turned, 2 * i + k + 1)
                        nc.scalar.activation(A[:, bass.ds((2 * i + k) * P, P)], pt[:, k, 0:P], ACT.Copy).then_inc(turned_copied, 1)
                act.wait_ge(floored, 1)
                nc.scalar.activation(M[:, :], M[:, :], ACT.Ln).then_inc(logged, 1)
                act.wait_ge(shifted, 1)
                with act.Fori(0, U // 2) as i:
                    for k in range(2):
                        act.wait_ge(back, 2 * i)
                        nc.scalar.activation(flat[:, k, :], A[:, bass.ds((2 * i + k) * P, P)], ACT.Exp).then_inc(expd, 1)

            @block.tensor
            def _(pe):
                with pe.Fori(0, U // 2) as i:
                    for k in range(2):
                        pe.wait_ge(turned_copied, 2 * i)
                        pe.wait_ge(flattened, 2 * i + k + 1)
                        nc.tensor.transpose(pt[:, k, 0:P], flat[:, k, :], s["ident"][:, :]).then_inc(turned, 1)
                for r in range(2):
                    pe.wait_ge(to_row, r + 1)
                    if r:
                        pe.wait_ge(dve, 1)
                    for c in range(3):
                        last = nc.tensor.matmul(pr[0:1, c * P:(c + 1) * P], ends[:, c:c + 1], s["ident"][:, :],
                                                start=True, stop=True)
                    last.then_inc(row, 1)
                    pe.wait_ge(to_col, r + 1)
                    nc.tensor.matmul(pr[:, 0:1], rows[0:1, 3, :], s["ones"][0:1, 0:1], start=True, stop=True).then_inc(col, 1)
                with pe.Fori(0, U // 2) as i:
                    for k in range(2):
                        pe.wait_ge(back_copied, 2 * i)
                        pe.wait_ge(expd, 2 * i + k + 1)
                        nc.tensor.transpose(pt[:, k, 0:P], flat[:, k, :], s["ident"][:, :]).then_inc(back, 1)


def aggregate(nc, d, s):
    sem = nc.alloc_semaphore
    loaded = [sem(f"a_loaded{i}") for i in range(RING)]
    cleared, hot, weighted, summed, added = sem("a_cleared"), sem("a_hot"), sem("a_weighted"), sem("a_summed"), sem("a_added")
    weights_put = sem("a_weights_put")
    with ExitStack() as scope:
        def sb(name, shape, dt=F32):
            return scope.enter_context(nc.sbuf_tensor(name, shape, dt))

        rows = sb("a_rows", [P, RING, G, D])
        hots = sb("a_hots", [P, 2, G, P])
        W = sb("a_W", [P, 2, G, D + H])
        acc = s["acc"]
        ps = scope.enter_context(nc.psum_tensor("a_ps", [P, 2, G, 512], F32))
        with nc.Block() as block:
            @block.gpsimd
            def _(pool):
                nc.gpsimd.memset(acc[:, :, :], 0.0).then_inc(cleared, 1)

                def weigh(g):
                    r = g.slot(RING)
                    wait(pool, summed, g.n - 1)
                    wait(pool, loaded[r], (g.turn(RING) + 1) * 16)
                    for n in range(G):
                        last = nc.gpsimd.tensor_tensor(
                            W[:, g.slot(2), n, 0:D].rearrange("p (h c) -> p h c", h=H),
                            rows[:, r, n, :].rearrange("p (h c) -> p h c", h=H),
                            s["alpha"][:, bass.ds(g.n * G + n, 1), :].rearrange("p a h -> p (a h)")
                            .unsqueeze(2).to_broadcast([P, H, C]), ALU.mult)
                    last.then_inc(weighted, 1)

                pipeline(pool, GROUPS, [(0, weigh)])

            @block.sync
            def _(sp):
                def load(g):
                    r = g.slot(RING)
                    wait(sp, weighted, g.n - (RING - 1))
                    sp.dma_start(rows[:, r, :, :].rearrange("p g f -> p (g f)"),
                                 d["rows"][bass.ds(g.n, 1), :, :].rearrange("a p f -> (a p) f")).then_inc(loaded[r], 16)

                pipeline(sp, GROUPS, [(0, load)])

            @block.scalar
            def _(act):
                def put_weights(g):
                    wait(act, summed, g.n - 1)
                    nc.scalar.activation(W[:, g.slot(2), :, D:D + H], s["alpha"][:, bass.ds(g.n * G, G), :],
                                         ACT.Copy).then_inc(weights_put, 1)

                pipeline(act, GROUPS, [(0, put_weights)])

            @block.vector
            def _(v):
                v.wait_ge(cleared, 1)

                def one_hot(g):
                    wait(v, summed, g.n - 1)
                    nc.vector.tensor_tensor(
                        hots[:, g.slot(2), :, :], s["iota"][:, :].unsqueeze(1).to_broadcast([P, G, P]),
                        s["dl"][:, bass.ds(g.n * G, G)].unsqueeze(2).to_broadcast([P, G, P]),
                        ALU.is_equal).then_inc(hot, 1)

                regs = [nc.vector.alloc_register(f"acc_tile{n}") for n in range(G)]

                def add(g):
                    tiles = node_tiles(nc.vector, regs, s, g)
                    wait(v, summed, g.n + 1)
                    for n in range(G):
                        j = tiles[n]
                        to = acc[:, bass.ds(j, 1), :].rearrange("p a f -> p (a f)")
                        wait(v, added, g.n * G + n)
                        nc.vector.tensor_tensor(to, to, ps[:, g.slot(2), n, 0:D + H], ALU.add).then_inc(added, 1)

                pipeline(v, GROUPS, [(1, one_hot), (-1, add)])

            @block.tensor
            def _(pe):
                def sum_(g):
                    wait(pe, weighted, g.n + 1)
                    wait(pe, weights_put, g.n + 1)
                    wait(pe, hot, g.n + 1)
                    wait(pe, added, (g.n - 1) * G)
                    for n in range(G):
                        last = nc.tensor.matmul(ps[:, g.slot(2), n, 0:D + H], hots[:, g.slot(2), n, :],
                                                W[:, g.slot(2), n, :], start=True, stop=True)
                    last.then_inc(summed, 1)

                pipeline(pe, GROUPS, [(0, sum_)])


def route(nc, s, Wg, bg):
    sem = nc.alloc_semaphore
    gate_in, dve, inverted, divided, added = sem("r_gate_in"), sem("dve_route"), sem("r_inverted"), sem("r_divided"), sem("r_added")
    sqrt_ready, sqrt_done, listed = sem("r_sqrt_ready"), sem("r_sqrt_done"), sem("r_listed")
    normed, turned, turned_copied, gated = sem("r_normed"), sem("r_turned"), sem("r_turned_copied"), sem("r_gated")
    consts, masked, counted = sem("r_consts"), sem("r_masked"), sem("r_counted")
    with ExitStack() as scope:
        def sb(name, shape, dt=F32):
            return scope.enter_context(nc.sbuf_tensor(name, shape, dt))

        X, acc = s["X"], s["acc"]
        TE = NT * EXPERTS
        wg, bgb = sb("r_wg", [P, KD, EXPERTS]), sb("r_bg", [P, EXPERTS])
        inv = sb("r_inv", [P, NT, H])
        stats, mv, std = sb("r_stats", [P, NT, 6]), sb("r_mv", [P, NT, 2]), sb("r_std", [P, 3, NT])
        xT = sb("r_xT", [P, 2, KD * P])
        staged = sb("r_staged", [P, 2, D])
        before, every = sb("r_before", [P, P]), sb("r_every", [P, P])
        lane = sb("r_lane", [P, NT, EXPERTS])
        token = sb("r_token", [P, NT])
        real = sb("r_real", [P, NT])
        g1, g2 = sb("r_g1", [P, NT, EXPERTS]), sb("r_g2", [P, NT, EXPERTS])
        best, which = sb("r_best", [P, NT]), sb("r_which", [P, NT])
        work = sb("r_work", [P, NT, EXPERTS])
        pick = [sb(f"r_pick{k}", [P, NT, EXPERTS]) for k in range(2)]
        both = sb("r_both", [P, NT, EXPERTS])
        total, cum, one = sb("r_total", [P, EXPERTS, NT]), sb("r_cum", [P, EXPERTS, NT]), sb("r_one", [P, NT])
        count_i = sb("r_count_i", [P, EXPERTS], I32)
        tiles, tiles_cum, start = sb("r_tiles", [P, EXPERTS]), sb("r_tiles_cum", [P, EXPERTS]), sb("r_start", [P, EXPERTS])
        slot = sb("r_slot", [P, NT, EXPERTS])
        slot_f = sb("r_slot_f", [P, NT, 2])
        expert_f = sb("r_expert_f", [1, P])
        pt = scope.enter_context(nc.psum_tensor("r_pt", [P, 2, 512], F32))
        pg = scope.enter_context(nc.psum_tensor("r_pg", [P, NT, EXPERTS], F32))
        pc = scope.enter_context(nc.psum_tensor("r_pc", [P, 2, 512], F32))

        def wide(a):
            return a.unsqueeze(2).to_broadcast([P, NT, EXPERTS])

        with nc.Block() as block:
            @block.gpsimd
            def _(pool):
                nc.gpsimd.memset(before[:, :], 1.0).then_inc(consts, 1)
                nc.gpsimd.memset(every[:, :], 1.0).then_inc(consts, 1)
                nc.gpsimd.memset(one[:, :], 1.0).then_inc(consts, 1)
                nc.gpsimd.iota(lane[:, :, :], [[0, NT], [1, EXPERTS]], base=0, channel_multiplier=0,
                               allow_small_or_imprecise_dtypes=True).then_inc(consts, 1)
                nc.gpsimd.iota(token[:, :], [[P, NT]], base=0, channel_multiplier=1,
                               allow_small_or_imprecise_dtypes=True).then_inc(consts, 1)
                pool.wait_ge(consts, 5)
                nc.gpsimd.affine_select(out=before[:, :], in_=before[:, :], compare_op=ALU.is_gt, fill=0.0,
                                        base=0, pattern=[[1, P]], channel_multiplier=-1).then_inc(consts, 1)
                pool.wait_ge(inverted, 1)

                def divide(g):
                    a = acc[:, bass.ds(g.n, 1), 0:D].rearrange("p a (h c) -> p (a h) c", h=H)
                    nc.gpsimd.tensor_tensor(a, a, inv[:, bass.ds(g.n, 1), :].rearrange("p a h -> p (a h)")
                                            .unsqueeze(2).to_broadcast([P, H, C]), ALU.mult).then_inc(divided, 1)

                pipeline(pool, NT, [(0, divide)])

            @block.sync
            def _(sp):
                sp.dma_start(wg[:, :, :], Wg.rearrange("(k p) e -> p k e", p=P)).then_inc(gate_in, 16)
                sp.dma_start(bgb[:, :], bg.partition_broadcast(P)).then_inc(gate_in, 16)

            @block.vector
            def _(v):
                step = Chain(v, dve)

                def row(g):
                    return X[:, bass.ds(g.n, 1), :].rearrange("p a f -> p (a f)")

                def sums(g):
                    return acc[:, bass.ds(g.n, 1), 0:D].rearrange("p a f -> p (a f)")

                step(nc.vector.tensor_scalar(inv[:, :, :], acc[:, :, D:D + H], 1e-16, None, ALU.add))
                nc.vector.reciprocal(inv[:, :, :], inv[:, :, :]).then_inc(inverted, 1)

                def add(g):
                    wait(v, divided, g.n + 1)
                    nc.vector.tensor_tensor(row(g), row(g), sums(g), ALU.add).then_inc(added, 1)

                pipeline(v, NT, [(0, add)])
                v.wait_ge(added, NT)
                moments(nc, v, step, stats, mv, std, X, sqrt_ready, sqrt_done)

                def norm(g):
                    nc.vector.tensor_scalar(sums(g), row(g), mv[:, bass.ds(g.n, 1), 0], std[:, 2, bass.ds(g.n, 1)],
                                            ALU.subtract, ALU.mult).then_inc(normed, 1)

                pipeline(v, NT, [(0, norm)])
                v.wait_ge(gate_in, 32)
                v.wait_ge(consts, 6)
                step(nc.vector.tensor_scalar(real[:, :], token[:, :], float(N), None, ALU.is_lt))
                v.wait_ge(gated, NT)
                step(nc.vector.tensor_tensor(g1[:, :, :], pg[:, :, :], bgb[:, :].unsqueeze(1).to_broadcast([P, NT, EXPERTS]),
                                             ALU.add))
                for k, g in enumerate((g1, g2)):
                    step(nc.vector.tensor_reduce(best[:, :], g[:, :, :], AX.X, ALU.max))
                    step(nc.vector.tensor_tensor(work[:, :, :], g[:, :, :], wide(best[:, :]), ALU.is_lt))
                    step(nc.vector.scalar_tensor_tensor(work[:, :, :], work[:, :, :], float(EXPERTS), lane[:, :, :],
                                                        ALU.mult, ALU.add))
                    step(nc.vector.tensor_reduce(which[:, :], work[:, :, :], AX.X, ALU.min))
                    step(nc.vector.tensor_tensor(pick[k][:, :, :], lane[:, :, :], wide(which[:, :]), ALU.is_equal))
                    if k == 0:
                        step(nc.vector.scalar_tensor_tensor(g2[:, :, :], pick[0][:, :, :], -BIG, g1[:, :, :],
                                                            ALU.mult, ALU.add))
                    step(nc.vector.tensor_tensor(pick[k][:, :, :], pick[k][:, :, :], wide(real[:, :]), ALU.mult))
                nc.vector.tensor_tensor(both[:, :, :], pick[0][:, :, :], pick[1][:, :, :], ALU.add).then_inc(masked, 1)
                v.wait_ge(counted, 1)
                step(nc.vector.tensor_copy(total[:, :, :], pc[:, 1, 0:TE].rearrange("p (t e) -> p e t", e=EXPERTS)))
                for e in range(EXPERTS):
                    last = nc.vector.tensor_tensor_scan(cum[:, e, :], one[:, :], total[:, e, :], 0.0, ALU.mult, ALU.add)
                step(last)
                step(nc.vector.tensor_scalar(tiles[:, :], cum[:, :, NT - 1], float(P - 1), None, ALU.add))
                step(nc.vector.tensor_copy(count_i[:, :], tiles[:, :]))
                step(nc.vector.tensor_scalar(count_i[:, :], count_i[:, :], 7, None, ALU.logical_shift_right))
                step(nc.vector.tensor_copy(tiles[:, :], count_i[:, :]))
                step(nc.vector.tensor_tensor_scan(tiles_cum[:, :], one[:, 0:EXPERTS], tiles[:, :], 0.0, ALU.mult, ALU.add))
                step(nc.vector.tensor_tensor(start[:, :], tiles_cum[:, :], tiles[:, :], ALU.subtract))
                step(nc.vector.tensor_scalar(start[:, :], start[:, :], float(P), None, ALU.mult))
                step(nc.vector.tensor_tensor(cum[:, :, :], cum[:, :, :], total[:, :, :], ALU.subtract))
                step(nc.vector.tensor_tensor(cum[:, :, :], cum[:, :, :], start[:, :].unsqueeze(2).to_broadcast([P, EXPERTS, NT]),
                                             ALU.add))
                step(nc.vector.tensor_tensor(slot[:, :, :], cum[:, :, :].rearrange("p e t -> p t e"),
                                             pc[:, 0, 0:TE].rearrange("p (t e) -> p t e", e=EXPERTS), ALU.add))
                for k in range(2):
                    step(nc.vector.tensor_tensor(work[:, :, :], slot[:, :, :], pick[k][:, :, :], ALU.mult))
                    step(nc.vector.tensor_reduce(slot_f[:, :, k], work[:, :, :], AX.X, ALU.add))
                step(nc.vector.tensor_copy(s["slot_of"][:, :, :], slot_f[:, :, :]))
                step(nc.vector.tensor_scalar(expert_f[:, :], s["iota"][0:1, :], tiles_cum[0:1, 0:1], None, ALU.is_ge))
                for e in range(1, EXPERTS - 1):
                    step(nc.vector.scalar_tensor_tensor(expert_f[:, :], s["iota"][0:1, :], tiles_cum[0:1, e:e + 1],
                                                        expert_f[:, :], ALU.is_ge, ALU.add))
                step(nc.vector.tensor_copy(s["tile_expert"][:, :], expert_f[:, :]))

            @block.scalar
            def _(act):
                act.wait_ge(sqrt_ready, 1)
                nc.scalar.activation(std[:, 1, :], std[:, 0, :], ACT.Sqrt).then_inc(sqrt_done, 1)

                def copy_turned(g):
                    wait(act, turned, g.n + 1)
                    wait(act, gated, g.n - 1)
                    nc.scalar.activation(xT[:, g.slot(2), :], pt[:, g.slot(2), 0:KD * P], ACT.Copy).then_inc(turned_copied, 1)

                def stage(g):
                    wait(act, normed, g.n + 1)
                    wait(act, turned, g.n - 1)
                    nc.scalar.activation(staged[:, g.slot(2), :], acc[:, bass.ds(g.n, 1), 0:D]
                                         .rearrange("p a f -> p (a f)"), ACT.Copy).then_inc(listed, 1)

                pipeline(act, NT, [(1, stage), (0, copy_turned)])

            @block.tensor
            def _(pe):
                pe.wait_ge(gate_in, 32)

                def turn(g):
                    wait(pe, listed, g.n + 1)
                    wait(pe, turned_copied, g.n - 1)
                    for h in range(KD):
                        last = nc.tensor.transpose(pt[:, g.slot(2), h * P:(h + 1) * P],
                                                   staged[:, g.slot(2), h * P:(h + 1) * P], s["ident"][:, :])
                    last.then_inc(turned, 1)

                def gate(g):
                    wait(pe, turned_copied, g.n + 1)
                    for h in range(KD):
                        last = nc.tensor.matmul(pg[:, bass.ds(g.n, 1), :].rearrange("p a e -> p (a e)"),
                                                xT[:, g.slot(2), h * P:(h + 1) * P], wg[:, h, :],
                                                start=(h == 0), stop=(h == KD - 1))
                    last.then_inc(gated, 1)

                pipeline(pe, NT, [(1, turn), (0, gate)])
                pe.wait_ge(consts, 6)
                pe.wait_ge(masked, 1)
                for a, m in enumerate((before, every)):
                    last = nc.tensor.matmul(pc[:, a, 0:TE], m[:, :], both[:, :, :].rearrange("p t e -> p (t e)"),
                                            start=True, stop=True)
                last.then_inc(counted, 1)


def spread_tokens(nc, d, s):
    sem = nc.alloc_semaphore
    copied, indexed, first = sem("s_copied"), sem("s_indexed"), sem("s_first")
    sent = [sem(f"s_sent{i}") for i in range(4)]
    last_tile = NODE_TILES - 1
    rest = N - last_tile * P
    with nc.sbuf_tensor("s_word", [P, 1], F32) as word, nc.sbuf_tensor("s_rows", [P, 4, D], F32) as rows, nc.sbuf_tensor("s_idx", [P, 4, 2], I32) as idx, \
            nc.Block() as block:
        @block.gpsimd
        def _(pool):
            nc.gpsimd.memset(word[:, :], 0.0).then_inc(first, 1)

            def send(g, parts=P):
                r = g.slot(4)
                goals = [(m, v if isinstance(v, int) else pool.to_reg(v)) for m, v in ((copied, 2 * g.n + 2),)]
                pool.wait_ge(first, 1)
                for m, v in goals:
                    wait(pool, m, v)
                for k in range(2):
                    nc.gpsimd.indirect_dma_start(
                        out=d["slots_in"][:, :], out_offset=bass.IndirectOffsetOnAxis(ap=idx[0:parts, r, k:k + 1], axis=0),
                        in_=rows[0:parts, r, :], in_offset=None).then_inc(sent[r], 16)

            pipeline(pool, last_tile, [(0, send)])
            send(Step(0, last_tile), rest)
            for r in range(4):
                pool.wait_ge(sent[r], 32 * len(range(r, NODE_TILES, 4)))

        @block.vector
        def _(v):
            def copy(g):
                r = g.slot(4)
                wait(v, sent[r], g.turn(4) * 32)
                nc.vector.tensor_copy(rows[:, r, :], s["acc"][:, bass.ds(g.n, 1), 0:D]
                                      .rearrange("p a f -> p (a f)")).then_inc(copied, 1)
                nc.vector.tensor_copy(idx[:, r, :], s["slot_of"][:, bass.ds(g.n, 1), :]
                                      .rearrange("p a k -> p (a k)")).then_inc(copied, 1)

            pipeline(v, NODE_TILES, [(0, copy)])


def experts(nc, d, s, W1, b1, W2, b2):
    sem = nc.alloc_semaphore
    w_in = sem("e_w_in")
    loaded = [sem(f"e_loaded{i}") for i in range(4)]
    stored = [sem(f"e_stored{i}") for i in range(4)]
    turned, turned_copied, up, biased = sem("e_turned"), sem("e_turned_copied"), sem("e_up"), sem("e_biased")
    gelued, back, back_copied, down, done = sem("e_gelued"), sem("e_back"), sem("e_back_copied"), sem("e_down"), sem("e_done")
    with ExitStack() as scope:
        def sb(name, shape, dt=F32):
            return scope.enter_context(nc.sbuf_tensor(name, shape, dt))

        w1, w2 = sb("e_w1", [P, EXPERTS, KD, HID]), sb("e_w2", [P, EXPERTS, KH, D])
        b1b, b2b = sb("e_b1", [P, EXPERTS, HID]), sb("e_b2", [P, EXPERTS, D])
        x = sb("e_x", [P, 4, D])
        xT = sb("e_xT", [P, 2, D])
        h = sb("e_h", [P, 2, HID])
        hg = sb("e_hg", [P, 2, HID])
        hT = sb("e_hT", [P, 2, HID])
        y = sb("e_y", [P, 4, D])
        pt = scope.enter_context(nc.psum_tensor("e_pt", [P, 2, 512], F32))
        ph = scope.enter_context(nc.psum_tensor("e_ph", [P, 2, 512], F32))
        pT = scope.enter_context(nc.psum_tensor("e_pT", [P, 2, 512], F32))
        py = scope.enter_context(nc.psum_tensor("e_py", [P, 2, 512], F32))

        def expert(eng, reg, g):
            eng.load(reg, s["tile_expert"][0:1, bass.ds(g.n, 1)])
            return eng.snap(reg, min_val=0, max_val=EXPERTS - 1)

        with nc.Block() as block:
            @block.sync
            def _(sp):
                for e in range(EXPERTS):
                    sp.dma_start(w1[:, e, :, :], W1[e, :, :].rearrange("(k p) f -> p k f", p=P)).then_inc(w_in, 16)
                    sp.dma_start(w2[:, e, :, :], W2[e, :, :].rearrange("(k p) f -> p k f", p=P)).then_inc(w_in, 16)
                sp.dma_start(b1b[:, :, :], b1.rearrange("e f -> (e f)").partition_broadcast(P)
                             .rearrange("p (e f) -> p e f", e=EXPERTS)).then_inc(w_in, 16)
                sp.dma_start(b2b[:, :, :], b2.rearrange("e f -> (e f)").partition_broadcast(P)
                             .rearrange("p (e f) -> p e f", e=EXPERTS)).then_inc(w_in, 16)

                def load(g):
                    r = g.slot(4)
                    wait(sp, turned, g.n - 3)
                    sp.dma_start(x[:, r, :], d["slots_in"][bass.ds(g.n * P, P), :]).then_inc(loaded[r], 16)

                def store(g):
                    r = g.slot(4)
                    wait(sp, done, g.n + 1)
                    sp.dma_start(d["slots_out"][bass.ds(g.n * P, P), :], y[:, r, :]).then_inc(stored[r], 16)

                pipeline(sp, SLOT_TILES, [(4, load), (-1, store)])
                for r in range(4):
                    sp.wait_ge(stored[r], 16 * (SLOT_TILES // 4))

            @block.vector
            def _(v):
                v.wait_ge(w_in, 16 * (2 * EXPERTS + 2))
                reg1, reg2 = nc.vector.alloc_register("b1_expert"), nc.vector.alloc_register("b2_expert")

                def copy_turned(g):
                    wait(v, turned, g.n + 1)
                    wait(v, up, g.n - 1)
                    nc.vector.tensor_copy(xT[:, g.slot(2), :], pt[:, g.slot(2), 0:D]).then_inc(turned_copied, 1)

                def add_b1(g):
                    e = expert(nc.vector, reg1, g)
                    wait(v, up, g.n + 1)
                    wait(v, gelued, g.n - 1)
                    nc.vector.tensor_tensor(h[:, g.slot(2), :], ph[:, g.slot(2), :],
                                            b1b[:, bass.ds(e, 1), :].rearrange("p a f -> p (a f)"),
                                            ALU.add).then_inc(biased, 1)

                def copy_back(g):
                    wait(v, back, g.n + 1)
                    wait(v, down, g.n - 1)
                    nc.vector.tensor_copy(hT[:, g.slot(2), :], pT[:, g.slot(2), :]).then_inc(back_copied, 1)

                def add_b2(g):
                    r = g.slot(4)
                    e = expert(nc.vector, reg2, g)
                    wait(v, down, g.n + 1)
                    wait(v, stored[r], g.turn(4) * 16)
                    nc.vector.tensor_tensor(y[:, r, :], py[:, g.slot(2), 0:D],
                                            b2b[:, bass.ds(e, 1), :].rearrange("p a f -> p (a f)"),
                                            ALU.add).then_inc(done, 1)

                pipeline(v, SLOT_TILES, [(2, copy_turned), (1, add_b1), (0, copy_back), (-1, add_b2)])

            @block.scalar
            def _(act):
                def gelu(g):
                    wait(act, biased, g.n + 1)
                    wait(act, back, g.n - 1)
                    nc.scalar.activation(hg[:, g.slot(2), :], h[:, g.slot(2), :], ACT.Gelu).then_inc(gelued, 1)

                pipeline(act, SLOT_TILES, [(0, gelu)])

            @block.tensor
            def _(pe):
                reg1, reg2 = nc.tensor.alloc_register("w1_expert"), nc.tensor.alloc_register("w2_expert")

                def turn(g):
                    wait(pe, loaded[g.slot(4)], (g.turn(4) + 1) * 16)
                    wait(pe, turned_copied, g.n - 1)
                    for k in range(KD):
                        last = nc.tensor.transpose(pt[:, g.slot(2), k * P:(k + 1) * P],
                                                   x[:, g.slot(4), k * P:(k + 1) * P], s["ident"][:, :])
                    last.then_inc(turned, 1)

                def layer1(g):
                    e = expert(nc.tensor, reg1, g)
                    wait(pe, turned_copied, g.n + 1)
                    wait(pe, biased, g.n - 1)
                    for k in range(KD):
                        last = nc.tensor.matmul(ph[:, g.slot(2), :], xT[:, g.slot(2), k * P:(k + 1) * P],
                                                w1[:, bass.ds(e, 1), k, :].rearrange("p a f -> p (a f)"),
                                                start=(k == 0), stop=(k == KD - 1))
                    last.then_inc(up, 1)

                def turn_back(g):
                    wait(pe, gelued, g.n + 1)
                    wait(pe, back_copied, g.n - 1)
                    for m in range(KH):
                        last = nc.tensor.transpose(pT[:, g.slot(2), m * P:(m + 1) * P],
                                                   hg[:, g.slot(2), m * P:(m + 1) * P], s["ident"][:, :])
                    last.then_inc(back, 1)

                def layer2(g):
                    e = expert(nc.tensor, reg2, g)
                    wait(pe, back_copied, g.n + 1)
                    wait(pe, done, g.n - 1)
                    for m in range(KH):
                        last = nc.tensor.matmul(py[:, g.slot(2), 0:D], hT[:, g.slot(2), m * P:(m + 1) * P],
                                                w2[:, bass.ds(e, 1), m, :].rearrange("p a f -> p (a f)"),
                                                start=(m == 0), stop=(m == KH - 1))
                    last.then_inc(down, 1)

                pe.wait_ge(w_in, 16 * (2 * EXPERTS + 2))
                pipeline(pe, SLOT_TILES, [(2, turn), (1, layer1), (0, turn_back), (-1, layer2)])


def combine(nc, d, s, out):
    sem = nc.alloc_semaphore
    listed, first, added = sem("c_listed"), sem("c_first"), sem("c_added")
    fetched = [sem(f"c_fetched{i}") for i in range(4)]
    stored = sem("c_stored")
    last_tile = NODE_TILES - 1
    rest = N - last_tile * P
    with nc.sbuf_tensor("c_rows", [P, 4, 2, D], F32) as rows, nc.sbuf_tensor("c_idx", [P, 4, 2], I32) as idx, \
            nc.sbuf_tensor("c_sum", [P, 2, D], F32) as both, nc.Block() as block:
        @block.gpsimd
        def _(pool):
            def fetch(g):
                r = g.slot(4)
                wait(pool, fetched[r], g.turn(4) * 32)
                nc.gpsimd.tensor_copy(idx[:, r, :], s["slot_of"][:, bass.ds(g.n, 1), :]
                                      .rearrange("p a k -> p (a k)")).then_inc(listed, 1)
                goals = [(m, v if isinstance(v, int) else pool.to_reg(v))
                         for m, v in ((listed, g.n + 1), (added, g.n - 3))]
                pool.wait_ge(listed, 1)
                for m, v in goals:
                    wait(pool, m, v)
                for k in range(2):
                    nc.gpsimd.indirect_dma_start(
                        out=rows[:, r, k, :], out_offset=None, in_=d["slots_out"][:, :],
                        in_offset=bass.IndirectOffsetOnAxis(ap=idx[:, r, k:k + 1], axis=0)).then_inc(fetched[r], 16)

            pipeline(pool, NODE_TILES, [(0, fetch)])

        @block.vector
        def _(v):
            def add(g):
                r = g.slot(4)
                xi = s["X"][:, bass.ds(g.n, 1), :].rearrange("p a f -> p (a f)")
                wait(v, fetched[r], (g.turn(4) + 1) * 32)
                wait(v, added, g.n - 1)
                nc.vector.tensor_tensor(both[:, g.slot(2), :], rows[:, r, 0, :], rows[:, r, 1, :], ALU.add).then_inc(first, 1)
                wait(v, first, g.n + 1)
                nc.vector.tensor_tensor(xi, xi, both[:, g.slot(2), :], ALU.add).then_inc(added, 1)

            pipeline(v, NODE_TILES, [(0, add)])

        @block.sync
        def _(sp):
            by = 8
            for t in range(0, last_tile, by):
                sp.wait_ge(added, t + by)
                sp.dma_start(out[t * P:(t + by) * P, :].rearrange("(t p) f -> p t f", p=P),
                             s["X"][:, t:t + by, :]).then_inc(stored, 16)
            sp.wait_ge(added, NODE_TILES)
            sp.dma_start(out[last_tile * P:N, :], s["X"][0:rest, last_tile, :]).then_inc(stored, 16)
            sp.wait_ge(stored, 16 * (last_tile // by + 1))


_INS = ["x", "src", "dst", "edge_weight", "L0_gnn_W_l", "L0_gnn_b_l", "L0_gnn_W_r", "L0_gnn_b_r", "L0_gnn_att",
        "L0_gnn_bias", "L0_ffn_Wg", "L0_ffn_bg", "L0_ffn_W1", "L0_ffn_b1", "L0_ffn_W2", "L0_ffn_b2"]


def kernel(**inputs):
    import numpy as np
    import concourse.bacc as bacc
    from concourse.bass_utils import run_bass_kernel_spmd

    nc = bacc.Bacc("TRN2", target_bir_lowering=False, num_devices=1)
    arrays, args = {}, []
    for name in _INS:
        a = np.ascontiguousarray(inputs[name])
        arrays[f"in_{name}"] = a
        args.append(nc.dram_tensor(f"in_{name}", a.shape, mybir.dt.from_np(a.dtype), kind="ExternalInput").ap())
    args.append(nc.dram_tensor("out", (N, D), F32, kind="ExternalOutput").ap())
    build(nc, *args)
    return run_bass_kernel_spmd(nc, [arrays], core_ids=[0]).results[0]["out"]
```

```python
from contextlib import ExitStack

import concourse.bass as bass
from concourse import mybir

F32 = mybir.dt.float32
BF16 = mybir.dt.bfloat16
I32 = mybir.dt.int32
U32 = mybir.dt.uint32
ALU = mybir.AluOpType
ACT = mybir.ActivationFunctionType
AX = mybir.AxisListType

P = 128
N, D = 6250, 256
E = 100000
H, C = 8, 32
EXPERTS, HID = 8, 512
KD = D // P
KH = HID // P
SLOPE = 0.2
EPS = 1e-5

NT = 50
NODE_TILES = -(-N // P)
ET = -(-E // P)
EPAD = ET * P
ITEMS = -(-(ET + NODE_TILES - 1) // 64) * 64
QI = -(-ITEMS // P)
BLOCKS = P // H
U = ITEMS // BLOCKS
SCAN = U * P
PAD_DST = NODE_TILES * P - 1
BIG = 1e30
SLOT_TILES = -(-((2 * N + EXPERTS * (P - 1)) // P) // 4) * 4
TINY_WEIGHT = 1e-19
DX = D + 4
NOWHERE = 2 * NT * P


class Chain:

    def __init__(self, eng, sem, base=0):
        self.eng, self.sem, self.base, self.n = eng, sem, base, 0

    def __call__(self, ins, constant=None):
        self.n += 1
        ins.then_inc(self.sem, 1)
        if constant is not None:
            goal = self.eng.to_reg(self.base + self.n)
            self.eng.wait_ge(constant, 1)
            self.eng.wait_ge(self.sem, goal)
            return
        self.eng.wait_ge(self.sem, self.base + self.n)


UN = 4


class Step:

    def __init__(self, i, c):
        self.i, self.c = i, c
        self.n = i * UN + c

    def ahead(self, by):
        return Step(self.i, self.c + by)

    def slot(self, ring):
        return self.c % ring

    def turn(self, ring):
        return self.i * (UN // ring) + self.c // ring


def wait(eng, sem, value):
    if not (isinstance(value, int) and value <= 0):
        eng.wait_ge(sem, value)


def pipeline(eng, steps, stages):
    most, least = max(a for a, _ in stages), min(a for a, _ in stages)

    def at(i, c):
        for by, stage in stages:
            g = Step(i, c + by)
            if not isinstance(i, int) or 0 <= g.n < steps:
                stage(g)

    turns = (steps - max(most, 0)) // UN
    for c in range(-most, UN):
        at(0, c)
    with eng.Fori(1, turns) as i:
        for c in range(UN):
            at(i, c)
    for c in range(turns * UN, steps - least):
        at(0, c)


def build(nc, x, src, dst, edge_weight, W_l, b_l, W_r, b_r, att, bias, Wg, bg, W1, b1, W2, b2, out):
    with ExitStack() as whole:
        def keep(name, shape, dt=F32):
            return whole.enter_context(nc.sbuf_tensor(name, shape, dt))

        def dram(name, shape, dt=F32):
            return nc.dram_tensor(name, shape, dt, kind="Internal").ap()

        d = dict(
            src=dram("src_tiles", (ET, P), I32), dst=dram("dst_tiles", (ET, P), I32),
            weight=dram("weight_tiles", (ET, P)),
            key=dram("item_keys", (1 + QI * P * P, 1)),
            log_weight=dram("item_log_weights", (QI * P, P)), breaks=dram("item_breaks", (QI * P * P, 1), BF16),
            node_tile=dram("item_node_tile", (QI * P, 1), I32),
            left=dram("left_rows", (NT * P, D)),
            rows=dram("item_rows", (ITEMS // 4, P, 4 * D)),
            slots_in=dram("slots_in", (SLOT_TILES * P, DX)),
            results=dram("results", (NOWHERE + SLOT_TILES * P, D)),
        )
        s = dict(
            ident=keep("ident", [P, P]), identb=keep("identb", [P, P], BF16),
            iota=keep("iota_row", [P, P]), ones=keep("ones_row", [1, P]),
            X=keep("X", [P, NT, D]),
            slot_of=keep("slot_of", [P, NT, 2], I32), tile_expert=keep("tile_expert", [1, P], I32),
        )
        constants(nc, s)
        with ExitStack() as graph:
            def held(name, shape, dt=F32):
                s[name] = graph.enter_context(nc.sbuf_tensor(name, shape, dt))

            held("jrow", [1, QI * P], I32)
            held("dl", [P, QI * P])
            with nc.sbuf_tensor("p_W", [P, KD, 2 * D], F32) as s["W"], nc.sbuf_tensor("p_b", [P, 3 * D], F32) as s["bb"], \
                    nc.sbuf_tensor("p_mv", [P, NT, 2], F32) as s["mv"], nc.sbuf_tensor("p_std", [P, 3, NT], F32) as s["std"]:
                pass
            with nc.sbuf_tensor("s_rows", [P, 4, 2, DX], F32) as s["spread_rows"]:
                pass
            held("alpha", [P, ITEMS, H])
            with ExitStack() as scope:
                s["srcs"] = scope.enter_context(nc.sbuf_tensor("item_src", [P, QI * P], I32))
                schedule(nc, d, s, x, src, dst, edge_weight, W_l, b_l, W_r, b_r, bias)
                s["right"] = scope.enter_context(nc.sbuf_tensor("right_rows", [P, NT, 3, D], BF16))
                project(nc, d, s, W_l, b_l, W_r, b_r, bias)
                scores(nc, d, s, att)
            segment_softmax(nc, d, s)
            held("acc", [P, NT, D + H])
            aggregate(nc, d, s)
            with nc.sbuf_tensor("w1", [P, EXPERTS, KD, HID], F32) as s["w1"], \
                    nc.sbuf_tensor("b1_column", [P, EXPERTS, KH], F32) as s["b1"]:
                route(nc, s, Wg, bg, W1, b1)
                with nc.sbuf_tensor("w2", [P, EXPERTS, KH, D], F32) as s["w2"]:
                    spread_tokens(nc, d, s, W2)
        experts(nc, d, s, b2)
        combine(nc, d, s, out)


def constants(nc, s):
    set_, ramp = nc.alloc_semaphore("const_set"), nc.alloc_semaphore("const_ramp")
    with nc.Block() as block:
        @block.gpsimd
        def _(pool):
            nc.gpsimd.memset(s["ident"][:, :], 0.0).then_inc(set_, 1)
            nc.gpsimd.memset(s["identb"][:, :], 0.0).then_inc(set_, 1)
            nc.gpsimd.memset(s["ones"][:, :], 1.0)
            nc.gpsimd.iota(s["iota"][:, :], [[1, P]], base=0, channel_multiplier=0,
                           allow_small_or_imprecise_dtypes=True).then_inc(ramp, 1)
            pool.wait_ge(set_, 2)
            for m in ("ident", "identb"):
                nc.gpsimd.affine_select(out=s[m][:, :], in_=s[m][:, :], compare_op=ALU.not_equal, fill=1.0,
                                        base=0, pattern=[[-1, P]], channel_multiplier=1).then_inc(ramp, 1)
            pool.wait_ge(ramp, 3)


def schedule(nc, d, s, x, src, dst, edge_weight, W_l, b_l, W_r, b_r, bias):
    sem = nc.alloc_semaphore
    pads_set, padded, ends_in, ends_done = sem("pads_set"), sem("padded"), sem("ends_in"), sem("ends_done")
    spread, spread_copied, items_done = sem("spread"), sem("spread_copied"), sem("items_done")
    gathered = [sem(f"gathered{i}") for i in range(3)]
    local_done, turned, turned_copied = sem("local_done"), sem("turned"), sem("turned_copied")
    cleared, s["x_in"], s["p_w_in"] = sem("x_cleared"), sem("x_in"), sem("p_w_in")
    sqrt_ready, sqrt_done = sem("p_sqrt_ready"), sem("p_sqrt_done")
    keys_back, floored, logged = sem("keys_back"), sem("weights_floored"), sem("weights_logged")
    weights_done, breaks_done = sem("weights_done"), sem("breaks_done")
    stored, row_in, dve, numbered = sem("stored"), sem("row_in"), sem("dve_schedule"), sem("numbered")
    with ExitStack() as scope:
        def sb(name, shape, dt=F32):
            return scope.enter_context(nc.sbuf_tensor(name, shape, dt))

        npad = EPAD - E
        pad_d, pad_s, pad_w = sb("pad_d", [1, npad], I32), sb("pad_s", [1, npad], I32), sb("pad_w", [1, npad])
        pad_k = sb("pad_k", [1, 1])
        ends = sb("ends", [1, 2, ET], I32)
        tile_i = sb("tile_i", [1, 2, ET], I32)
        tile_f = sb("tile_f", [1, 2, ET])
        count = sb("count", [1, ET])
        cum = sb("cum", [1, ET])
        one = sb("one", [1, ET])
        offs = sb("offs", [1, 2, ET])
        offs_all = sb("offs_all", [P, 2, ET])
        number = sb("number", [P, QI])
        stats = sb("stats", [P, NT, 6])
        work, work2 = sb("work", [P, ET]), sb("work2", [P, ET])
        found = sb("found", [P, 2, QI])
        jt = sb("jt", [P, QI])
        t_idx, j_idx, base = sb("t_idx", [P, QI], I32), sb("j_idx", [P, QI], I32), sb("base", [P, QI])
        rows_s, rows_d = sb("rows_s", [P, QI, P], I32), sb("rows_d", [P, QI, P], I32)
        rows_w = sb("rows_w", [P, QI, P])
        sf, df = sb("sf", [P, QI, P]), sb("df", [P, QI, P])
        with_last = sb("with_last", [P, QI, P])
        breaks = sb("breaks", [P, QI, P], BF16)
        no_weight = sb("no_weight", [P, QI, P])
        local, live, key = sb("local", [P, QI, P]), sb("live", [P, QI, P]), sb("key", [P, QI, P])
        ps = scope.enter_context(nc.psum_tensor("ps_spread", [P, 4, 512], F32))
        pt = scope.enter_context(nc.psum_tensor("ps_turn", [P, 2, 512], F32))
        half = ET // 2
        with nc.Block() as block:
            @block.gpsimd
            def _(pool):
                nc.gpsimd.memset(s["X"][:, N // P:NT, :], 0.0).then_inc(cleared, 1)
                nc.gpsimd.memset(pad_d[:, :], PAD_DST).then_inc(pads_set, 1)
                nc.gpsimd.memset(pad_s[:, :], 0).then_inc(pads_set, 1)
                nc.gpsimd.memset(pad_w[:, :], 1.0).then_inc(pads_set, 1)
                nc.gpsimd.memset(pad_k[:, :], -2.0).then_inc(pads_set, 1)
                nc.gpsimd.memset(one[:, :], 1.0).then_inc(pads_set, 1)
                nc.gpsimd.iota(number[:, :], [[P, QI]], base=0, channel_multiplier=1,
                               allow_small_or_imprecise_dtypes=True).then_inc(numbered, 1)
                pool.wait_ge(items_done, 1)
                pool.wait_ge(padded, 16 * 6)
                for q in range(QI):
                    for i, (rows, table) in enumerate(((rows_d, "dst"), (rows_s, "src"), (rows_w, "weight"))):
                        nc.gpsimd.indirect_dma_start(
                            out=rows[:, q, :], out_offset=None, in_=d[table][:, :],
                            in_offset=bass.IndirectOffsetOnAxis(ap=t_idx[:, q:q + 1], axis=0),
                        ).then_inc(gathered[i], 16)

            @block.sync
            def _(sp):
                flat = {k: d[k].rearrange("t p -> (t p)") for k in ("src", "dst", "weight")}
                for k, a in (("src", src), ("dst", dst), ("weight", edge_weight)):
                    sp.dma_start(flat[k][0:E].rearrange("(a b) -> a b", a=16),
                                 a.rearrange("(a b) -> a b", a=16)).then_inc(padded, 16)
                sp.wait_ge(pads_set, 5)
                for k, pad in (("src", pad_s), ("dst", pad_d), ("weight", pad_w)):
                    sp.dma_start(flat[k][E:EPAD].rearrange("(a b) -> a b", a=1), pad[:, :]).then_inc(padded, 16)
                sp.dma_start(d["key"][0:1, :], pad_k[:, :]).then_inc(stored, 16)
                sp.wait_ge(padded, 16 * 6)
                for i, at in ((0, 0), (1, P - 1)):
                    sp.dma_start(ends[:, i:i + 1, :].rearrange("a i t -> a (i t)"),
                                 d["dst"][:, at:at + 1].rearrange("t o -> o t"),
                                 allow_slow_non_contiguous=True).then_inc(ends_in, 16)
                sp.wait_ge(items_done, 1)
                sp.dma_start(d["node_tile"].rearrange("(q p) o -> p (q o)", p=P), j_idx[:, :],
                             allow_slow_non_contiguous=True).then_inc(stored, 16)
                sp.wait_ge(local_done, 2)
                sp.dma_start(d["key"][1:1 + QI * P * P, :].rearrange("(q p e) o -> p q (e o)", p=P, q=QI),
                             key[:, :, :]).then_inc(stored, 16)
                sp.wait_ge(stored, 16 * 3)
                sp.dma_start(with_last[:, :, :], d["key"].rearrange("e o -> (e o)")[0:QI * P * P]
                             .rearrange("(q p e) -> p q e", p=P, q=QI)).then_inc(keys_back, 16)
                sp.dma_start(s["jrow"][:, :], d["node_tile"].rearrange("n o -> o n"),
                             allow_slow_non_contiguous=True).then_inc(row_in, 16)
                sp.wait_ge(weights_done, 1)
                sp.dma_start(d["log_weight"].rearrange("(q p) e -> p q e", p=P), rows_w[:, :, :]).then_inc(stored, 16)
                sp.wait_ge(breaks_done, 1)
                sp.dma_start(d["breaks"].rearrange("(q p e) o -> p q (e o)", p=P, q=QI), breaks[:, :, :]).then_inc(stored, 16)
                sp.wait_ge(stored, 16 * 5)
                sp.wait_ge(row_in, 16)

            @block.tensor
            def _(pe):
                pe.wait_ge(ends_done, 1)
                for a in range(2):
                    for b in range(2):
                        last = nc.tensor.matmul(ps[:, 2 * a + b, 0:half], s["ones"][0:1, :],
                                                offs[0:1, a, b * half:(b + 1) * half], start=True, stop=True)
                last.then_inc(spread, 1)
                for i in range(2 * QI):
                    pe.wait_ge(local_done, 1 if i < QI else 3)
                    if i >= 2:
                        pe.wait_ge(turned_copied, i - 1)
                    from_ = local if i < QI else sf
                    nc.tensor.transpose(pt[:, i % 2, 0:P], from_[:, i % QI, :], s["ident"][:, :]).then_inc(turned, 1)

            @block.scalar
            def _(act):
                full = N // P
                act.wait_ge(padded, 16 * 6)
                act.dma_start(s["X"][:, 0:full, :], x[0:full * P, :].rearrange("(t p) f -> p t f", p=P)).then_inc(s["x_in"], 16)
                act.wait_ge(cleared, 1)
                act.dma_start(s["X"][0:N - full * P, full, :], x[full * P:N, :]).then_inc(s["x_in"], 16)
                for i, w in enumerate((W_l, W_r)):
                    act.dma_start(s["W"][:, :, i * D:(i + 1) * D], w.rearrange("(k p) f -> p k f", p=P)).then_inc(s["p_w_in"], 16)
                for i, b in enumerate((b_l, b_r, bias)):
                    act.dma_start(s["bb"][:, i * D:(i + 1) * D], b.partition_broadcast(P)).then_inc(s["p_w_in"], 16)
                act.wait_ge(sqrt_ready, 1)
                nc.scalar.activation(s["std"][:, 1, :], s["std"][:, 0, :], ACT.Sqrt).then_inc(sqrt_done, 1)
                for i in range(2 * QI):
                    act.wait_ge(turned, i + 1)
                    to = (s["dl"] if i < QI else s["srcs"])[:, (i % QI) * P:(i % QI + 1) * P]
                    nc.scalar.activation(to, pt[:, i % 2, 0:P], ACT.Copy).then_inc(turned_copied, 1)
                act.wait_ge(floored, 1)
                nc.scalar.activation(rows_w[:, :, :], rows_w[:, :, :], ACT.Ln).then_inc(logged, 1)

            @block.vector
            def _(v):
                step = Chain(v, dve)
                v.wait_ge(ends_in, 32)
                step(nc.vector.tensor_scalar(tile_i[:, :, :], ends[:, :, :], 7, None, ALU.logical_shift_right))
                step(nc.vector.tensor_copy(tile_f[:, :, :], tile_i[:, :, :]))
                step(nc.vector.scalar_tensor_tensor(count[:, :], tile_f[:, 1, :], 1.0, tile_f[:, 0, :],
                                                    ALU.add, ALU.subtract))
                v.wait_ge(pads_set, 5)
                step(nc.vector.tensor_tensor_scan(cum[:, :], one[:, :], count[:, :], 0.0, ALU.mult, ALU.add))
                step(nc.vector.tensor_tensor(offs[:, 0, :], cum[:, :], count[:, :], ALU.subtract))
                step(nc.vector.tensor_tensor(count[:, :], tile_f[:, 0, :], offs[:, 0, :], ALU.subtract))
                step(nc.vector.tensor_copy(offs[:, 1, 0:1], count[:, 0:1]))
                nc.vector.tensor_tensor(offs[:, 1, 1:ET], count[:, 1:ET], count[:, 0:ET - 1], ALU.subtract
                                        ).then_inc(ends_done, 1)
                v.wait_ge(spread, 1)
                for a in range(2):
                    step(nc.vector.tensor_copy(offs_all[:, a, :].rearrange("p (b n) -> p b n", b=2),
                                               ps[:, 2 * a:2 * a + 2, 0:half]))
                v.wait_ge(numbered, 1)
                for q in range(QI):
                    own = number[:, q:q + 1]
                    step(nc.vector.tensor_scalar(work[:, :], offs_all[:, 0, :], own, None, ALU.is_le))
                    step(nc.vector.tensor_reduce(found[:, 0, q:q + 1], work[:, :], AX.X, ALU.add))
                    step(nc.vector.scalar_tensor_tensor(work2[:, :], offs_all[:, 0, :], own, offs_all[:, 1, :],
                                                        ALU.is_le, ALU.mult))
                    step(nc.vector.tensor_reduce(found[:, 1, q:q + 1], work2[:, :], AX.X, ALU.add))
                step(nc.vector.tensor_scalar(t_idx[:, :], found[:, 0, :], -1.0, None, ALU.add))
                step(nc.vector.tensor_tensor(jt[:, :], found[:, 1, :], number[:, :], ALU.add))
                step(nc.vector.tensor_scalar(base[:, :], jt[:, :], float(P), None, ALU.mult))
                nc.vector.tensor_scalar(j_idx[:, :], jt[:, :], float(NT - 1), None, ALU.min).then_inc(items_done, 1)
                v.wait_ge(s["x_in"], 32)
                for i in range(NT):
                    last = nc.vector.bn_stats(stats[:, i, :], s["X"][:, i, :])
                step(last)
                moments(nc, v, step, stats, s["mv"], s["std"], sqrt_ready, sqrt_done)
                v.wait_ge(gathered[0], 16 * QI)
                step(nc.vector.tensor_copy(df[:, :, :], rows_d[:, :, :]))
                for q in range(QI):
                    last = nc.vector.tensor_scalar(local[:, q, :], df[:, q, :], base[:, q:q + 1], None, ALU.subtract)
                last.then_inc(local_done, 1)
                v.wait_ge(local_done, 1)
                step(nc.vector.tensor_scalar(live[:, :, :], local[:, :, :], 0.0, None, ALU.is_ge))
                step(nc.vector.scalar_tensor_tensor(live[:, :, :], local[:, :, :], float(P), live[:, :, :],
                                                    ALU.is_lt, ALU.mult))
                step(nc.vector.scalar_tensor_tensor(key[:, :, :], df[:, :, :], 1.0, live[:, :, :],
                                                    ALU.add, ALU.mult))
                nc.vector.tensor_scalar(key[:, :, :], key[:, :, :], -1.0, None, ALU.add).then_inc(local_done, 1)
                v.wait_ge(gathered[1], 16 * QI)
                nc.vector.tensor_copy(sf[:, :, :], rows_s[:, :, :]).then_inc(local_done, 1)
                v.wait_ge(gathered[2], 16 * QI)
                v.wait_ge(local_done, 2)
                step(nc.vector.tensor_scalar(no_weight[:, :, :], rows_w[:, :, :], TINY_WEIGHT, None, ALU.is_lt))
                nc.vector.tensor_scalar(rows_w[:, :, :], rows_w[:, :, :], TINY_WEIGHT, None, ALU.max).then_inc(floored, 1)
                step(nc.vector.scalar_tensor_tensor(no_weight[:, :, :], key[:, :, :], 0.0, no_weight[:, :, :],
                                                    ALU.is_lt, ALU.add))
                v.wait_ge(logged, 1)
                nc.vector.scalar_tensor_tensor(rows_w[:, :, :], no_weight[:, :, :], -BIG, rows_w[:, :, :],
                                               ALU.mult, ALU.add).then_inc(weights_done, 1)
                v.wait_ge(keys_back, 16)
                step(nc.vector.tensor_tensor(live[:, :, :], with_last[:, :, :], key[:, :, :], ALU.not_equal))
                nc.vector.tensor_scalar(breaks[:, :, :], live[:, :, :], -BIG, None, ALU.mult).then_inc(breaks_done, 1)


def moments(nc, v, step, stats, mv, std, sqrt_ready, sqrt_done):
    for i in range(NT):
        last = nc.vector.bn_aggr(mv[:, i, :], stats[:, i, :])
    step(last)
    nc.vector.tensor_scalar(std[:, 0, :], mv[:, :, 1], EPS, None, ALU.add).then_inc(sqrt_ready, 1)
    v.wait_ge(sqrt_done, 1)
    step(nc.vector.reciprocal(std[:, 2, :], std[:, 1, :]))


def project(nc, d, s, W_l, b_l, W_r, b_r, bias):
    sem = nc.alloc_semaphore
    w_in = s["p_w_in"]
    zero_set, zeroed = sem("zero_set"), sem("zeroed")
    normed, turned, turned_copied = sem("p_normed"), sem("p_turned"), sem("p_turned_copied")
    projected, biased, high, less_high = sem("p_projected"), sem("p_biased"), sem("p_high"), sem("p_less_high")
    middle, less_middle, low, residual = sem("p_middle"), sem("p_less_middle"), sem("p_low"), sem("p_residual")
    stored = [sem(f"left_stored{i}") for i in range(4)]
    with ExitStack() as scope:
        def sb(name, shape, dt=F32):
            return scope.enter_context(nc.sbuf_tensor(name, shape, dt))

        X = s["X"]
        W, bb, mv, std = s["W"], s["bb"], s["mv"], s["std"]
        xn = sb("p_xn", [P, 2, D])
        xT = sb("p_xT", [P, 2, KD * P])
        y = sb("p_y", [P, 4, 2 * D])
        zero = sb("p_zero", [P, 2, DX])
        r1, r2 = sb("p_r1", [P, 2, D]), sb("p_r2", [P, 2, D])
        pt = scope.enter_context(nc.psum_tensor("p_pt", [P, 2, 512], F32))
        py = scope.enter_context(nc.psum_tensor("p_py", [P, 2, 512], F32))
        def row(g):
            return X[:, bass.ds(g.n, 1), :].rearrange("p a f -> p (a f)")

        def part(g, c):
            return s["right"][:, bass.ds(g.n, 1), c, :].rearrange("p a f -> p (a f)")

        with nc.Block() as block:
            @block.gpsimd
            def _(pool):
                nc.gpsimd.memset(zero[:, :, 0:D], 0.0).then_inc(zero_set, 1)
                nc.gpsimd.memset(zero[:, :, D:DX], float(NOWHERE)).then_inc(zero_set, 1)
                pool.wait_ge(w_in, 80)

                def add_bias(g):
                    wait(pool, normed, g.n + 1)
                    nc.gpsimd.tensor_tensor(row(g), row(g), bb[:, 2 * D:3 * D], ALU.add).then_inc(residual, 1)

                pipeline(pool, NT, [(0, add_bias)])

            @block.sync
            def _(sp):
                sp.wait_ge(zero_set, 2)

                def clear(t):
                    sp.dma_start(d["slots_in"][bass.ds(t * (2 * P), 2 * P), :].rearrange("(p a) f -> p (a f)", a=2),
                                 zero[:, :, :].rearrange("p a f -> p (a f)")).then_inc(zeroed, 16)

                def store(g):
                    wait(sp, biased, g.n + 1)
                    sp.dma_start(d["left"][bass.ds(g.n * P, P), :], y[:, g.slot(4), 0:D]).then_inc(stored[g.slot(4)], 16)
                    clear(g.n)

                pipeline(sp, NT, [(0, store)])
                for t in range(NT, SLOT_TILES // 2):
                    clear(t)
                sp.wait_ge(zeroed, 16 * (SLOT_TILES // 2))
                for k in range(4):
                    sp.wait_ge(stored[k], 16 * len(range(k, NT, 4)))

            @block.vector
            def _(v):
                v.wait_ge(w_in, 80)

                def norm(g):
                    wait(v, turned, g.n - 1)
                    nc.vector.tensor_scalar(xn[:, g.slot(2), :], row(g), mv[:, bass.ds(g.n, 1), 0],
                                            std[:, 2, bass.ds(g.n, 1)], ALU.subtract, ALU.mult).then_inc(normed, 1)

                def add_biases(g):
                    wait(v, projected, g.n + 1)
                    wait(v, stored[g.slot(4)], g.turn(4) * 16)
                    wait(v, less_high, g.n - 3)
                    nc.vector.tensor_tensor(y[:, g.slot(4), :], py[:, g.slot(2), :], bb[:, 0:2 * D],
                                            ALU.add).then_inc(biased, 1)

                def take_high(g):
                    wait(v, high, g.n + 1)
                    wait(v, middle, g.n - 1)
                    wait(v, less_middle, g.n - 1)
                    nc.vector.tensor_tensor(r1[:, g.slot(2), :], y[:, g.slot(4), D:2 * D], part(g, 0),
                                            ALU.subtract).then_inc(less_high, 1)

                def take_middle(g):
                    wait(v, middle, g.n + 1)
                    wait(v, low, g.n - 1)
                    nc.vector.tensor_tensor(r2[:, g.slot(2), :], r1[:, g.slot(2), :], part(g, 1),
                                            ALU.subtract).then_inc(less_middle, 1)

                pipeline(v, NT, [(2, norm), (0, add_biases), (-1, take_high), (-2, take_middle)])

            @block.scalar
            def _(act):
                def copy_turned(g):
                    wait(act, turned, g.n + 1)
                    wait(act, projected, g.n - 1)
                    nc.scalar.activation(xT[:, g.slot(2), :], pt[:, g.slot(2), 0:KD * P], ACT.Copy).then_inc(turned_copied, 1)

                def copy_high(g):
                    wait(act, biased, g.n + 1)
                    nc.scalar.activation(part(g, 0), y[:, g.slot(4), D:2 * D], ACT.Copy).then_inc(high, 1)

                def copy_middle(g):
                    wait(act, less_high, g.n + 1)
                    nc.scalar.activation(part(g, 1), r1[:, g.slot(2), :], ACT.Copy).then_inc(middle, 1)

                def copy_low(g):
                    wait(act, less_middle, g.n + 1)
                    nc.scalar.activation(part(g, 2), r2[:, g.slot(2), :], ACT.Copy).then_inc(low, 1)

                pipeline(act, NT, [(1, copy_turned), (0, copy_high), (-1, copy_middle), (-2, copy_low)])

            @block.tensor
            def _(pe):
                pe.wait_ge(w_in, 80)

                def turn(g):
                    wait(pe, normed, g.n + 1)
                    wait(pe, turned_copied, g.n - 1)
                    for h in range(KD):
                        last = nc.tensor.transpose(pt[:, g.slot(2), h * P:(h + 1) * P],
                                                   xn[:, g.slot(2), h * P:(h + 1) * P], s["ident"][:, :])
                    last.then_inc(turned, 1)

                def multiply(g):
                    wait(pe, turned_copied, g.n + 1)
                    wait(pe, biased, g.n - 1)
                    for h in range(KD):
                        last = nc.tensor.matmul(py[:, g.slot(2), :], xT[:, g.slot(2), h * P:(h + 1) * P], W[:, h, :],
                                                start=(h == 0), stop=(h == KD - 1))
                    last.then_inc(projected, 1)

                pipeline(pe, NT, [(1, turn), (0, multiply)])


G = 4
RING = 4
GROUPS = ITEMS // G


def node_tiles(eng, regs, s, g):
    eng.load(regs, s["jrow"][0:1, bass.ds(g.n * G, len(regs))])
    return [eng.snap(r, min_val=0, max_val=NT - 1) for r in regs]


def scores(nc, d, s, att):
    sem = nc.alloc_semaphore
    att_in, att_set = sem("att_in"), sem("att_set")
    listed = sem("listed")
    gathered = [sem(f"g_gathered{i}") for i in range(RING)]
    spilled = [sem(f"g_spilled{i}") for i in range(RING)]
    hot, hot_turned, hot_copied = sem("g_hot"), sem("g_hot_turned"), sem("g_hot_copied")
    spread, summed, leaked = sem("g_spread"), sem("g_summed"), sem("g_leaked")
    turned, turned_copied, scored, kept = sem("g_turned"), sem("g_turned_copied"), sem("g_scored"), sem("g_kept")
    with ExitStack() as scope:
        def sb(name, shape, dt=F32):
            return scope.enter_context(nc.sbuf_tensor(name, shape, dt))

        def pb(name, shape, dt=F32):
            return scope.enter_context(nc.psum_tensor(name, shape, dt))

        idx = sb("idx", [P, RING, G], I32)
        rows = sb("rows", [P, RING, G, D])
        hots = sb("hots", [P, 2, G, P], BF16)
        hotT = sb("hotT", [P, 2, G, P], BF16)
        S = sb("S", [P, G * D])
        L = sb("L", [P, 2, G * D])
        LT = sb("LT", [P, 2, G * KD * P])
        attm = sb("attm", [P, KD, H])
        p_hot = pb("p_hot", [P, 1024], BF16)
        p_row = pb("p_row", [P, 2, G * D])
        p_T = pb("p_T", [P, G * KD * P])
        p_a = pb("p_a", [P, 512])
        with nc.Block() as block:
            @block.gpsimd
            def _(pool):
                nc.gpsimd.memset(attm[:, :, :], 0.0).then_inc(att_set, 1)

                def gather(g):
                    r = g.slot(RING)
                    goals = ((listed, g.n + 1),
                             (spilled[r], g.turn(RING) * 16),
                             (summed, g.n - (RING - 1)))
                    goals = [(m, v if isinstance(v, int) else pool.to_reg(v)) for m, v in goals]
                    pool.wait_ge(att_set, 1)
                    for m, v in goals:
                        wait(pool, m, v)
                    for n in range(G):
                        nc.gpsimd.indirect_dma_start(
                            out=rows[:, r, n, :], out_offset=None, in_=d["left"][:, :],
                            in_offset=bass.IndirectOffsetOnAxis(ap=idx[:, r, n:n + 1], axis=0),
                        ).then_inc(gathered[r], 16)

                pipeline(pool, GROUPS, [(0, gather)])

            @block.sync
            def _(sp):
                sp.wait_ge(att_set, 1)
                for h in range(H):
                    at = h * C
                    sp.dma_start(attm[at % P:at % P + C, at // P, h:h + 1],
                                 att[h:h + 1, :].rearrange("a c -> c a"),
                                 allow_slow_non_contiguous=True).then_inc(att_in, 16)

                def spill(g):
                    r = g.slot(RING)
                    wait(sp, gathered[r], (g.turn(RING) + 1) * (16 * G))
                    sp.dma_start(d["rows"][bass.ds(g.n, 1), :, :].rearrange("a p f -> (a p) f"),
                                 rows[:, r, :, :].rearrange("p g f -> p (g f)")).then_inc(spilled[r], 16)

                pipeline(sp, GROUPS, [(0, spill)])
                for r in range(RING):
                    sp.wait_ge(spilled[r], 16 * (GROUPS // RING))

            @block.vector
            def _(v):
                def one_hot(g):
                    wait(v, hot_turned, g.n - 1)
                    nc.vector.tensor_tensor(
                        hots[:, g.slot(2), :, :],
                        s["iota"][:, :].unsqueeze(1).to_broadcast([P, G, P]),
                        s["dl"][:, bass.ds(g.n * G, G)].unsqueeze(2).to_broadcast([P, G, P]),
                        ALU.is_equal).then_inc(hot, 1)

                def add_and_leak(g):
                    r = g.slot(RING)
                    wait(v, spread, g.n + 1)
                    wait(v, gathered[r], (g.turn(RING) + 1) * (16 * G))
                    wait(v, leaked, g.n)
                    nc.vector.tensor_tensor(S[:, :], p_row[:, g.slot(2), :],
                                            rows[:, r, :, :].rearrange("p g f -> p (g f)"),
                                            ALU.add).then_inc(summed, 1)
                    wait(v, summed, g.n + 1)
                    wait(v, turned, g.n - 1)
                    nc.vector.scalar_tensor_tensor(L[:, g.slot(2), :], S[:, :], SLOPE, S[:, :],
                                                   ALU.mult, ALU.max).then_inc(leaked, 1)

                def list_sources(g):
                    r = g.slot(RING)
                    wait(v, gathered[r], g.turn(RING) * (16 * G))
                    nc.vector.tensor_copy(idx[:, r, :], s["srcs"][:, bass.ds(g.n * G, G)]).then_inc(listed, 1)

                pipeline(v, GROUPS, [(1 + RING, list_sources), (3, one_hot), (1, add_and_leak)])

            @block.scalar
            def _(act):
                def copy_hot(g):
                    wait(act, hot_turned, g.n + 1)
                    wait(act, spread, g.n - 1)
                    nc.scalar.activation(hotT[:, g.slot(2), :, :],
                                         p_hot[:, 0:G * P].rearrange("p (n e) -> p n e", n=G), ACT.Copy).then_inc(hot_copied, 1)

                def copy_turned(g):
                    wait(act, turned, g.n + 1)
                    wait(act, scored, g.n - 1)
                    nc.scalar.activation(LT[:, g.slot(2), :], p_T[:, :], ACT.Copy).then_inc(turned_copied, 1)

                def keep_scores(g):
                    wait(act, scored, g.n + 1)
                    nc.scalar.activation(s["alpha"][:, bass.ds(g.n * G, G), :],
                                         p_a[:, 0:G * H].rearrange("p (n h) -> p n h", n=G), ACT.Copy).then_inc(kept, 1)

                pipeline(act, GROUPS, [(2, copy_hot), (0, copy_turned), (-1, keep_scores)])

            @block.tensor
            def _(pe):
                pe.wait_ge(att_in, 16 * H)

                def turn_hot(g):
                    wait(pe, hot, g.n + 1)
                    wait(pe, hot_copied, g.n)
                    for n in range(G):
                        last = nc.tensor.transpose(p_hot[:, n * P:(n + 1) * P], hots[:, g.slot(2), n, :], s["identb"][:, :])
                    last.then_inc(hot_turned, 1)

                regs = [nc.tensor.alloc_register(f"right_tile{n}") for n in range(G)]

                def spread_rows(g):
                    tiles = node_tiles(nc.tensor, regs, s, g)
                    wait(pe, hot_copied, g.n + 1)
                    wait(pe, summed, g.n - 1)
                    for n in range(G):
                        j = tiles[n]
                        for c in range(3):
                            last = nc.tensor.matmul(p_row[:, g.slot(2), n * D:(n + 1) * D], hotT[:, g.slot(2), n, :],
                                                    s["right"][:, bass.ds(j, 1), c, :].rearrange("p a f -> p (a f)"),
                                                    start=(c == 0), stop=(c == 2))
                    last.then_inc(spread, 1)

                def turn_leaked(g):
                    wait(pe, leaked, g.n + 1)
                    wait(pe, turned_copied, g.n)
                    for n in range(G * KD):
                        last = nc.tensor.transpose(p_T[:, n * P:(n + 1) * P], L[:, g.slot(2), n * P:(n + 1) * P],
                                                   s["ident"][:, :])
                    last.then_inc(turned, 1)

                def score(g):
                    wait(pe, turned_copied, g.n + 1)
                    wait(pe, kept, g.n)
                    for n in range(G):
                        for h in range(KD):
                            at = (n * KD + h) * P
                            last = nc.tensor.matmul(p_a[:, n * H:(n + 1) * H], LT[:, g.slot(2), at:at + P], attm[:, h, :],
                                                    start=(h == 0), stop=(h == KD - 1))
                    last.then_inc(scored, 1)

                pipeline(pe, GROUPS, [(2, turn_hot), (1, spread_rows), (0, turn_leaked), (-1, score)])


BY = 4


def segment_softmax(nc, d, s):
    sem = nc.alloc_semaphore
    inputs_in, ends_in, spreads = sem("m_inputs_in"), sem("m_ends_in"), sem("m_spreads")
    last_spread, last_copied = sem("m_last_spread"), sem("m_last_copied")
    flattened, turned, scores_copied = sem("m_flattened"), sem("m_turned"), sem("m_scores_copied")
    breaks_copied, dve = sem("m_breaks_copied"), sem("dve_softmax")
    to_row, row, to_col, col = sem("m_to_row"), sem("m_row"), sem("m_to_col"), sem("m_col")
    logs_in = sem("m_logs_in")
    shifted, expd, back, back_copied = sem("m_shifted"), sem("m_expd"), sem("m_back"), sem("m_back_copied")
    with ExitStack() as scope:
        def sb(name, shape, dt=F32):
            return scope.enter_context(nc.sbuf_tensor(name, shape, dt))

        A = sb("m_A", [P, SCAN])
        R = sb("m_R", [P, SCAN + 1])
        to_heads = sb("m_to_heads", [BLOCKS, P], BF16)
        ends = sb("m_ends", [P, 2])
        end_keys = sb("m_end_keys", [1, 2, BLOCKS])
        rows = sb("m_rows", [1, 8, P])
        carry = sb("m_carry", [P, 2])
        flat = sb("m_flat", [P, 2, BY * P])
        M = sb("m_M", [P, SCAN])
        with nc.sbuf_tensor("m_breaks", [BLOCKS, SCAN + 1], BF16) as breaks:
            pass
        K = sb("m_K", [P, SCAN])
        pt = scope.enter_context(nc.psum_tensor("m_pt", [P, 2, BY * P], F32))
        pb = scope.enter_context(nc.psum_tensor("m_pb", [P, 2, BY * P], F32))
        pr = scope.enter_context(nc.psum_tensor("m_pr", [P, 512], F32))
        turns = U // BY
        by_block = s["alpha"][:, :, :].rearrange("p (b u) h -> p u h b", b=BLOCKS)

        def of_turn(tensor, g):
            return tensor[:, bass.ds(g.n * (BY * P), BY * P)]

        with nc.Block() as block:
            @block.sync
            def _(sp):
                sp.dma_start(breaks[:, 0:SCAN], d["breaks"][0:BLOCKS * SCAN, :]
                             .rearrange("(b e) o -> b (e o)", b=BLOCKS)).then_inc(inputs_in, 16)
                sp.dma_start(breaks[:, SCAN:SCAN + 1], d["breaks"][SCAN:SCAN + (BLOCKS - 1) * SCAN + 1, :][::SCAN, :],
                             allow_slow_non_contiguous=True).then_inc(inputs_in, 16)
                for h in range(H):
                    sp.dma_start(M[h * BLOCKS:(h + 1) * BLOCKS, :], d["log_weight"][0:ITEMS, :]
                                 .rearrange("(b u) e -> b (u e)", b=BLOCKS)).then_inc(logs_in, 16)
                for i, at in enumerate((1, SCAN)):
                    sp.dma_start(end_keys[:, i:i + 1, :].rearrange("a i b -> a (i b)"),
                                 d["key"][at:at + (BLOCKS - 1) * SCAN + 1, :][::SCAN, :].rearrange("b o -> o b"),
                                 allow_slow_non_contiguous=True).then_inc(ends_in, 16)

            @block.vector
            def _(v):
                step = Chain(v, dve)
                nc.vector.tensor_copy(to_heads[:, :].rearrange("p (h b) -> p h b", h=H),
                                      s["identb"][0:BLOCKS, 0:BLOCKS].unsqueeze(1)
                                      .to_broadcast([BLOCKS, H, BLOCKS])).then_inc(spreads, 1)

                def flatten(g):
                    wait(v, turned, g.n - 1)
                    nc.vector.tensor_copy(flat[:, g.slot(2), :].rearrange("p (u h b) -> p u h b", u=BY, h=H),
                                          by_block[:, bass.ds(g.n * BY, BY), :, :]).then_inc(flattened, 1)

                def add_logs(g):
                    wait(v, turned, g.n + 1)
                    wait(v, logs_in, 16 * H)
                    nc.vector.tensor_tensor(of_turn(A, g), pt[:, g.slot(2), :], of_turn(M, g), ALU.add).then_inc(scores_copied, 1)

                pipeline(v, turns, [(1, flatten), (0, add_logs)])
                v.wait_ge(last_spread, 1)
                nc.vector.tensor_copy(R[:, SCAN:SCAN + 1], pr[:, 0:1]).then_inc(last_copied, 1)
                heads = lambda a: rows[:, a, :].rearrange("o (h b) -> o h b", h=H)
                v.wait_ge(ends_in, 32)
                step(nc.vector.tensor_tensor(end_keys[:, 0, :], end_keys[:, 0, :], end_keys[:, 1, :], ALU.not_equal))
                step(nc.vector.tensor_scalar(heads(2), end_keys[:, 0:1, :].to_broadcast([1, H, BLOCKS]),
                                             -BIG, None, ALU.mult))
                v.wait_ge(breaks_copied, turns)
                v.wait_ge(last_copied, 1)
                v.wait_ge(scores_copied, turns)
                step(nc.vector.tensor_tensor_scan(M[:, :], R[:, 0:SCAN], A[:, :], -BIG, ALU.add, ALU.max))
                step(nc.vector.tensor_copy(ends[:, 0:1], M[:, SCAN - 1:SCAN]))
                nc.vector.tensor_copy(ends[:, 1:2], R[:, 0:1]).then_inc(to_row, 1)
                step(nc.vector.memset(rows[:, 3:8, :], -BIG))
                v.wait_ge(row, 1)
                step(nc.vector.tensor_copy(rows[:, 0:2, :], pr[0:1, 0:2 * P].rearrange("o (c b) -> o c b", c=2)))

                def pass_on(onward):
                    to, from_ = slice(1, BLOCKS), slice(0, BLOCKS - 1)
                    if not onward:
                        to, from_ = from_, to
                    step(nc.vector.tensor_tensor(heads(5)[:, :, to], heads(2)[:, :, from_], heads(1)[:, :, to], ALU.add))
                    step(nc.vector.tensor_tensor(heads(6)[:, :, to], heads(0)[:, :, from_], heads(1)[:, :, to], ALU.add))
                    along = slice(None, None, 1 if onward else -1)
                    step(nc.vector.tensor_tensor_scan(rows[:, 3, along], rows[:, 5, along], rows[:, 6, along], -BIG,
                                                      ALU.add, ALU.max))
                    nc.vector.tensor_scalar(rows[:, 3, :], rows[:, 3, :], -BIG, None, ALU.max).then_inc(to_col, 1)

                pass_on(True)
                v.wait_ge(col, 1)
                step(nc.vector.tensor_copy(carry[:, 0:1], pr[:, 0:1]))
                step(nc.vector.tensor_tensor_scan(M[:, :], R[:, 0:SCAN], A[:, :], carry[:, 0:1], ALU.add, ALU.max))
                step(nc.vector.tensor_tensor_scan(K[:, ::-1], R[:, SCAN:0:-1], M[:, ::-1], -BIG,
                                                  ALU.add, ALU.max))
                step(nc.vector.tensor_copy(ends[:, 0:1], K[:, 0:1]))
                nc.vector.tensor_copy(ends[:, 1:2], R[:, SCAN:SCAN + 1]).then_inc(to_row, 1)
                step(nc.vector.memset(rows[:, 3:8, :], -BIG))
                v.wait_ge(row, 2)
                step(nc.vector.tensor_copy(rows[:, 0:2, :], pr[0:1, 0:2 * P].rearrange("o (c b) -> o c b", c=2)))
                pass_on(False)
                v.wait_ge(col, 2)
                step(nc.vector.tensor_copy(carry[:, 1:2], pr[:, 0:1]))
                step(nc.vector.tensor_tensor_scan(K[:, ::-1], R[:, SCAN:0:-1], M[:, ::-1], carry[:, 1:2],
                                                  ALU.add, ALU.max))

                def shift(g):
                    wait(v, expd, g.n - 1)
                    wait(v, back, g.n - 1)
                    nc.vector.tensor_tensor(flat[:, g.slot(2), :], of_turn(A, g), of_turn(K, g),
                                            ALU.subtract).then_inc(shifted, 1)

                def put_back(g):
                    wait(v, back, g.n + 1)
                    nc.vector.tensor_copy(by_block[:, bass.ds(g.n * BY, BY), :, :],
                                          pt[:, g.slot(2), :].rearrange("p (u h b) -> p u h b", u=BY, h=H)
                                          ).then_inc(back_copied, 1)

                pipeline(v, turns, [(1, shift), (0, put_back)])

            @block.scalar
            def _(act):
                def copy_breaks(g):
                    wait(act, turned, g.n + 1)
                    nc.scalar.activation(of_turn(R, g), pb[:, g.slot(2), :], ACT.Copy).then_inc(breaks_copied, 1)

                pipeline(act, turns, [(0, copy_breaks)])
                nc.scalar.preload_act_table_set("natural_log_exp_and_others")

                def exp(g):
                    wait(act, shifted, g.n + 1)
                    nc.scalar.activation(flat[:, g.slot(2), :], flat[:, g.slot(2), :], ACT.Exp).then_inc(expd, 1)

                pipeline(act, turns, [(0, exp)])

            @block.tensor
            def _(pe):
                pe.wait_ge(spreads, 1)
                pe.wait_ge(inputs_in, 32)

                def turn(g):
                    wait(pe, flattened, g.n + 1)
                    wait(pe, scores_copied, g.n - 1)
                    wait(pe, breaks_copied, g.n - 1)
                    nc.tensor.matmul(pb[:, g.slot(2), :], to_heads[:, :], of_turn(breaks, g), start=True, stop=True)
                    for n in range(BY):
                        last = nc.tensor.transpose(pt[:, g.slot(2), n * P:(n + 1) * P],
                                                   flat[:, g.slot(2), n * P:(n + 1) * P], s["ident"][:, :])
                    last.then_inc(turned, 1)

                pipeline(pe, turns, [(0, turn)])
                nc.tensor.matmul(pr[:, 0:1], to_heads[:, :], breaks[:, SCAN:SCAN + 1], start=True, stop=True
                                 ).then_inc(last_spread, 1)
                pe.wait_ge(last_copied, 1)
                for r in range(2):
                    pe.wait_ge(to_row, r + 1)
                    for c in range(2):
                        last = nc.tensor.matmul(pr[0:1, c * P:(c + 1) * P], ends[:, c:c + 1], s["ident"][:, :],
                                                start=True, stop=True)
                    last.then_inc(row, 1)
                    pe.wait_ge(to_col, r + 1)
                    nc.tensor.matmul(pr[:, 0:1], rows[0:1, 3, :], s["ones"][0:1, 0:1], start=True, stop=True).then_inc(col, 1)

                def turn_back(g):
                    wait(pe, expd, g.n + 1)
                    wait(pe, back_copied, g.n - 1)
                    for n in range(BY):
                        last = nc.tensor.transpose(pt[:, g.slot(2), n * P:(n + 1) * P],
                                                   flat[:, g.slot(2), n * P:(n + 1) * P], s["ident"][:, :])
                    last.then_inc(back, 1)

                pipeline(pe, turns, [(0, turn_back)])


def aggregate(nc, d, s):
    sem = nc.alloc_semaphore
    loaded = [sem(f"a_loaded{i}") for i in range(RING)]
    cleared, distance, hot = sem("a_cleared"), sem("a_distance"), sem("a_hot")
    weighted, weights_put = sem("a_weighted"), sem("a_weights_put")
    summed, added = sem("a_summed"), sem("a_added")
    with ExitStack() as scope:
        def sb(name, shape, dt=F32):
            return scope.enter_context(nc.sbuf_tensor(name, shape, dt))

        rows = sb("a_rows", [P, RING, G, D])
        far = sb("a_far", [P, 2, G, P])
        hots = sb("a_hots", [P, RING, G, P])
        W = sb("a_W", [P, RING, G, D + H])
        unit = sb("a_unit", [P, 1])
        acc = s["acc"]
        ps = scope.enter_context(nc.psum_tensor("a_ps", [P, 2, G, 512], F32))

        with nc.Block() as block:
            @block.gpsimd
            def _(pool):
                nc.gpsimd.memset(unit[:, :], 1.0).then_inc(cleared, 1)

                def weigh(g):
                    wait(pool, summed, g.n - (RING - 1))
                    wait(pool, loaded[g.slot(RING)], (g.turn(RING) + 1) * 16)
                    for n in range(G):
                        last = nc.gpsimd.tensor_tensor(
                            W[:, g.slot(RING), n, 0:D].rearrange("p (h c) -> p h c", c=C),
                            rows[:, g.slot(RING), n, 0:D].rearrange("p (h c) -> p h c", c=C),
                            s["alpha"][:, bass.ds(g.n * G + n, 1), :].rearrange("p a h -> p (a h)")
                            .unsqueeze(2).to_broadcast([P, H, C]), ALU.mult)
                    last.then_inc(weighted, 1)

                pipeline(pool, GROUPS, [(0, weigh)])

            @block.sync
            def _(sp):
                def load(g):
                    r = g.slot(RING)
                    wait(sp, weighted, g.n - (RING - 1))
                    sp.dma_start(rows[:, r, :, :].rearrange("p g f -> p (g f)"),
                                 d["rows"][bass.ds(g.n, 1), :, :].rearrange("a p f -> (a p) f")).then_inc(loaded[r], 16)

                pipeline(sp, GROUPS, [(0, load)])

            @block.scalar
            def _(act):
                act.wait_ge(cleared, 1)

                def distances(g):
                    wait(act, hot, g.n - 1)
                    for n in range(G):
                        last = nc.scalar.activation(far[:, g.slot(2), n, :], s["iota"][:, :], ACT.Abs,
                                                    bias=s["dl"][:, bass.ds(g.n * G + n, 1)], scale=-1.0)
                    last.then_inc(distance, 1)

                def one_hot(g):
                    wait(act, distance, g.n + 1)
                    wait(act, summed, g.n - (RING - 1))
                    nc.scalar.activation(hots[:, g.slot(RING), :, :], far[:, g.slot(2), :, :], ACT.Relu,
                                         bias=unit[:, 0:1], scale=-1.0).then_inc(hot, 1)
                    nc.scalar.activation(W[:, g.slot(RING), :, D:D + H], s["alpha"][:, bass.ds(g.n * G, G), :],
                                         ACT.Copy).then_inc(weights_put, 1)

                pipeline(act, GROUPS, [(1, distances), (0, one_hot)])

            @block.vector
            def _(v):
                nc.vector.memset(acc[:, :, :], 0.0).then_inc(added, 2)
                regs = [nc.vector.alloc_register(f"acc_tile{n}") for n in range(UN * G)]
                tiles = []

                def add(n, half):
                    def stage(g):
                        if n == 0 and half == 0:
                            if g.c % UN == 0:
                                tiles[:] = node_tiles(nc.vector, regs, s, g)
                            wait(v, summed, g.n + 1)
                        to = acc[:, bass.ds(tiles[g.c % UN * G + n], 1), cut[half]:cut[half + 1]].rearrange("p a f -> p (a f)")
                        wait(v, added, g.n * (2 * G) + (2 * n + half + 1))
                        nc.vector.tensor_tensor(to, to, ps[:, g.slot(2), n, cut[half]:cut[half + 1]],
                                                ALU.add).then_inc(added, 1)
                    return stage

                cut = (0, (D + H) // 2, D + H)
                stages = [(0, add(n, half)) for n in range(G) for half in range(2)]
                pipeline(v, GROUPS, stages)

            @block.tensor
            def _(pe):
                def sum_(g):
                    wait(pe, weighted, g.n + 1)
                    wait(pe, weights_put, g.n + 1)
                    wait(pe, hot, g.n + 1)
                    wait(pe, added, (g.n - 1) * (2 * G) + 2)
                    for n in range(G):
                        last = nc.tensor.matmul(ps[:, g.slot(2), n, 0:D + H], hots[:, g.slot(RING), n, :],
                                                W[:, g.slot(RING), n, :], start=True, stop=True)
                    last.then_inc(summed, 1)

                pipeline(pe, GROUPS, [(0, sum_)])


def route(nc, s, Wg, bg, W1, b1):
    sem = nc.alloc_semaphore
    measured = sem("r_measured")
    gate_in, dve, inverted, divided, added = sem("r_gate_in"), sem("dve_route"), sem("r_inverted"), sem("r_divided"), sem("r_added")
    sqrt_ready, sqrt_done, listed = sem("r_sqrt_ready"), sem("r_sqrt_done"), sem("r_listed")
    normed, turned, turned_copied, gated = sem("r_normed"), sem("r_turned"), sem("r_turned_copied"), sem("r_gated")
    consts, masked, counted = sem("r_consts"), sem("r_masked"), sem("r_counted")
    w_in = s["w_in"] = sem("w_in_experts")
    with ExitStack() as scope:
        def sb(name, shape, dt=F32):
            return scope.enter_context(nc.sbuf_tensor(name, shape, dt))

        X, acc = s["X"], s["acc"]
        TE = NT * EXPERTS
        wg, bgb = sb("r_wg", [P, KD, EXPERTS]), sb("r_bg", [P, EXPERTS])
        inv = sb("r_inv", [P, NT, H])
        stats, mv, std = sb("r_stats", [P, NT, 6]), sb("r_mv", [P, NT, 2]), sb("r_std", [P, 3, NT])
        xT = sb("r_xT", [P, 4, KD * P])
        staged = sb("r_staged", [P, 4, D])
        before, every = sb("r_before", [P, P]), sb("r_every", [P, P])
        lane = sb("r_lane", [P, NT, EXPERTS])
        token = sb("r_token", [P, NT])
        real = sb("r_real", [P, NT])
        g1, g2 = sb("r_g1", [P, NT, EXPERTS]), sb("r_g2", [P, NT, EXPERTS])
        best, which = sb("r_best", [P, NT]), sb("r_which", [P, NT])
        work = sb("r_work", [P, NT, EXPERTS])
        pick = [sb(f"r_pick{k}", [P, NT, EXPERTS]) for k in range(2)]
        both = sb("r_both", [P, NT, EXPERTS])
        total, cum, one = sb("r_total", [P, EXPERTS, NT]), sb("r_cum", [P, EXPERTS, NT]), sb("r_one", [P, NT])
        count_i = sb("r_count_i", [P, EXPERTS], I32)
        tiles, tiles_cum, start = sb("r_tiles", [P, EXPERTS]), sb("r_tiles_cum", [P, EXPERTS]), sb("r_start", [P, EXPERTS])
        slot = sb("r_slot", [P, NT, EXPERTS])
        slot_f = sb("r_slot_f", [P, NT, 2])
        expert_f = sb("r_expert_f", [1, P])
        pt = scope.enter_context(nc.psum_tensor("r_pt", [P, 4, 512], F32))
        pg = scope.enter_context(nc.psum_tensor("r_pg", [P, NT, EXPERTS], F32))
        pc = scope.enter_context(nc.psum_tensor("r_pc", [P, 2, 512], F32))

        def wide(a):
            return a.unsqueeze(2).to_broadcast([P, NT, EXPERTS])

        with nc.Block() as block:
            @block.gpsimd
            def _(pool):
                nc.gpsimd.memset(before[:, :], 1.0).then_inc(consts, 1)
                nc.gpsimd.memset(every[:, :], 1.0).then_inc(consts, 1)
                nc.gpsimd.memset(one[:, :], 1.0).then_inc(consts, 1)
                nc.gpsimd.iota(lane[:, :, :], [[0, NT], [1, EXPERTS]], base=0, channel_multiplier=0,
                               allow_small_or_imprecise_dtypes=True).then_inc(consts, 1)
                nc.gpsimd.iota(token[:, :], [[P, NT]], base=0, channel_multiplier=1,
                               allow_small_or_imprecise_dtypes=True).then_inc(consts, 1)
                pool.wait_ge(consts, 5)
                nc.gpsimd.affine_select(out=before[:, :], in_=before[:, :], compare_op=ALU.is_gt, fill=0.0,
                                        base=0, pattern=[[1, P]], channel_multiplier=-1).then_inc(consts, 1)
                pool.wait_ge(inverted, 1)

                def divide(g):
                    a = acc[:, bass.ds(g.n, 1), 0:D].rearrange("p a (h c) -> p (a h) c", h=H)
                    nc.gpsimd.tensor_tensor(a, a, inv[:, bass.ds(g.n, 1), :].rearrange("p a h -> p (a h)")
                                            .unsqueeze(2).to_broadcast([P, H, C]), ALU.mult).then_inc(divided, 1)

                pipeline(pool, NT, [(0, divide)])

            @block.sync
            def _(sp):
                sp.dma_start(wg[:, :, :], Wg.rearrange("(k p) e -> p k e", p=P)).then_inc(gate_in, 16)
                sp.dma_start(bgb[:, :], bg.partition_broadcast(P)).then_inc(gate_in, 16)
                for e in range(EXPERTS):
                    sp.dma_start(s["b1"][:, e, :], b1[e, :].rearrange("(m p) -> p m", p=P),
                                 allow_slow_non_contiguous=True).then_inc(w_in, 16)
                    sp.dma_start(s["w1"][:, e, :, :], W1[e, :, :].rearrange("(k p) f -> p k f", p=P)).then_inc(w_in, 16)

            @block.vector
            def _(v):
                step = Chain(v, dve)

                def row(g):
                    return X[:, bass.ds(g.n, 1), :].rearrange("p a f -> p (a f)")

                def sums(g):
                    return acc[:, bass.ds(g.n, 1), 0:D].rearrange("p a f -> p (a f)")

                step(nc.vector.tensor_scalar(inv[:, :, :], acc[:, :, D:D + H], 1e-16, None, ALU.add))
                nc.vector.reciprocal(inv[:, :, :], inv[:, :, :]).then_inc(inverted, 1)

                def add(g):
                    wait(v, divided, g.n + 1)
                    nc.vector.tensor_tensor(row(g), row(g), sums(g), ALU.add).then_inc(added, 1)

                def take_stats(g):
                    wait(v, added, g.n + 1)
                    nc.vector.bn_stats(stats[:, bass.ds(g.n, 1), :].rearrange("p a k -> p (a k)"), row(g)).then_inc(measured, 1)

                pipeline(v, NT, [(1, add), (0, take_stats)])
                v.wait_ge(measured, NT)
                moments(nc, v, step, stats, mv, std, sqrt_ready, sqrt_done)

                def norm(g):
                    wait(v, turned, g.n - 3)
                    wait(v, listed, g.n - 3)
                    nc.vector.tensor_scalar(staged[:, g.slot(4), :], row(g), mv[:, bass.ds(g.n, 1), 0],
                                            std[:, 2, bass.ds(g.n, 1)], ALU.subtract, ALU.mult).then_inc(normed, 1)

                pipeline(v, NT, [(0, norm)])
                v.wait_ge(gate_in, 32)
                v.wait_ge(consts, 6)
                step(nc.vector.tensor_scalar(real[:, :], token[:, :], float(N), None, ALU.is_lt))
                v.wait_ge(gated, NT)
                step(nc.vector.tensor_tensor(g1[:, :, :], pg[:, :, :], bgb[:, :].unsqueeze(1).to_broadcast([P, NT, EXPERTS]),
                                             ALU.add))
                for k, g in enumerate((g1, g2)):
                    step(nc.vector.tensor_reduce(best[:, :], g[:, :, :], AX.X, ALU.max))
                    step(nc.vector.tensor_tensor(work[:, :, :], g[:, :, :], wide(best[:, :]), ALU.is_lt))
                    step(nc.vector.scalar_tensor_tensor(work[:, :, :], work[:, :, :], float(EXPERTS), lane[:, :, :],
                                                        ALU.mult, ALU.add))
                    step(nc.vector.tensor_reduce(which[:, :], work[:, :, :], AX.X, ALU.min))
                    step(nc.vector.tensor_tensor(pick[k][:, :, :], lane[:, :, :], wide(which[:, :]), ALU.is_equal))
                    if k == 0:
                        step(nc.vector.scalar_tensor_tensor(g2[:, :, :], pick[0][:, :, :], -BIG, g1[:, :, :],
                                                            ALU.mult, ALU.add))
                    step(nc.vector.tensor_tensor(pick[k][:, :, :], pick[k][:, :, :], wide(real[:, :]), ALU.mult))
                nc.vector.tensor_tensor(both[:, :, :], pick[0][:, :, :], pick[1][:, :, :], ALU.add).then_inc(masked, 1)
                v.wait_ge(counted, 1)
                step(nc.vector.tensor_copy(total[:, :, :], pc[:, 1, 0:TE].rearrange("p (t e) -> p e t", e=EXPERTS)))
                for e in range(EXPERTS):
                    last = nc.vector.tensor_tensor_scan(cum[:, e, :], one[:, :], total[:, e, :], 0.0, ALU.mult, ALU.add)
                step(last)
                step(nc.vector.tensor_scalar(tiles[:, :], cum[:, :, NT - 1], float(P - 1), None, ALU.add))
                step(nc.vector.tensor_copy(count_i[:, :], tiles[:, :]))
                step(nc.vector.tensor_scalar(count_i[:, :], count_i[:, :], 7, None, ALU.logical_shift_right))
                step(nc.vector.tensor_copy(tiles[:, :], count_i[:, :]))
                step(nc.vector.tensor_tensor_scan(tiles_cum[:, :], one[:, 0:EXPERTS], tiles[:, :], 0.0, ALU.mult, ALU.add))
                step(nc.vector.tensor_tensor(start[:, :], tiles_cum[:, :], tiles[:, :], ALU.subtract))
                step(nc.vector.tensor_scalar(start[:, :], start[:, :], float(P), None, ALU.mult))
                step(nc.vector.tensor_tensor(cum[:, :, :], cum[:, :, :], total[:, :, :], ALU.subtract))
                step(nc.vector.tensor_tensor(cum[:, :, :], cum[:, :, :], start[:, :].unsqueeze(2).to_broadcast([P, EXPERTS, NT]),
                                             ALU.add))
                step(nc.vector.tensor_tensor(slot[:, :, :], cum[:, :, :].rearrange("p e t -> p t e"),
                                             pc[:, 0, 0:TE].rearrange("p (t e) -> p t e", e=EXPERTS), ALU.add))
                for k in range(2):
                    step(nc.vector.tensor_tensor(work[:, :, :], slot[:, :, :], pick[k][:, :, :], ALU.mult))
                    step(nc.vector.tensor_reduce(slot_f[:, :, k], work[:, :, :], AX.X, ALU.add))
                step(nc.vector.tensor_copy(s["slot_of"][:, :, :], slot_f[:, :, :]))
                step(nc.vector.tensor_scalar(expert_f[:, :], s["iota"][0:1, :], tiles_cum[0:1, 0:1], None, ALU.is_ge))
                for e in range(1, EXPERTS - 1):
                    step(nc.vector.scalar_tensor_tensor(expert_f[:, :], s["iota"][0:1, :], tiles_cum[0:1, e:e + 1],
                                                        expert_f[:, :], ALU.is_ge, ALU.add))
                step(nc.vector.tensor_copy(s["tile_expert"][:, :], expert_f[:, :]))

            @block.scalar
            def _(act):
                act.wait_ge(sqrt_ready, 1)
                nc.scalar.activation(std[:, 1, :], std[:, 0, :], ACT.Sqrt).then_inc(sqrt_done, 1)

                def copy_turned(g):
                    wait(act, turned, g.n + 1)
                    wait(act, gated, g.n - 3)
                    nc.scalar.activation(xT[:, g.slot(4), :], pt[:, g.slot(4), 0:KD * P], ACT.Copy).then_inc(turned_copied, 1)

                def keep_normed(g):
                    wait(act, normed, g.n + 1)
                    nc.scalar.activation(acc[:, bass.ds(g.n, 1), 0:D].rearrange("p a f -> p (a f)"),
                                         staged[:, g.slot(4), :], ACT.Copy).then_inc(listed, 1)

                pipeline(act, NT, [(1, keep_normed), (0, copy_turned)])

            @block.tensor
            def _(pe):
                pe.wait_ge(gate_in, 32)

                def turn(g):
                    wait(pe, normed, g.n + 1)
                    wait(pe, turned_copied, g.n - 3)
                    for h in range(KD):
                        last = nc.tensor.transpose(pt[:, g.slot(4), h * P:(h + 1) * P],
                                                   staged[:, g.slot(4), h * P:(h + 1) * P], s["ident"][:, :])
                    last.then_inc(turned, 1)

                def gate(g):
                    wait(pe, turned_copied, g.n + 1)
                    for h in range(KD):
                        last = nc.tensor.matmul(pg[:, bass.ds(g.n, 1), :].rearrange("p a e -> p (a e)"),
                                                xT[:, g.slot(4), h * P:(h + 1) * P], wg[:, h, :],
                                                start=(h == 0), stop=(h == KD - 1))
                    last.then_inc(gated, 1)

                pipeline(pe, NT, [(2, turn), (0, gate)])
                pe.wait_ge(consts, 6)
                pe.wait_ge(masked, 1)
                for a, m in enumerate((before, every)):
                    last = nc.tensor.matmul(pc[:, a, 0:TE], m[:, :], both[:, :, :].rearrange("p t e -> p (t e)"),
                                            start=True, stop=True)
                last.then_inc(counted, 1)


def spread_tokens(nc, d, s, W2):
    sem = nc.alloc_semaphore
    w_in = s["w_in"]
    rows = s["spread_rows"]
    copied, placed, first = sem("s_copied"), sem("s_placed"), sem("s_first")
    sent = [sem(f"s_sent{i}") for i in range(4)]
    last_tile = NODE_TILES - 1
    rest = N - last_tile * P
    with nc.sbuf_tensor("s_word", [P, 1], F32) as word, nc.sbuf_tensor("s_idx", [P, 4, 2], I32) as idx, nc.sbuf_tensor("s_place", [P, NT, 2], F32) as place, \
            nc.Block() as block:
        @block.gpsimd
        def _(pool):
            nc.gpsimd.iota(place[:, :, :], [[P, NT], [NT * P, 2]], base=0, channel_multiplier=1,
                           allow_small_or_imprecise_dtypes=True).then_inc(placed, 1)
            nc.gpsimd.memset(word[:, :], 0.0).then_inc(first, 1)

            def send(g, parts=P):
                r = g.slot(4)
                goals = [(m, v if isinstance(v, int) else pool.to_reg(v)) for m, v in ((copied, 3 * g.n + 3),)]
                pool.wait_ge(first, 1)
                for m, v in goals:
                    wait(pool, m, v)
                for k in range(2):
                    nc.gpsimd.indirect_dma_start(
                        out=d["slots_in"][:, :], out_offset=bass.IndirectOffsetOnAxis(ap=idx[0:parts, r, k:k + 1], axis=0),
                        in_=rows[0:parts, r, k, :], in_offset=None).then_inc(sent[r], 16)

            pipeline(pool, last_tile, [(0, send)])
            send(Step(0, last_tile), rest)
            for r in range(4):
                pool.wait_ge(sent[r], 32 * len(range(r, NODE_TILES, 4)))

        @block.vector
        def _(v):
            v.wait_ge(placed, 1)

            def copy(g):
                r = g.slot(4)
                wait(v, sent[r], g.turn(4) * 32)
                nc.vector.tensor_copy(rows[:, r, :, 0:D], s["acc"][:, bass.ds(g.n, 1), 0:D]
                                      .to_broadcast([P, 2, D])).then_inc(copied, 1)
                nc.vector.tensor_copy(rows[:, r, :, D:DX], place[:, bass.ds(g.n, 1), :].rearrange("p a k -> p (a k)")
                                      .unsqueeze(2).to_broadcast([P, 2, DX - D])).then_inc(copied, 1)
                nc.vector.tensor_copy(idx[:, r, :], s["slot_of"][:, bass.ds(g.n, 1), :]
                                      .rearrange("p a k -> p (a k)")).then_inc(copied, 1)

            pipeline(v, NODE_TILES, [(0, copy)])

        @block.sync
        def _(sp):
            for e in range(EXPERTS):
                sp.dma_start(s["w2"][:, e, :, :], W2[e, :, :].rearrange("(k p) f -> p k f", p=P)).then_inc(w_in, 16)


def experts(nc, d, s, b2):
    sem = nc.alloc_semaphore
    w_in, w_goal, b2_in = s["w_in"], 16 * 3 * EXPERTS, sem("e_b2_in")
    loaded = [sem(f"e_loaded{i}") for i in range(4)]
    stored = [sem(f"e_stored{i}") for i in range(4)]
    turned, turned_copied, placed, up = sem("e_turned"), sem("e_turned_copied"), sem("e_placed"), sem("e_up")
    taken, started, numbered, parted = sem("e_taken"), sem("e_started"), sem("e_numbered"), sem("e_parted")
    gelued, down, done = sem("e_gelued"), sem("e_down"), sem("e_done")
    with ExitStack() as scope:
        def sb(name, shape, dt=F32):
            return scope.enter_context(nc.sbuf_tensor(name, shape, dt))

        w1, w2, b1 = s["w1"], s["w2"], s["b1"]
        b2b = sb("e_b2", [P, EXPERTS, D])
        x = sb("e_x", [P, 4, DX])
        goes_to = sb("e_goes_to", [P, 4, 1], I32)
        slot_number = sb("e_slot_number", [P, SLOT_TILES])
        apart = sb("e_apart", [P, 4, 1])
        word = sb("e_word", [P, 1])
        xT = sb("e_xT", [P, 2, D])
        w1_own = sb("e_w1_own", [P, 2, KD, HID])
        hT = sb("e_hT", [P, 2, HID])
        y = sb("e_y", [P, 4, D])
        pt = scope.enter_context(nc.psum_tensor("e_pt", [P, 2, 512], F32))
        ph = scope.enter_context(nc.psum_tensor("e_ph", [P, 2, 512], F32))
        py = scope.enter_context(nc.psum_tensor("e_py", [P, 2, 512], F32))

        def expert_reader(eng, name, ahead=0):
            regs = [eng.alloc_register(f"{name}{c}") for c in range(UN)]
            first, held = [0], []

            def expert(g):
                if not held or (g.c - ahead) % UN == 0:
                    eng.load(regs, s["tile_expert"][0:1, bass.ds(g.n, UN)])
                    first[0], held[:] = g.c, [eng.snap(r, min_val=0, max_val=EXPERTS - 1) for r in regs]
                return held[g.c - first[0]]
            return expert

        with nc.Block() as block:
            @block.sync
            def _(sp):
                sp.dma_start(b2b[:, :, :], b2.rearrange("e f -> (e f)").partition_broadcast(P)
                             .rearrange("p (e f) -> p e f", e=EXPERTS)).then_inc(b2_in, 16)

                def load(g):
                    r = g.slot(4)
                    wait(sp, turned, g.n - 3)
                    wait(sp, taken, g.n - 3)
                    sp.dma_start(x[:, r, :], d["slots_in"][bass.ds(g.n * P, P), :]).then_inc(loaded[r], 16)

                pipeline(sp, SLOT_TILES, [(4, load)])

            @block.gpsimd
            def _(pool):
                nc.gpsimd.iota(slot_number[:, :], [[P, SLOT_TILES]], base=0, channel_multiplier=1,
                               allow_small_or_imprecise_dtypes=True).then_inc(numbered, 1)
                nc.gpsimd.memset(word[:, :], 0.0).then_inc(started, 1)

                def send(g):
                    r = g.slot(4)
                    goals = [(m, g.n + 1 if isinstance(g.n, int) else pool.to_reg(g.n + 1)) for m in (taken, done)]
                    pool.wait_ge(started, 1)
                    for m, v in goals:
                        wait(pool, m, v)
                    nc.gpsimd.indirect_dma_start(
                        out=d["results"][:, :], out_offset=bass.IndirectOffsetOnAxis(ap=goes_to[:, r, 0:1], axis=0),
                        in_=y[:, r, :], in_offset=None).then_inc(stored[r], 16)

                pipeline(pool, SLOT_TILES, [(0, send)])
                for r in range(4):
                    pool.wait_ge(stored[r], 16 * (SLOT_TILES // 4))

            @block.vector
            def _(v):
                expert, next_expert = expert_reader(nc.vector, "b2_expert"), expert_reader(nc.vector, "w1_expert", 2)
                v.wait_ge(b2_in, 16)
                v.wait_ge(w_in, w_goal)
                v.wait_ge(numbered, 1)

                def place(g):
                    e = next_expert(g)
                    wait(v, up, g.n - 1)
                    nc.vector.tensor_copy(w1_own[:, g.slot(2), :, :],
                                          w1[:, bass.ds(e, 1), :, :].rearrange("p a k f -> p (a k) f")
                                          ).then_inc(placed, 1)

                def copy_turned(g):
                    wait(v, turned, g.n + 1)
                    wait(v, up, g.n - 1)
                    nc.vector.tensor_copy(xT[:, g.slot(2), :], pt[:, g.slot(2), 0:D]).then_inc(turned_copied, 1)

                def add_b2(g):
                    r = g.slot(4)
                    e = expert(g)
                    wait(v, down, g.n + 1)
                    wait(v, stored[r], g.turn(4) * 16)
                    nc.vector.scalar_tensor_tensor(apart[:, r, :], x[:, r, D:D + 1], float(NOWHERE),
                                                   slot_number[:, bass.ds(g.n, 1)], ALU.is_ge, ALU.mult).then_inc(parted, 1)
                    wait(v, parted, g.n + 1)
                    nc.vector.tensor_tensor(goes_to[:, r, :], x[:, r, D:D + 1], apart[:, r, :], ALU.add).then_inc(taken, 1)
                    nc.vector.tensor_tensor(y[:, r, :], py[:, g.slot(2), 0:D],
                                            b2b[:, bass.ds(e, 1), :].rearrange("p a f -> p (a f)"),
                                            ALU.add).then_inc(done, 1)

                pipeline(v, SLOT_TILES, [(2, copy_turned), (2, place), (0, add_b2)])

            @block.scalar
            def _(act):
                expert = expert_reader(nc.scalar, "b1_expert")
                act.wait_ge(w_in, w_goal)

                def gelu(g):
                    e = expert(g)
                    wait(act, up, g.n + 1)
                    wait(act, down, g.n - 1)
                    for m in range(KH):
                        last = nc.scalar.activation(hT[:, g.slot(2), m * P:(m + 1) * P], ph[:, g.slot(2), m * P:(m + 1) * P],
                                                    ACT.Gelu, bias=b1[:, bass.ds(e, 1), m])
                    last.then_inc(gelued, 1)

                pipeline(act, SLOT_TILES, [(0, gelu)])

            @block.tensor
            def _(pe):
                expert = expert_reader(nc.tensor, "w2_expert")

                def turn(g):
                    wait(pe, loaded[g.slot(4)], (g.turn(4) + 1) * 16)
                    wait(pe, turned_copied, g.n - 1)
                    for k in range(KD):
                        last = nc.tensor.transpose(pt[:, g.slot(2), k * P:(k + 1) * P],
                                                   x[:, g.slot(4), k * P:(k + 1) * P], s["ident"][:, :])
                    last.then_inc(turned, 1)

                def layer1(g):
                    wait(pe, turned_copied, g.n + 1)
                    wait(pe, placed, g.n + 1)
                    wait(pe, gelued, g.n - 1)
                    for m in range(KH):
                        for k in range(KD):
                            last = nc.tensor.matmul(ph[:, g.slot(2), m * P:(m + 1) * P],
                                                    w1_own[:, g.slot(2), k, m * P:(m + 1) * P],
                                                    xT[:, g.slot(2), k * P:(k + 1) * P],
                                                    start=(k == 0), stop=(k == KD - 1))
                    last.then_inc(up, 1)

                def layer2(g):
                    e = expert(g)
                    wait(pe, gelued, g.n + 1)
                    wait(pe, done, g.n - 1)
                    for m in range(KH):
                        last = nc.tensor.matmul(py[:, g.slot(2), 0:D], hT[:, g.slot(2), m * P:(m + 1) * P],
                                                w2[:, bass.ds(e, 1), m, :].rearrange("p a f -> p (a f)"),
                                                start=(m == 0), stop=(m == KH - 1))
                    last.then_inc(down, 1)

                pe.wait_ge(w_in, w_goal)
                pipeline(pe, SLOT_TILES, [(2, turn), (1, layer1), (0, layer2)])


def combine(nc, d, s, out):
    sem = nc.alloc_semaphore
    by = 8
    full = N // P
    rest = N - full * P
    chunks = [(P, t, min(by, full - t)) for t in range(0, full, by)] + [(rest, full, 1)] * (rest > 0)
    fetched = [sem(f"c_fetched{i}") for i in range(len(chunks))]
    first, added, stored = sem("c_first"), sem("c_added"), sem("c_stored")
    with nc.sbuf_tensor("c_rows", [P, 2, NODE_TILES, D], F32) as rows, nc.Block() as block:
        @block.sync
        def _(sp):
            for i, (parts, t, n) in enumerate(chunks):
                for k in range(2):
                    at = (k * NT + t) * P
                    sp.dma_start(rows[0:parts, k, t:t + n, :], d["results"][at:at + parts * n, :]
                                 .rearrange("(t p) f -> p t f", p=parts)).then_inc(fetched[i], 16)

        @block.vector
        def _(v):
            for i, (parts, t, n) in enumerate(chunks):
                to = s["X"][0:parts, t:t + n, :]
                v.wait_ge(fetched[i], 32)
                nc.vector.tensor_tensor(to, to, rows[0:parts, 0, t:t + n, :], ALU.add).then_inc(first, 1)
                v.wait_ge(first, i + 1)
                nc.vector.tensor_tensor(to, to, rows[0:parts, 1, t:t + n, :], ALU.add).then_inc(added, 1)

        @block.scalar
        def _(act):
            for i, (parts, t, n) in enumerate(chunks):
                act.wait_ge(added, i + 1)
                act.dma_start(out[t * P:t * P + parts * n, :].rearrange("(t p) f -> p t f", p=parts),
                              s["X"][0:parts, t:t + n, :]).then_inc(stored, 16)
            act.wait_ge(stored, 16 * len(chunks))


_INS = ["x", "src", "dst", "edge_weight", "L0_gnn_W_l", "L0_gnn_b_l", "L0_gnn_W_r", "L0_gnn_b_r", "L0_gnn_att",
        "L0_gnn_bias", "L0_ffn_Wg", "L0_ffn_bg", "L0_ffn_W1", "L0_ffn_b1", "L0_ffn_W2", "L0_ffn_b2"]


def kernel(**inputs):
    import numpy as np
    import concourse.bacc as bacc
    from concourse.bass_utils import run_bass_kernel_spmd

    nc = bacc.Bacc("TRN2", target_bir_lowering=False, num_devices=1)
    arrays, args = {}, []
    for name in _INS:
        a = np.ascontiguousarray(inputs[name])
        arrays[f"in_{name}"] = a
        args.append(nc.dram_tensor(f"in_{name}", a.shape, mybir.dt.from_np(a.dtype), kind="ExternalInput").ap())
    args.append(nc.dram_tensor("out", (N, D), F32, kind="ExternalOutput").ap())
    build(nc, *args)
    return run_bass_kernel_spmd(nc, [arrays], core_ids=[0]).results[0]["out"]
```
